# Optimizing a Trainium2 kernel written in Bass

```python
import numpy as np
import jax
import jax.numpy as jnp

def _softmax(x, axis=-1):
    return jax.nn.softmax(x, axis=axis)

def _gelu(x):
    return jax.nn.gelu(x, approximate=True)

def _silu(x):
    return jax.nn.silu(x)

def _sigmoid(x):
    return jax.nn.sigmoid(x)

def _layernorm(x, axis=-1, eps=1e-05):
    m = jnp.mean(x, axis=axis, keepdims=True)
    v = jnp.var(x, axis=axis, keepdims=True)
    return (x - m) / jnp.sqrt(v + eps)

def _scatter_add(tgt, idx, src, axis=0):
    return tgt.at[idx].add(src)

def _segment_sum(src, seg, n):
    return jax.ops.segment_sum(src, seg, n)
kernel_name = 'mk_recurrent_d2_jaxref_r8_cbd5b3'

def setup_inputs(seed: int=0):
    np.random.seed(seed)
    _w = jnp.asarray

    def _L0_attn_setup():
        import jax, jax.numpy as jnp
        import numpy as np
        D_MODEL = 128
        N_HEADS = 16
        HEAD_DIM = D_MODEL // N_HEADS
        MAX_REL = 128
        B, S = (8, 128)
        key = jax.random.key(seed)
        ks = jax.random.split(key, 12)
        sc = 1.0 / np.sqrt(D_MODEL)
        return {'hidden_states': jax.random.normal(ks[0], (B, S, D_MODEL), jnp.float32), 'Wq': jax.random.normal(ks[1], (D_MODEL, D_MODEL), jnp.float32) * sc, 'bq': jnp.zeros((D_MODEL,), jnp.float32), 'Wk': jax.random.normal(ks[2], (D_MODEL, D_MODEL), jnp.float32) * sc, 'bk': jnp.zeros((D_MODEL,), jnp.float32), 'Wv': jax.random.normal(ks[3], (D_MODEL, D_MODEL), jnp.float32) * sc, 'bv': jnp.zeros((D_MODEL,), jnp.float32), 'Wo': jax.random.normal(ks[4], (D_MODEL, D_MODEL), jnp.float32) * sc, 'bo': jnp.zeros((D_MODEL,), jnp.float32), 'rel_emb': jax.random.normal(ks[5], (2 * MAX_REL + 1, HEAD_DIM), jnp.float32) * 0.02, 'M': jax.random.uniform(ks[6], (N_HEADS, HEAD_DIM, HEAD_DIM), jnp.float32), 'z': jax.random.uniform(ks[7], (N_HEADS, HEAD_DIM), jnp.float32), 'gate_alpha': jnp.float32(0.5)}
    _L0_attn_in = _L0_attn_setup()

    def _L0_ffn_setup():
        import jax, jax.numpy as jnp
        import numpy as np
        E = 32
        H = 128
        I = 64
        G = 8
        TKG = 4
        TOPK = 8
        NSH = 2
        SCALE = 2.5
        key = jax.random.key(seed)
        ks = jax.random.split(key, 10)
        s = 0.02
        return {'hidden_states': jax.random.normal(ks[0], (2, 128, H), jnp.float32), 'gate_w': jax.random.normal(ks[1], (E, H), jnp.float32) * s, 'gate_bias': jax.random.normal(ks[2], (E,), jnp.float32) * s, 'w_gate': jax.random.normal(ks[3], (E, I, H), jnp.float32) * s, 'w_up': jax.random.normal(ks[4], (E, I, H), jnp.float32) * s, 'w_down': jax.random.normal(ks[5], (E, H, I), jnp.float32) * s, 'sh_gate': jax.random.normal(ks[6], (I * NSH, H), jnp.float32) * s, 'sh_up': jax.random.normal(ks[7], (I * NSH, H), jnp.float32) * s, 'sh_down': jax.random.normal(ks[8], (H, I * NSH), jnp.float32) * s}
    _L0_ffn_in = _L0_ffn_setup()

    def _L1_attn_setup():
        import jax, jax.numpy as jnp
        import numpy as np
        import math
        B, S, H = (4, 128, 128)
        NQ, NKV = (16, 8)
        HD = H // NQ
        G = HD * NKV
        DEPTH = 1
        LAMBDA_INIT = 0.8 - 0.6 * math.exp(-0.3 * DEPTH)
        key = jax.random.key(seed)
        ks = jax.random.split(key, 7)
        x = jax.random.normal(ks[0], (B, S, H), jnp.float32)
        Wqkv = jax.random.normal(ks[1], (H, 2 * H + 2 * G), jnp.float32) / math.sqrt(H)
        Wproj = jax.random.normal(ks[2], (H, H), jnp.float32) / math.sqrt(H)
        lambda_q1 = 0.1 * jax.random.normal(ks[3], (G,), jnp.float32)
        lambda_k1 = 0.1 * jax.random.normal(ks[4], (G,), jnp.float32)
        lambda_q2 = 0.1 * jax.random.normal(ks[5], (G,), jnp.float32)
        lambda_k2 = 0.1 * jax.random.normal(ks[6], (G,), jnp.float32)
        return {'x': x, 'Wqkv': Wqkv, 'Wproj': Wproj, 'lambda_q1': lambda_q1, 'lambda_k1': lambda_k1, 'lambda_q2': lambda_q2, 'lambda_k2': lambda_k2}
    _L1_attn_in = _L1_attn_setup()

    def _L1_ffn_setup():
        import jax, jax.numpy as jnp
        import numpy as np
        DIM = 128
        DEPTH = 6
        HEADS = 16
        DIM_HEAD = 64
        WINDOW = 32
        INNER = HEADS * DIM_HEAD
        DIM_INNER = int(DIM * 4 * 2 / 3)
        QK_SCALE = 8.0

        def shift_tokens(t):
            a, s = jnp.split(t, 2, -1)
            s = jnp.pad(s, ((0, 0), (1, 0), (0, 0)))[:, :-1]
            return jnp.concatenate([a, s], -1)

        def l2norm(t):
            return t / jnp.maximum(jnp.linalg.norm(t, axis=-1, keepdims=True), 1e-12)

        def rotate_half(x):
            x1, x2 = jnp.split(x, 2, -1)
            return jnp.concatenate([-x2, x1], -1)

        def rotary_tables(n):
            half = jnp.arange(0, DIM_HEAD, 2, dtype=jnp.float32)
            inv_freq = 1.0 / 10000.0 ** (half / DIM_HEAD)
            t = jnp.arange(n, dtype=jnp.float32)
            freqs = t[:, None] * inv_freq[None, :]
            freqs = jnp.concatenate([freqs, freqs], -1)
            base_scale = (half + 0.4 * DIM_HEAD) / (1.4 * DIM_HEAD)
            power = (t - n // 2) / (WINDOW // 2)
            scale = base_scale[None, :] ** power[:, None]
            scale = jnp.concatenate([scale, scale], -1)
            return (freqs, scale)

        def local_attention(q, k, v):
            b, h, n, d = q.shape
            w = WINDOW
            nw = n // w
            bq = q.reshape(b, h, nw, w, d)
            bk = k.reshape(b, h, nw, w, d)
            bv = v.reshape(b, h, nw, w, d)

            def look(t):
                p = jnp.pad(t, ((0, 0), (0, 0), (1, 0), (0, 0), (0, 0)))
                return jnp.concatenate([p[:, :, :nw], p[:, :, 1:]], axis=3)
            bk2, bv2 = (look(bk), look(bv))
            seq = jnp.arange(n).reshape(nw, w)
            seq_p = jnp.pad(seq, ((1, 0), (0, 0)), constant_values=-1)
            jt = jnp.concatenate([seq_p[:nw], seq_p[1:]], axis=1)
            it = seq[:, :, None]
            jb = jt[:, None, :]
            mask = (it < jb) | (it > jb + w) | (jb == -1)
            sim = jnp.einsum('bhwie,bhwje->bhwij', bq, bk2) * QK_SCALE
            sim = jnp.where(mask, -jnp.finfo(sim.dtype).max, sim)
            attn = jax.nn.softmax(sim, -1)
            out = jnp.einsum('bhwij,bhwje->bhwie', attn, bv2)
            return out.reshape(b, h, n, d)

        def attn_layer(x, Wqkv, qs, ksc, Wo):
            b, n, _ = x.shape
            qkv = x @ Wqkv
            q, k, v = jnp.split(qkv, 3, -1)
            sh = lambda t: t.reshape(b, n, HEADS, DIM_HEAD).transpose(0, 2, 1, 3)
            q, k, v = (sh(q), sh(k), sh(v))
            q = l2norm(q) * qs
            k = l2norm(k) * ksc
            freqs, scale = rotary_tables(n)
            cos, sin = (jnp.cos(freqs), jnp.sin(freqs))
            q = q * cos * scale + rotate_half(q) * sin * scale
            inv = 1.0 / scale
            k = k * cos * inv + rotate_half(k) * sin * inv
            out = local_attention(q, k, v)
            out = out.transpose(0, 2, 1, 3).reshape(b, n, INNER)
            return out @ Wo

        def ffn_layer(x, g, bln, W1, b1, W2, b2):
            mu = x.mean(-1, keepdims=True)
            var = ((x - mu) ** 2).mean(-1, keepdims=True)
            xn = (x - mu) / jnp.sqrt(var + 1e-05) * g + bln
            hg = xn @ W1 + b1
            a, gate = jnp.split(hg, 2, -1)
            return a * jax.nn.gelu(gate, approximate=False) @ W2 + b2
        key = jax.random.key(seed)
        ks = jax.random.split(key, 8)
        B, N = (2, 256)
        init = lambda k, shape: jax.random.normal(k, shape, jnp.float32) * 0.02
        return {'x': jax.random.normal(ks[0], (B, N, DIM), jnp.float32), 'Wqkv': init(ks[1], (DEPTH, DIM, 3 * INNER)), 'q_scale': jnp.ones((DEPTH, DIM_HEAD), jnp.float32), 'k_scale': jnp.ones((DEPTH, DIM_HEAD), jnp.float32), 'Wo': init(ks[2], (DEPTH, INNER, DIM)), 'ln_g': jnp.ones((DEPTH, DIM), jnp.float32), 'ln_b': jnp.zeros((DEPTH, DIM), jnp.float32), 'W1': init(ks[3], (DEPTH, DIM, 2 * DIM_INNER)), 'b1': jnp.zeros((DEPTH, 2 * DIM_INNER), jnp.float32), 'W2': init(ks[4], (DEPTH, DIM_INNER, DIM)), 'b2': jnp.zeros((DEPTH, DIM), jnp.float32)}
    _L1_ffn_in = _L1_ffn_setup()
    _d = {'L0_attn_hidden_states': _L0_attn_in['hidden_states'], 'L0_attn_Wq': _L0_attn_in['Wq'], 'L0_attn_bq': _L0_attn_in['bq'], 'L0_attn_Wk': _L0_attn_in['Wk'], 'L0_attn_bk': _L0_attn_in['bk'], 'L0_attn_Wv': _L0_attn_in['Wv'], 'L0_attn_bv': _L0_attn_in['bv'], 'L0_attn_Wo': _L0_attn_in['Wo'], 'L0_attn_bo': _L0_attn_in['bo'], 'L0_attn_rel_emb': _L0_attn_in['rel_emb'], 'L0_attn_M': _L0_attn_in['M'], 'L0_attn_z': _L0_attn_in['z'], 'L0_attn_gate_alpha': _L0_attn_in['gate_alpha'], 'L0_ffn_gate_w': _L0_ffn_in['gate_w'], 'L0_ffn_gate_bias': _L0_ffn_in['gate_bias'], 'L0_ffn_w_gate': _L0_ffn_in['w_gate'], 'L0_ffn_w_up': _L0_ffn_in['w_up'], 'L0_ffn_w_down': _L0_ffn_in['w_down'], 'L0_ffn_sh_gate': _L0_ffn_in['sh_gate'], 'L0_ffn_sh_up': _L0_ffn_in['sh_up'], 'L0_ffn_sh_down': _L0_ffn_in['sh_down'], 'L1_attn_Wqkv': _L1_attn_in['Wqkv'], 'L1_attn_Wproj': _L1_attn_in['Wproj'], 'L1_attn_lambda_q1': _L1_attn_in['lambda_q1'], 'L1_attn_lambda_k1': _L1_attn_in['lambda_k1'], 'L1_attn_lambda_q2': _L1_attn_in['lambda_q2'], 'L1_attn_lambda_k2': _L1_attn_in['lambda_k2'], 'L1_ffn_Wqkv': _L1_ffn_in['Wqkv'], 'L1_ffn_q_scale': _L1_ffn_in['q_scale'], 'L1_ffn_k_scale': _L1_ffn_in['k_scale'], 'L1_ffn_Wo': _L1_ffn_in['Wo'], 'L1_ffn_ln_g': _L1_ffn_in['ln_g'], 'L1_ffn_ln_b': _L1_ffn_in['ln_b'], 'L1_ffn_W1': _L1_ffn_in['W1'], 'L1_ffn_b1': _L1_ffn_in['b1'], 'L1_ffn_W2': _L1_ffn_in['W2'], 'L1_ffn_b2': _L1_ffn_in['b2']}
    _x0 = _d['L0_attn_hidden_states']
    _d['L0_attn_hidden_states'] = jax.random.normal(jax.random.fold_in(jax.random.key(seed), 1), (2, 1024, 128), dtype=_x0.dtype)
    del _x0
    return _d

def reference(L0_attn_hidden_states, L0_attn_Wq, L0_attn_bq, L0_attn_Wk, L0_attn_bk, L0_attn_Wv, L0_attn_bv, L0_attn_Wo, L0_attn_bo, L0_attn_rel_emb, L0_attn_M, L0_attn_z, L0_attn_gate_alpha, L0_ffn_gate_w, L0_ffn_gate_bias, L0_ffn_w_gate, L0_ffn_w_up, L0_ffn_w_down, L0_ffn_sh_gate, L0_ffn_sh_up, L0_ffn_sh_down, L1_attn_Wqkv, L1_attn_Wproj, L1_attn_lambda_q1, L1_attn_lambda_k1, L1_attn_lambda_q2, L1_attn_lambda_k2, L1_ffn_Wqkv, L1_ffn_q_scale, L1_ffn_k_scale, L1_ffn_Wo, L1_ffn_ln_g, L1_ffn_ln_b, L1_ffn_W1, L1_ffn_b1, L1_ffn_W2, L1_ffn_b2):

    def _L0_attn_ref(hidden_states, Wq, bq, Wk, bk, Wv, bv, Wo, bo, rel_emb, M, z, gate_alpha):
        import jax, jax.numpy as jnp
        import numpy as np
        D_MODEL = 128
        N_HEADS = 16
        HEAD_DIM = D_MODEL // N_HEADS
        MAX_REL = 128
        B, S = (8, 128)
        b, s, _ = hidden_states.shape

        def proj(W, bias):
            y = hidden_states @ W.T + bias
            return y.reshape(b, s, N_HEADS, HEAD_DIM).transpose(0, 2, 1, 3)
        q = proj(Wq, bq)
        k = proj(Wk, bk)
        v = proj(Wv, bv)
        dist = jnp.arange(s)[:, None] - jnp.arange(s)[None, :]
        dist = jnp.clip(dist, -MAX_REL, MAX_REL) + MAX_REL
        rel_pos = rel_emb[dist]
        scores = jnp.einsum('bhqd,bhkd->bhqk', q, k)
        scores = scores + jnp.einsum('bhqd,qkd->bhqk', q, rel_pos)
        scores = scores / np.sqrt(HEAD_DIM).astype(np.float32)
        attn = jax.nn.softmax(scores, axis=-1)
        local_ctx = jnp.einsum('bhqk,bhkd->bhqd', attn, v)
        sigma_q = jax.nn.elu(q) + 1.0
        num = jnp.einsum('bhqk,hkv->bhqv', sigma_q, M)
        den = jnp.einsum('bhqk,hk->bhq', sigma_q, z) + 1e-06
        global_attn = num / den[..., None]
        gate = jax.nn.sigmoid(gate_alpha)
        combined = gate * local_ctx + (1.0 - gate) * global_attn
        out = combined.transpose(0, 2, 1, 3).reshape(b, s, D_MODEL)
        return out @ Wo.T + bo

    def _L0_ffn_ref(hidden_states, gate_w, gate_bias, w_gate, w_up, w_down, sh_gate, sh_up, sh_down):
        import jax, jax.numpy as jnp
        import numpy as np
        E = 32
        H = 128
        I = 64
        G = 8
        TKG = 4
        TOPK = 8
        NSH = 2
        SCALE = 2.5
        B, S, Hd = hidden_states.shape
        h = hidden_states.reshape(-1, Hd)
        logits = h.astype(jnp.float32) @ gate_w.T
        scores = jax.nn.sigmoid(logits)
        sc = scores + gate_bias
        grp = sc.reshape(-1, G, E // G)
        group_scores = jax.lax.top_k(grp, 2)[0].sum(-1)
        gidx = jax.lax.top_k(group_scores, TKG)[1]
        gmask = jnp.sum(jax.nn.one_hot(gidx, G, dtype=sc.dtype), axis=1)
        smask = jnp.repeat(gmask, E // G, axis=1)
        masked = jnp.where(smask > 0, sc, jnp.zeros_like(sc))
        tki = jax.lax.top_k(masked, TOPK)[1]
        tkw = jnp.take_along_axis(scores, tki, axis=1)
        tkw = tkw / (tkw.sum(-1, keepdims=True) + 1e-20)
        tkw = tkw * SCALE
        combine = (jax.nn.one_hot(tki, E, dtype=tkw.dtype) * tkw[..., None]).sum(1)
        g = jax.nn.silu(jnp.einsum('th,eih->tei', h, w_gate))
        u = jnp.einsum('th,eih->tei', h, w_up)
        routed = jnp.einsum('tei,ehi->th', g * u * combine[:, :, None], w_down)
        sg = jax.nn.silu(h @ sh_gate.T)
        shared = sg * (h @ sh_up.T) @ sh_down.T
        return (routed + shared).reshape(B, S, Hd)

    def _L1_attn_ref(x, Wqkv, Wproj, lambda_q1, lambda_k1, lambda_q2, lambda_k2):
        import jax, jax.numpy as jnp
        import numpy as np
        import math
        B, S, H = (4, 128, 128)
        NQ, NKV = (16, 8)
        HD = H // NQ
        G = HD * NKV
        DEPTH = 1
        LAMBDA_INIT = 0.8 - 0.6 * math.exp(-0.3 * DEPTH)
        Bx, Sx, Hx = x.shape
        qkv = x @ Wqkv
        q = qkv[..., :2 * Hx].reshape(Bx, 2 * NQ, Sx, HD)
        k = qkv[..., 2 * Hx:2 * Hx + G].reshape(Bx, NKV, Sx, HD)
        v = qkv[..., 2 * Hx + G:].reshape(Bx, NKV, Sx, HD)
        k = jnp.repeat(k, 2 * NQ // NKV, axis=1)
        v = jnp.repeat(v, NQ // NKV, axis=1)
        scores = jnp.einsum('bhqd,bhkd->bhqk', q, k) / math.sqrt(HD)
        causal = jnp.tril(jnp.ones((Sx, Sx), dtype=bool))
        scores = jnp.where(causal, scores, -jnp.inf)
        aw = jax.nn.softmax(scores, axis=-1)
        lam1 = jnp.exp(jnp.sum(lambda_q1 * lambda_k1))
        lam2 = jnp.exp(jnp.sum(lambda_q2 * lambda_k2))
        lam = lam1 - lam2 + LAMBDA_INIT
        aw = aw.reshape(Bx, NQ, 2, Sx, Sx)
        aw = aw[:, :, 0] - lam * aw[:, :, 1]
        attn = jnp.einsum('bhqk,bhkd->bhqd', aw, v) * (1.0 - LAMBDA_INIT)
        attn = jnp.transpose(attn, (0, 2, 1, 3)).reshape(Bx, Sx, Hx)
        y = attn @ Wproj
        y = jnp.transpose(y, (0, 2, 1)).reshape(Bx, Sx, Hx)
        return y @ Wproj

    def _L1_ffn_ref(x, Wqkv, q_scale, k_scale, Wo, ln_g, ln_b, W1, b1, W2, b2):
        import jax, jax.numpy as jnp
        import numpy as np
        DIM = 128
        DEPTH = 6
        HEADS = 16
        DIM_HEAD = 64
        WINDOW = 32
        INNER = HEADS * DIM_HEAD
        DIM_INNER = int(DIM * 4 * 2 / 3)
        QK_SCALE = 8.0

        def shift_tokens(t):
            a, s = jnp.split(t, 2, -1)
            s = jnp.pad(s, ((0, 0), (1, 0), (0, 0)))[:, :-1]
            return jnp.concatenate([a, s], -1)

        def l2norm(t):
            return t / jnp.maximum(jnp.linalg.norm(t, axis=-1, keepdims=True), 1e-12)

        def rotate_half(x):
            x1, x2 = jnp.split(x, 2, -1)
            return jnp.concatenate([-x2, x1], -1)

        def rotary_tables(n):
            half = jnp.arange(0, DIM_HEAD, 2, dtype=jnp.float32)
            inv_freq = 1.0 / 10000.0 ** (half / DIM_HEAD)
            t = jnp.arange(n, dtype=jnp.float32)
            freqs = t[:, None] * inv_freq[None, :]
            freqs = jnp.concatenate([freqs, freqs], -1)
            base_scale = (half + 0.4 * DIM_HEAD) / (1.4 * DIM_HEAD)
            power = (t - n // 2) / (WINDOW // 2)
            scale = base_scale[None, :] ** power[:, None]
            scale = jnp.concatenate([scale, scale], -1)
            return (freqs, scale)

        def local_attention(q, k, v):
            b, h, n, d = q.shape
            w = WINDOW
            nw = n // w
            bq = q.reshape(b, h, nw, w, d)
            bk = k.reshape(b, h, nw, w, d)
            bv = v.reshape(b, h, nw, w, d)

            def look(t):
                p = jnp.pad(t, ((0, 0), (0, 0), (1, 0), (0, 0), (0, 0)))
                return jnp.concatenate([p[:, :, :nw], p[:, :, 1:]], axis=3)
            bk2, bv2 = (look(bk), look(bv))
            seq = jnp.arange(n).reshape(nw, w)
            seq_p = jnp.pad(seq, ((1, 0), (0, 0)), constant_values=-1)
            jt = jnp.concatenate([seq_p[:nw], seq_p[1:]], axis=1)
            it = seq[:, :, None]
            jb = jt[:, None, :]
            mask = (it < jb) | (it > jb + w) | (jb == -1)
            sim = jnp.einsum('bhwie,bhwje->bhwij', bq, bk2) * QK_SCALE
            sim = jnp.where(mask, -jnp.finfo(sim.dtype).max, sim)
            attn = jax.nn.softmax(sim, -1)
            out = jnp.einsum('bhwij,bhwje->bhwie', attn, bv2)
            return out.reshape(b, h, n, d)

        def attn_layer(x, Wqkv, qs, ksc, Wo):
            b, n, _ = x.shape
            qkv = x @ Wqkv
            q, k, v = jnp.split(qkv, 3, -1)
            sh = lambda t: t.reshape(b, n, HEADS, DIM_HEAD).transpose(0, 2, 1, 3)
            q, k, v = (sh(q), sh(k), sh(v))
            q = l2norm(q) * qs
            k = l2norm(k) * ksc
            freqs, scale = rotary_tables(n)
            cos, sin = (jnp.cos(freqs), jnp.sin(freqs))
            q = q * cos * scale + rotate_half(q) * sin * scale
            inv = 1.0 / scale
            k = k * cos * inv + rotate_half(k) * sin * inv
            out = local_attention(q, k, v)
            out = out.transpose(0, 2, 1, 3).reshape(b, n, INNER)
            return out @ Wo

        def ffn_layer(x, g, bln, W1, b1, W2, b2):
            mu = x.mean(-1, keepdims=True)
            var = ((x - mu) ** 2).mean(-1, keepdims=True)
            xn = (x - mu) / jnp.sqrt(var + 1e-05) * g + bln
            hg = xn @ W1 + b1
            a, gate = jnp.split(hg, 2, -1)
            return a * jax.nn.gelu(gate, approximate=False) @ W2 + b2
        for i in range(DEPTH):
            x = attn_layer(shift_tokens(x), Wqkv[i], q_scale[i], k_scale[i], Wo[i]) + x
            x = ffn_layer(shift_tokens(x), ln_g[i], ln_b[i], W1[i], b1[i], W2[i], b2[i]) + x
        return x
    x = L0_attn_hidden_states
    xn = _layernorm(x, axis=-1)
    s = _L0_attn_ref(xn, L0_attn_Wq, L0_attn_bq, L0_attn_Wk, L0_attn_bk, L0_attn_Wv, L0_attn_bv, L0_attn_Wo, L0_attn_bo, L0_attn_rel_emb, L0_attn_M, L0_attn_z, L0_attn_gate_alpha)
    g = _silu(_L0_ffn_ref(xn, L0_ffn_gate_w, L0_ffn_gate_bias, L0_ffn_w_gate, L0_ffn_w_up, L0_ffn_w_down, L0_ffn_sh_gate, L0_ffn_sh_up, L0_ffn_sh_down))
    x = x + s * g
    xn = _layernorm(x, axis=-1)
    s = _L1_attn_ref(xn, L1_attn_Wqkv, L1_attn_Wproj, L1_attn_lambda_q1, L1_attn_lambda_k1, L1_attn_lambda_q2, L1_attn_lambda_k2)
    g = _silu(_L1_ffn_ref(xn, L1_ffn_Wqkv, L1_ffn_q_scale, L1_ffn_k_scale, L1_ffn_Wo, L1_ffn_ln_g, L1_ffn_ln_b, L1_ffn_W1, L1_ffn_b1, L1_ffn_W2, L1_ffn_b2))
    x = x + s * g
    return x

_drawn_inputs = setup_inputs


def setup_inputs(seed=0):
    import zlib

    import numpy as np

    out = dict(_drawn_inputs(seed))
    spreads = {'L0_attn_bq': (0.0, 0.1),
     'L0_attn_bk': (0.0, 0.1),
     'L0_attn_bv': (0.0, 0.1),
     'L0_attn_bo': (0.0, 0.1),
     'L1_ffn_q_scale': (1.0, 0.2),
     'L1_ffn_k_scale': (1.0, 0.2),
     'L1_ffn_ln_g': (1.0, 0.2),
     'L1_ffn_ln_b': (0.0, 0.1),
     'L1_ffn_b1': (0.0, 0.1),
     'L1_ffn_b2': (0.0, 0.1)}
    factors = {}
    for name, (base, spread) in spreads.items():
        noise = np.random.default_rng([zlib.crc32(name.encode()), seed]).standard_normal(out[name].shape)
        drawn = base * np.exp(spread * noise) if base else spread * noise
        out[name] = jnp.asarray(drawn.astype(out[name].dtype))
    for name, factor in factors.items():
        out[name] = (out[name] * factor).astype(out[name].dtype)
    return out
```

```python
from contextlib import ExitStack

import concourse.bass as bass
from concourse import mybir

F32 = mybir.dt.float32
BF16 = mybir.dt.bfloat16
ALU = mybir.AluOpType
ACT = mybir.ActivationFunctionType
AX = mybir.AxisListType

P = 128
B, S, D = 2, 1024, 128
T = B * S
NT = T // P
CH = 512
NC = T // CH
ST = S // P
LN_EPS = 1e-5

HD = 8
H0 = 16
NREL = 257
NPACK = 6
KROWS = NPACK * HD
QPART = (0, 0, 1, 1, 0, 2)
KPART = (0, 1, 0, 1, 2, 0)
VW = 32
SCALE = float(1.0 / (HD ** 0.5))


class Chain:

    def __init__(self, eng, sem, start=0, per=0, turn=None):
        self.eng, self.sem, self.n, self.per, self.turn, self.start = eng, sem, start, per, turn, start

    def value(self):
        return self.n if self.turn is None else self.turn * self.per + self.n

    def __call__(self, ins):
        self.n += 1
        ins.then_inc(self.sem, 1)
        self.eng.wait_ge(self.sem, self.value())

    def end(self):
        assert self.turn is None or self.n - self.start == self.per, (self.n - self.start, self.per)
        return self.start + self.per


class Stage:

    def __init__(self, nc, name):
        self.nc, self.name, self.ctx, self.sems = nc, name, ExitStack(), []

    def __enter__(self):
        self.ctx.__enter__()
        return self

    def __exit__(self, *a):
        done = self.ctx.__exit__(*a)
        if a[0] is None:
            self.nc.clear_and_free_semaphores(self.sems)
            self.nc.all_engine_barrier()
        return done

    def sb(self, name, shape, dt=F32):
        return self.ctx.enter_context(self.nc.sbuf_tensor(f"{self.name}_{name}", shape, dt))

    def ps(self, name, shape, dt=F32):
        return self.ctx.enter_context(self.nc.psum_tensor(f"{self.name}_{name}", shape, dt))

    def sem(self, name):
        self.sems.append(self.nc.alloc_semaphore(f"{self.name}_{name}"))
        return self.sems[-1]

    def block(self):
        return self.ctx.enter_context(self.nc.Block())


def stage_norm(nc, name, ident, xT, xnT, x_dram=None, ident_dram=None):
    with Stage(nc, name) as st:
        x = st.sb("x", [P, NT, D])
        xc = st.sb("xc", [P, NT, D])
        sq = st.sb("sq", [P, NT, D])
        small = st.sb("small", [P, 4, NT])
        ps = st.ps("turned", [P, 8, CH])
        loaded, tokens_turned, tokens_ready = st.sem("loaded"), st.sem("tokens_turned"), st.sem("tokens_ready")
        var_ready, std_ready, normed = st.sem("var_ready"), st.sem("std_ready"), st.sem("normed")
        turned, chain = st.sem("turned"), st.sem("chain")
        block = st.block()

        @block.sync
        def _(sp):
            if x_dram is not None:
                sp.dma_start(ident[:], ident_dram).then_inc(loaded, 16)
                sp.dma_start(x[:], x_dram.rearrange("(n p) d -> p n d", p=P)).then_inc(loaded, 16)

        @block.tensor
        def _(pe):
            if x_dram is not None:
                pe.wait_ge(loaded, 32)
            for n in range(NT):
                src = x[:, n, :] if x_dram is not None else xT[:, n * P:(n + 1) * P]
                mm = pe.transpose(ps[:, n // 4, (n % 4) * P:(n % 4 + 1) * P], src, ident[:])
                if n % 4 == 3:
                    mm.then_inc(tokens_turned, 1)
            pe.wait_ge(normed, 1)
            for n in range(NT):
                mm = pe.transpose(ps[:, 4 + n // 4, (n % 4) * P:(n % 4 + 1) * P], xc[:, n, :], ident[:])
                if n % 4 == 3:
                    mm.then_inc(turned, 1)

        @block.scalar
        def _(act):
            for c in range(NC):
                act.wait_ge(tokens_turned, c + 1)
                if x_dram is not None:
                    dst = xT[:, c * CH:(c + 1) * CH]
                else:
                    dst = x[:, 4 * c:4 * c + 4, :].rearrange("p n d -> p (n d)")
                act.copy(dst, ps[:, c, :]).then_inc(tokens_ready, 1)
            act.wait_ge(var_ready, 1)
            act.activation(small[:, 2, :], small[:, 1, :], ACT.Sqrt).then_inc(std_ready, 1)

        @block.vector
        def _(dve):
            link = Chain(dve, chain)
            if x_dram is not None:
                dve.wait_ge(loaded, 32)
            else:
                dve.wait_ge(tokens_ready, NC)
            mean, var, std = small[:, 0, :], small[:, 1, :], small[:, 2, :]
            link(dve.tensor_reduce(mean, x[:], AX.X, ALU.add))
            link(dve.tensor_scalar(mean, mean, 1.0 / D, None, ALU.mult))
            link(dve.tensor_tensor(xc[:], x[:], mean.unsqueeze(2).broadcast_to((P, NT, D)), ALU.subtract))
            link(dve.tensor_tensor(sq[:], xc[:], xc[:], ALU.mult))
            link(dve.tensor_reduce(var, sq[:], AX.X, ALU.add))
            dve.tensor_scalar(var, var, 1.0 / D, LN_EPS, ALU.mult, ALU.add).then_inc(var_ready, 1)
            dve.wait_ge(std_ready, 1)
            link(dve.reciprocal(small[:, 3, :], std))
            dve.tensor_tensor(xc[:], xc[:], small[:, 3, :].unsqueeze(2).broadcast_to((P, NT, D)),
                              ALU.mult).then_inc(normed, 1)
            for c in range(NC):
                dve.wait_ge(turned, c + 1)
                dve.tensor_copy(xnT[:, c * CH:(c + 1) * CH], ps[:, 4 + c, :])


def split_parts(link, dve, src, hi, mid, lo, r1, r2):
    link(dve.tensor_copy(hi, src))
    link(dve.tensor_tensor(r1, src, hi, ALU.subtract))
    link(dve.tensor_copy(mid, r1))
    link(dve.tensor_tensor(r2, r1, mid, ALU.subtract))
    link(dve.tensor_copy(lo, r2))


def stage_project0(nc, d, xnT, qT, vaug, relmax):
    with Stage(nc, "proj0") as st:
        wq, wk, wv = st.sb("wq", [P, D]), st.sb("wk", [P, D]), st.sb("wv", [P, D])
        bq, bk, bv = st.sb("bq", [P, 1]), st.sb("bk", [P, 1]), st.sb("bv", [P, D])
        rel = st.sb("rel", [P, NREL])
        kT = st.sb("kT", [P, 3, T])
        parts = st.sb("parts", [P, 4, 3, T], BF16)
        r1, r2 = st.sb("r1", [P, T]), st.sb("r2", [P, T])
        ones = st.sb("ones", [P, S], BF16)
        ps = st.ps("qkv", [P, 8, CH])
        loaded, mm_done, copied, chain = st.sem("loaded"), st.sem("mm_done"), st.sem("copied"), st.sem("chain")
        v_mm, split_done, stored = st.sem("v_mm"), st.sem("split_done"), st.sem("stored")
        ones_ready, v_copied = st.sem("ones_ready"), st.sem("v_copied")
        block = st.block()

        @block.sync
        def _(sp):
            for dst, src in ((wq, d["wqT"]), (wk, d["wkT"]), (wv, d["wvT"]), (bq, d["bq"]), (bk, d["bk"]),
                             (rel, d["rel_rows"])):
                sp.dma_start(dst[:], src).then_inc(loaded, 16)
            sp.dma_start(bv[:], d["bv"].partition_broadcast(P)).then_inc(loaded, 16)
            sp.wait_ge(ones_ready, 1)
            n = 0
            for v in range(3):
                sp.dma_start(d["kp"][v, 0:B * H0, KROWS, :], ones[0:B * H0, :]).then_inc(stored, 16)
                sp.dma_start(d["kp"][v, B * H0:, :, :].rearrange("h r s -> (h r) s"),
                             ones[0:2 * (KROWS + 1), :]).then_inc(stored, 16)
                n += 2
            for v in range(4):
                sp.wait_ge(split_done, v + 1)
                for blk in range(NPACK):
                    part = (QPART if v == 0 else KPART)[blk]
                    for b in range(B):
                        pack = d["qp"] if v == 0 else d["kp"][v - 1]
                        for h0 in range(0, H0, H0):
                            dst = pack[b * H0:(b + 1) * H0, blk * HD:(blk + 1) * HD, :]
                            sp.dma_start(dst, parts[:, v, part, b * S:(b + 1) * S]).then_inc(stored, 16)
                            n += 1
            sp.wait_ge(stored, 16 * n)

        @block.tensor
        def _(pe):
            pe.wait_ge(loaded, 16 * 7)
            for c in range(NC):
                cols = xnT[:, c * CH:(c + 1) * CH]
                if c >= 2:
                    pe.wait_ge(copied, 2 * c - 2)
                pe.matmul(ps[:, 2 * (c % 2), :], wq[:], cols, start=True, stop=True).then_inc(mm_done, 1)
                pe.matmul(ps[:, 2 * (c % 2) + 1, :], wk[:], cols, start=True, stop=True).then_inc(mm_done, 1)
            for n in range(NT):
                mm = pe.matmul(ps[:, 4 + n // 4, (n % 4) * P:(n % 4 + 1) * P], xnT[:, n * P:(n + 1) * P], wv[:],
                               start=True, stop=True)
                if n % 4 == 3:
                    mm.then_inc(v_mm, 1)

        @block.scalar
        def _(act):
            for c in range(NC):
                act.wait_ge(mm_done, 2 * c + 1)
                act.activation(qT[:, c * CH:(c + 1) * CH], ps[:, 2 * (c % 2), :], ACT.Identity,
                               bias=bq[:, 0:1]).then_inc(copied, 1)
                act.wait_ge(mm_done, 2 * c + 2)
                act.activation(kT[:, 0, c * CH:(c + 1) * CH], ps[:, 2 * (c % 2) + 1, :], ACT.Identity,
                               bias=bk[:, 0:1]).then_inc(copied, 1)

        @block.vector
        def _(dve):
            link = Chain(dve, chain)
            dve.memset(ones[:], 1.0).then_inc(ones_ready, 1)
            dve.memset(vaug[:], 1.0).then_inc(v_copied, 1)
            dve.wait_ge(loaded, 16 * 7)
            dve.tensor_reduce(relmax[:, 0:1], rel[:], AX.X, ALU.max)
            dve.tensor_reduce(relmax[:, 1:2], rel[:], AX.X, ALU.min)
            dve.wait_ge(copied, 2 * NC)
            link(dve.tensor_scalar(kT[:, 1, :], kT[:, 0, :], rel[:, 0:1], None, ALU.add))
            link(dve.tensor_scalar(kT[:, 2, :], kT[:, 0, :], rel[:, NREL - 1:NREL], None, ALU.add))
            for v in range(4):
                src = qT[:] if v == 0 else kT[:, v - 1, :]
                link(dve.tensor_copy(parts[:, v, 0, :], src))
                link(dve.tensor_tensor(r1[:], src, parts[:, v, 0, :], ALU.subtract))
                link(dve.tensor_copy(parts[:, v, 1, :], r1[:]))
                link(dve.tensor_tensor(r2[:], r1[:], parts[:, v, 1, :], ALU.subtract))
                link(dve.tensor_copy(parts[:, v, 2, :], r2[:]))
                dve.sem_inc(split_done, 1)
            dve.wait_ge(v_copied, 1)
            for c in range(NC):
                dve.wait_ge(v_mm, c + 1)
                for u in range(4):
                    n = 4 * c + u
                    b, J = n // ST, n % ST
                    dve.tensor_tensor(vaug[:, b * H0:(b + 1) * H0, J, 0:HD],
                                      ps[:, 4 + c, u * P:(u + 1) * P].rearrange("p (h e) -> p h e", e=HD),
                                      bv[:].rearrange("p (h e) -> p h e", e=HD), ALU.add)


def stage_max0(nc, d, ident, qT, relmax):
    NH = B * H0
    with Stage(nc, "max0") as st:
        qh = st.sb("qh", [P, 2, S], BF16)
        kh = st.sb("kh", [P, 2, S], BF16)
        mcol = st.sb("mcol", [P, ST, NH])
        headsel = st.sb("headsel", [P, H0])
        relsel = st.sb("relsel", [P, 2, 2, NH])
        qpos, qneg = st.sb("qpos", [P, T]), st.sb("qneg", [P, T])
        mrow = st.sb("mrow", [NH, S], BF16)
        ps = st.ps("scores", [P, 4, 2 * CH])
        loaded = [st.sem("loaded0"), st.sem("loaded1")]
        zeroed, scored, maxed = st.sem("zeroed"), st.sem("scored"), st.sem("maxed")
        sel_loaded, bound_ready, rows, rows_out = (st.sem("sel_loaded"), st.sem("bound_ready"), st.sem("rows"),
                                                   st.sem("rows_out"))
        stored, chain, head_used = st.sem("stored"), st.sem("chain"), st.sem("head_used")
        block = st.block()

        @block.sync
        def _(sp):
            sp.dma_start(headsel[:], d["headsel"]).then_inc(sel_loaded, 16)
            sp.wait_ge(zeroed, 1)

            def load(bh, slot):
                sp.dma_start(qh[0:KROWS, slot, :], d["qp"][bh, 0:KROWS, :]).then_inc(loaded[slot], 16)
                sp.dma_start(kh[0:KROWS, slot, :], d["kp"][0, bh, 0:KROWS, :]).then_inc(loaded[slot], 16)

            load(0, 0)
            load(1, 1)
            with sp.Fori(0, NH // 2 - 1) as i:
                for s in range(2):
                    sp.wait_ge(head_used, 2 * i + s + 1)
                    load(2 * i + 2 + s, s)
            sp.wait_ge(rows_out, 2)
            sp.dma_start(d["qp"][:, KROWS, :], mrow[:]).then_inc(stored, 16)
            sp.wait_ge(stored, 16)

        @block.gpsimd
        def _(pool):
            pool.memset(qh[:], 0.0)
            pool.memset(kh[:], 0.0).then_inc(zeroed, 1)

        @block.tensor
        def _(pe):
            with pe.Fori(0, NH // 2) as i:
                for s in range(2):
                    pe.wait_ge(loaded[s], 32 * i + 32)
                    for u in range(ST):
                        pe.wait_ge(maxed, (2 * i + s) * ST + u + 1)
                        for c in range(2):
                            mm = pe.matmul(ps[:, u % 4, c * CH:(c + 1) * CH], qh[:, s, u * P:(u + 1) * P],
                                           kh[:, s, c * CH:(c + 1) * CH], start=True, stop=True)
                        mm.then_inc(scored, 1)
                        if u == ST - 1:
                            pass
            pe.wait_ge(bound_ready, 1)
            pe.wait_ge(maxed, NH * ST + 4)
            for u in range(ST):
                out = ps[0:NH, 0, u * P:(u + 1) * P]
                pe.matmul(out, mcol[:, u, :], ident[:], start=True, stop=False)
                for b in range(B):
                    cols = slice(b * S + u * P, b * S + (u + 1) * P)
                    pe.matmul(out, relsel[:, 0, b, :], qpos[:, cols], start=False, stop=False)
                    mm = pe.matmul(out, relsel[:, 1, b, :], qneg[:, cols], start=False, stop=(b == B - 1))
                if u % 4 == 3:
                    mm.then_inc(rows, 1)

        @block.scalar
        def _(act):
            for c in range(2):
                act.wait_ge(rows, c + 1)
                act.mul(mrow[:, c * CH:(c + 1) * CH], ps[0:NH, 0, c * CH:(c + 1) * CH], -1.0).then_inc(rows_out, 1)

        @block.vector
        def _(dve):
            link = Chain(dve, chain)
            dve.sem_inc(maxed, 4)
            link(dve.tensor_scalar(qpos[:], qT[:], 0.0, None, ALU.max))
            link(dve.tensor_scalar(qneg[:], qT[:], 0.0, None, ALU.min))
            link(dve.memset(relsel[:], 0.0))
            dve.wait_ge(sel_loaded, 16)
            for w in range(2):
                for b in range(B):
                    link(dve.tensor_scalar(relsel[:, w, b, b * H0:(b + 1) * H0], headsel[:], relmax[:, w:w + 1],
                                           None, ALU.mult))
            dve.sem_inc(bound_ready, 1)
            with dve.Fori(0, NH // 2) as i:
                for s in range(2):
                    for u in range(ST):
                        dve.wait_ge(scored, (2 * i + s) * ST + u + 1)
                        ins = dve.tensor_reduce(mcol[:, u, bass.ds(2 * i + s, 1)], ps[:, u % 4, :], AX.X, ALU.max)
                        ins.then_inc(maxed, 1)
                        if u == ST - 1:
                            dve.sem_inc(head_used, 1)


def stage_attend0(nc, d, vaug):
    NH = B * H0
    G = 8
    NG = NH // G
    U = CH // (ST * G)
    NW = 3 * P // U
    HALF = NW // 2
    with Stage(nc, "att0") as st:
        relrow = st.sb("relrow", [HD, CH])
        relparts = st.sb("relparts", [HD, 3, CH], BF16)
        relr = st.sb("relr", [HD, 2, CH])
        relpack = st.sb("relpack", [P, CH], BF16)
        qg = st.sb("qg", [P, G, S], BF16)
        rel = st.sb("rel", [P, 3, P, ST, G])
        kh = st.sb("kh", [P, 2, 3, S], BF16)
        pr = st.sb("pr", [P, 4, S])
        vh = st.sb("vh", [P, 2, ST, VW])
        ob = st.sb("ob", [P, 2, CH])
        ps = st.ps("ps", [P, 8, CH])
        rel_loaded, rel_split, chain = st.sem("rel_loaded"), st.sem("rel_split"), st.sem("chain")
        rel_packed, zeroed = st.sem("rel_packed"), st.sem("zeroed")
        q_loaded = st.sem("q_loaded")
        k_loaded = [st.sem("k_loaded0"), st.sem("k_loaded1")]
        stored = [st.sem("stored0"), st.sem("stored1")]
        win_done, win_act, win_dve = st.sem("win_done"), st.sem("win_act"), st.sem("win_dve")
        qk_done, rel_added, exp_done = st.sem("qk_done"), st.sem("rel_added"), st.sem("exp_done")
        pv_done, out_copied, v_copied = st.sem("pv_done"), st.sem("out_copied"), st.sem("v_copied")
        turns_begun = st.sem("turns_begun")
        block = st.block()

        @block.sync
        def _(sp):
            sp.dma_start(relrow[:], d["rel_reversed"]).then_inc(rel_loaded, 16)
            sp.wait_ge(zeroed, 1)
            sp.wait_ge(rel_split, 1)
            for blk in range(NPACK):
                sp.dma_start(relpack[blk * HD:(blk + 1) * HD, :], relparts[:, KPART[blk], :]).then_inc(rel_packed, 16)

            def load_k(bh, slot):
                sp.dma_start(kh[0:KROWS + 1, slot, :, :],
                             d["kp"][:, bh, :, :].rearrange("v r s -> r v s")).then_inc(k_loaded[slot], 16)

            def load_q(g):
                sp.dma_start(qg[0:KROWS + 1, :, :],
                             d["qp"][bass.ds(g * G, G), :, :].rearrange("h r s -> r h s")).then_inc(q_loaded, 16)

            def store(row, slot):
                for quad in range(4):
                    sp.dma_start(d["o0"][row, quad // 2, :, (quad % 2) * CH:(quad % 2 + 1) * CH],
                                 ob[32 * quad:32 * quad + HD + 1, slot, :]).then_inc(stored[slot], 16)

            load_k(0, 0)
            load_k(1, 1)
            with sp.Fori(0, NG) as g:
                sp.wait_ge(qk_done, g * G * ST + 1)
                load_q(g)
                with sp.Fori(0, G // 2) as i:
                    for s in range(2):
                        bh = g * G + 2 * i + s
                        sp.wait_ge(out_copied, bh + 3)
                        store(bh, 1 - s)
                        sp.wait_ge(qk_done, (bh + 1) * ST + 1)
                        load_k(bh + 2, s)
            sp.wait_ge(out_copied, NH + 3)
            store(NH, 1)
            for s in range(2):
                sp.wait_ge(stored[s], 16 + 64 * (NH // 2 + s))
                sp.wait_ge(k_loaded[s], 16 * (NH // 2 + 1))

        @block.gpsimd
        def _(pool):
            pool.memset(relpack[:], 0.0)
            pool.memset(qg[:], 0.0)
            pool.memset(kh[:], 0.0)
            pool.memset(pr[:], 0.0)
            pool.memset(vh[:], 0.0).then_inc(zeroed, 1)
            pool.wait_ge(zeroed, 1)
            with pool.Fori(0, NH // 2) as i:
                for s in range(2):
                    bh = 2 * i + s
                    pool.wait_ge(pv_done, bh * (ST // 2) + 1)
                    pool.tensor_copy(vh[:, s, :, 0:HD + 1], vaug[:, bass.ds(bh, 1), :, :]).then_inc(v_copied, 1)

        @block.tensor
        def _(pe):
            def qk(h, slot, J, n):
                pe.wait_ge(exp_done, n + 1)
                near = (max(J - 1, 0) * P, min(J + 2, ST) * P)
                for v, lo, hi in ((1, 0, near[0]), (0, *near), (2, near[1], S)):
                    while lo < hi:
                        end = min(hi, CH if lo < CH else S)
                        mm = pe.matmul(ps[:, 2 * (J % 2) + lo // CH, lo % CH:(end - 1) % CH + 1],
                                       kh[:, slot, v, J * P:(J + 1) * P], qg[:, h, lo:end], start=True, stop=True)
                        lo = end
                mm.then_inc(qk_done, 1)

            def pv(slot, m, n):
                pe.wait_ge(exp_done, n + 3)
                for J in (2 * m, 2 * m + 1):
                    for c in range(2):
                        quad = 32 * (2 * (J % 2) + c)
                        mm = pe.matmul(ps[quad:quad + VW, 6 + slot, :], vh[:, slot, J, :],
                                       pr[:, J % 4, c * CH:(c + 1) * CH], start=(m == 0), stop=(m == ST // 2 - 1),
                                       skip_group_check=True, tile_position=(0, quad))
                mm.then_inc(pv_done, 1)

            pe.sem_inc(qk_done, 1)
            pe.wait_ge(zeroed, 1)
            pe.wait_ge(out_copied, 2)
            pe.wait_ge(rel_packed, 16 * NPACK)
            with pe.Fori(0, NG) as g:
                pe.wait_ge(q_loaded, 16 * g + 16)
                pe.wait_ge(exp_done, g * G * ST + 2)
                for k in range(NW):
                    pe.wait_ge((win_act, win_dve)[k % 2], g * HALF + k // 2 + 1)
                    for u in range(U):
                        ii = (k // 3) * U + u
                        mm = pe.matmul(ps[:, k % 6, u * ST * G:(u + 1) * ST * G],
                                       relpack[:, 255 - P * (k % 3 - 1) - ii:][:, 0:P],
                                       qg[:].rearrange("p h (t i) -> p t h i", i=P)[:, :, :, ii],
                                       start=True, stop=True)
                    mm.then_inc(win_done, 1)
                pe.wait_ge(win_act, (g + 1) * HALF + 3)
                pe.wait_ge(win_dve, (g + 1) * HALF + 3)
                pe.sem_inc(turns_begun, 1)
                with pe.Fori(0, G // 2) as i:
                    for s in range(2):
                        bh = g * G + 2 * i + s
                        pe.wait_ge(k_loaded[s], (g * (G // 2) + i) * 16 + 16)
                        for m in range(ST // 2):
                            n = bh * ST + 2 * m
                            qk(bass.ds(2 * i + s, 1), s, 2 * m, n)
                            qk(bass.ds(2 * i + s, 1), s, 2 * m + 1, n + 1)
                            if m == 0:
                                pv(1 - s, ST // 2 - 1, n - 1)
                                pe.wait_ge(v_copied, bh + 1)
                                pe.wait_ge(out_copied, bh + 2)
                            else:
                                pv(s, m - 1, n - 1)
            pv(1, ST // 2 - 1, NH * ST - 1)

        @block.scalar
        def _(act):
            act.sem_inc(exp_done, 2)
            act.sem_inc(win_act, 3)
            act.wait_ge(zeroed, 1)
            with act.Fori(0, NG) as g:
                act.wait_ge(rel_added, g * G * ST + 1)
                for k in range(0, NW, 2):
                    act.wait_ge(win_done, g * NW + k + 1)
                    act.copy(rel[:, k % 3, (k // 3) * U:(k // 3 + 1) * U, :, :].rearrange("p a b c -> p (a b c)"),
                             ps[:, k % 6, :]).then_inc(win_act, 1)
                with act.Fori(0, G) as h:
                    for J in range(ST):
                        bh = g * G + h
                        act.wait_ge(rel_added, bh * ST + J + 2)
                        act.wait_ge(pv_done, bh * (ST // 2) + J // 2 + 4)
                        act.activation(pr[:, J % 4, :],
                                       ps[:, 2 * (J % 2):2 * (J % 2) + 2, :].rearrange("p a b -> p (a b)"),
                                       ACT.Exp, scale=SCALE).then_inc(exp_done, 1)

        @block.vector
        def _(dve):
            link = Chain(dve, chain)
            dve.sem_inc(win_dve, 3)
            dve.sem_inc(rel_added, 1)
            dve.sem_inc(pv_done, 4)
            dve.sem_inc(stored[0], 16)
            dve.sem_inc(stored[1], 16)
            link(dve.memset(ps[:, 6:8, :], 0.0))
            dve.sem_inc(out_copied, 2)
            dve.wait_ge(rel_loaded, 16)
            split_parts(link, dve, relrow[:], relparts[:, 0, :], relparts[:, 1, :], relparts[:, 2, :],
                        relr[:, 0, :], relr[:, 1, :])
            dve.sem_inc(rel_split, 1)

            def copy_out(slot, bh_done, rounds):
                dve.wait_ge(pv_done, bh_done * (ST // 2) + 5)
                dve.wait_ge(stored[slot], rounds)
                dve.tensor_copy(ob[:, slot, :], ps[:, 6 + slot, :]).then_inc(out_copied, 1)

            with dve.Fori(0, NG) as g:
                for k in range(1, NW, 2):
                    dve.wait_ge(win_done, g * NW + k + 1)
                    dve.tensor_copy(
                        rel[:, k % 3, (k // 3) * U:(k // 3 + 1) * U, :, :].rearrange("p a b c -> p (a b c)"),
                        ps[:, k % 6, :]).then_inc(win_dve, 1)
                dve.wait_ge(win_act, (g + 1) * HALF + 3)
                dve.wait_ge(win_dve, (g + 1) * HALF + 3)
                dve.sem_inc(turns_begun, 1)
                with dve.Fori(0, G // 2) as i:
                    for s in range(2):
                        bh = g * G + 2 * i + s
                        for J in range(ST):
                            dve.wait_ge(qk_done, bh * ST + J + 2)
                            for D_ in range(3):
                                I = J + D_ - 1
                                if not 0 <= I < ST:
                                    continue
                                sc = ps[:, 2 * (J % 2) + I // 4, (I % 4) * P:(I % 4 + 1) * P]
                                ins = dve.tensor_tensor(sc, sc, rel[:, D_, :, I, bass.ds(2 * i + s, 1)], ALU.add)
                            ins.then_inc(rel_added, 1)
                            if J == 3:
                                copy_out(1 - s, bh, 16 + 64 * (g * (G // 2) + i))
            copy_out(1, NH, 16 + 64 * (NH // 2))


def stage_combine0(nc, d, qT, sT):
    with Stage(nc, "comb0") as st:
        num, den = st.sb("num", [P, 2, T]), st.sb("den", [P, 2, T])
        wo, bo, mrep, z, blk = (st.sb("wo", [P, D]), st.sb("bo", [P, 1]), st.sb("mrep", [P, P]), st.sb("z", [P, 1]),
                                st.sb("blk", [P, P]))
        mblk, zblk = st.sb("mblk", [P, P]), st.sb("zblk", [P, P])
        gate = st.sb("gate", [P, 3])
        sig, neg = st.sb("sig", [P, T]), st.sb("neg", [P, T])
        ps = st.ps("ps", [P, 8, CH])
        weights, sums, chain = st.sem("weights"), st.sem("sums"), st.sem("chain")
        neg_ready, exp_ready, blocks_ready, glob = (st.sem("neg_ready"), st.sem("exp_ready"),
                                                    st.sem("blocks_ready"), st.sem("glob"))
        gate_ready, mixed, projected = st.sem("gate_ready"), st.sem("mixed"), st.sem("projected")
        block = st.block()

        @block.sync
        def _(sp):
            for dst, src in ((wo, d["woT"]), (bo, d["bo"]), (mrep, d["mrep"]), (z, d["z"]), (blk, d["headblk"])):
                sp.dma_start(dst[:], src).then_inc(weights, 16)
            sp.dma_start(gate[:, 0:1], d["alpha"].partition_broadcast(P)).then_inc(weights, 16)
            for quad in range(2):
                for b in range(B):
                    rows = d["o0"][1 + b * H0:1 + (b + 1) * H0, quad, :, :]
                    sp.dma_start(num[:, quad, b * S:(b + 1) * S], rows[:, 0:HD, :]).then_inc(sums, 16)
                    sp.dma_start(den[:, quad, b * S:(b + 1) * S],
                                 rows[:, HD:HD + 1, :].broadcast_to((H0, HD, S))).then_inc(sums, 16)

        @block.scalar
        def _(act):
            act.wait_ge(weights, 16 * 6)
            act.activation(gate[:, 1:2], gate[:, 0:1], ACT.Sigmoid).then_inc(gate_ready, 1)
            act.wait_ge(neg_ready, 1)
            act.activation(neg[:], neg[:], ACT.Exp).then_inc(exp_ready, 1)
            for c in range(NC):
                act.wait_ge(projected, c + 1)
                act.activation(sT[:, c * CH:(c + 1) * CH], ps[:, c, :], ACT.Identity, bias=bo[:, 0:1])

        @block.tensor
        def _(pe):
            pe.wait_ge(blocks_ready, 1)
            for c in range(NC):
                pe.matmul(ps[:, c, :], mblk[:], sig[:, c * CH:(c + 1) * CH], start=True, stop=True)
                mm = pe.matmul(ps[:, 4 + c, :], zblk[:], sig[:, c * CH:(c + 1) * CH], start=True, stop=True)
            mm.then_inc(glob, 1)
            pe.wait_ge(mixed, 1)
            for c in range(NC):
                pe.matmul(ps[:, c, :], wo[:], num[:, 0, c * CH:(c + 1) * CH],
                          start=True, stop=True).then_inc(projected, 1)

        @block.vector
        def _(dve):
            link = Chain(dve, chain)
            dve.tensor_scalar(neg[:], qT[:], 0.0, None, ALU.min).then_inc(neg_ready, 1)
            link(dve.tensor_scalar(sig[:], qT[:], 0.0, None, ALU.max))
            dve.wait_ge(weights, 16 * 6)
            link(dve.tensor_tensor(mblk[:], mrep[:], blk[:], ALU.mult))
            link(dve.tensor_scalar(zblk[:], blk[:], z[:, 0:1], None, ALU.mult))
            dve.wait_ge(exp_ready, 1)
            dve.tensor_tensor(sig[:], sig[:], neg[:], ALU.add).then_inc(blocks_ready, 1)
            dve.wait_ge(gate_ready, 1)
            link(dve.tensor_scalar(gate[:, 2:3], gate[:, 1:2], -1.0, 1.0, ALU.mult, ALU.add))
            dve.wait_ge(sums, 16 * 8)
            for x in (num, den):
                link(dve.tensor_tensor(x[:, 0, :], x[:, 0, :], x[:, 1, :], ALU.add))
            link(dve.reciprocal(den[:, 0, :], den[:, 0, :]))
            link(dve.tensor_tensor(num[:, 0, :], num[:, 0, :], den[:, 0, :], ALU.mult))
            dve.wait_ge(glob, 1)
            for c in range(NC):
                g = den[:, 1, c * CH:(c + 1) * CH]
                link(dve.tensor_scalar(g, ps[:, 4 + c, :], 1e-6, None, ALU.add))
                link(dve.reciprocal(g, g))
                link(dve.tensor_tensor(g, g, ps[:, c, :], ALU.mult))
            link(dve.tensor_scalar(den[:, 1, :], den[:, 1, :], gate[:, 2:3], None, ALU.mult))
            dve.scalar_tensor_tensor(num[:, 0, :], num[:, 0, :], gate[:, 1:2], den[:, 1, :], ALU.mult,
                                     ALU.add).then_inc(mixed, 1)


E_, EI = 32, 64
EG, EPG = 8, 4
TOP_GROUPS, TOP_K = 4, 8
ROUTE_SCALE = 2.5


def stage_route(nc, d, xnT):
    with Stage(nc, "route") as st:
        gw, gb = st.sb("gw", [P, E_]), st.sb("gb", [P, E_])
        lower = st.sb("lower", [P, E_, E_])
        score, sc, pick = st.sb("score", [P, NT, E_]), st.sb("sc", [P, NT, E_]), st.sb("pick", [P, NT, E_])
        grp, gsel, t8 = st.sb("grp", [P, NT, EG]), st.sb("gsel", [P, NT, EG]), st.sb("t8", [P, NT, EG])
        cmp_, eq = st.sb("cmp", [P, NT // 4, E_, E_]), st.sb("eq", [P, NT // 4, E_, E_])
        tot = st.sb("tot", [P, NT])
        ident = st.sb("ident", [P, P])
        cT = st.sb("cT", [E_, T])
        ps = st.ps("ps", [P, CH])
        psT = st.ps("psT", [E_, 4, CH])
        loaded, logits, scored, weighted = st.sem("loaded"), st.sem("logits"), st.sem("scored"), st.sem("weighted")
        turned, copied, stored, chain = st.sem("turned"), st.sem("copied"), st.sem("stored"), st.sem("chain")
        block = st.block()

        @block.sync
        def _(sp):
            sp.dma_start(gw[:], d["gate_wT"]).then_inc(loaded, 16)
            sp.dma_start(gb[:], d["gate_bias"].partition_broadcast(P)).then_inc(loaded, 16)
            sp.dma_start(lower[:].rearrange("p a b -> p (a b)"), d["lower"].partition_broadcast(P)).then_inc(loaded, 16)
            sp.dma_start(ident[:], d["ident"]).then_inc(loaded, 16)
            sp.wait_ge(copied, 4)
            sp.dma_start(d["combineT"], cT[:]).then_inc(stored, 16)
            sp.wait_ge(stored, 16)

        @block.tensor
        def _(pe):
            pe.wait_ge(loaded, 64)
            for n in range(NT):
                mm = pe.matmul(ps[:, n * E_:(n + 1) * E_], xnT[:, n * P:(n + 1) * P], gw[:], start=True, stop=True)
            mm.then_inc(logits, 1)
            pe.wait_ge(weighted, 1)
            for n in range(NT):
                mm = pe.transpose(psT[:, n // 4, (n % 4) * P:(n % 4 + 1) * P], pick[:, n, :], ident[:])
                if n % 4 == 3:
                    mm.then_inc(turned, 1)

        @block.scalar
        def _(act):
            act.wait_ge(logits, 1)
            act.activation(score[:].rearrange("p a b -> p (a b)"), ps[:], ACT.Sigmoid).then_inc(scored, 1)
            for c in range(4):
                act.wait_ge(turned, c + 1)
                act.copy(cT[:, c * CH:(c + 1) * CH], psT[:, c, :]).then_inc(copied, 1)

        @block.vector
        def _(dve):
            link = Chain(dve, chain)
            dve.wait_ge(scored, 1)
            dve.wait_ge(loaded, 64)
            link(dve.tensor_tensor(sc[:], score[:], gb[:].unsqueeze(1).broadcast_to((P, NT, E_)), ALU.add))
            v = sc[:].rearrange("p n (g e) -> p n g e", e=EPG)
            pairs = [(i, j) for i in range(EPG) for j in range(i + 1, EPG)]
            for n, (i, j) in enumerate(pairs):
                link(dve.tensor_tensor((t8 if n else grp)[:], v[:, :, :, i], v[:, :, :, j], ALU.add))
                if n:
                    link(dve.tensor_tensor(grp[:], grp[:], t8[:], ALU.max))

            def rank(vals, n_of, q):
                K = n_of
                mine = vals.unsqueeze(3).broadcast_to((P, NT // 4, K, K))
                other = vals.unsqueeze(2).broadcast_to((P, NT // 4, K, K))
                c_, e_ = cmp_[:, :, 0:K, 0:K], eq[:, :, 0:K, 0:K]
                low = lower[:, 0:K, 0:K]
                link(dve.tensor_tensor(c_, other, mine, ALU.is_gt))
                link(dve.tensor_tensor(e_, other, mine, ALU.is_equal))
                for t in range(NT // 4):
                    last = dve.tensor_tensor(e_[:, t], e_[:, t], low, ALU.mult)
                link(last)
                link(dve.tensor_tensor(c_, c_, e_, ALU.add))
                return c_

            for q in range(4):
                c_ = rank(grp[:, 4 * q:4 * q + 4, :], EG, q)
                link(dve.tensor_reduce(t8[:, 4 * q:4 * q + 4, :], c_, AX.X, ALU.add))
            link(dve.tensor_scalar(gsel[:], t8[:], TOP_GROUPS - 0.5, None, ALU.is_lt))
            link(dve.tensor_tensor(v, v, gsel[:].unsqueeze(3).broadcast_to((P, NT, EG, EPG)), ALU.mult))
            for q in range(4):
                c_ = rank(sc[:, 4 * q:4 * q + 4, :], E_, q)
                link(dve.tensor_reduce(pick[:, 4 * q:4 * q + 4, :], c_, AX.X, ALU.add))
            link(dve.tensor_scalar(pick[:], pick[:], TOP_K - 0.5, None, ALU.is_lt))
            link(dve.tensor_tensor(pick[:], pick[:], score[:], ALU.mult))
            link(dve.tensor_reduce(tot[:], pick[:], AX.X, ALU.add))
            link(dve.tensor_scalar(tot[:], tot[:], 1e-20, None, ALU.add))
            link(dve.reciprocal(tot[:], tot[:]))
            link(dve.tensor_scalar(tot[:], tot[:], ROUTE_SCALE, None, ALU.mult))
            dve.tensor_tensor(pick[:], pick[:], tot[:].unsqueeze(2).broadcast_to((P, NT, E_)),
                              ALU.mult).then_inc(weighted, 1)


def stage_experts(nc, d, xnT, sT, xT):
    NP = E_ // 2
    with Stage(nc, "moe") as st:
        w = st.sb("w", [P, 2, 3, P])
        cb = st.sb("cb", [P, 2, T])
        g, h = st.sb("g", [P, 2, CH]), st.sb("h", [P, 2, CH])
        y, t = st.sb("y", [P, T]), st.sb("t", [P, T])
        ps = st.ps("ps", [P, 4, CH])
        acc = st.ps("acc", [P, 4, CH])
        loaded = [st.sem("loaded0"), st.sem("loaded1")]
        cb_loaded = [st.sem("cb_loaded0"), st.sem("cb_loaded1")]
        ones_ready = st.sem("ones_ready")
        up_done, silu_done, h_ready, h_scaled, down_done = (st.sem("up_done"), st.sem("silu_done"),
                                                            st.sem("h_ready"), st.sem("h_scaled"),
                                                            st.sem("down_done"))
        out_silu, chain = st.sem("out_silu"), st.sem("chain")
        block = st.block()

        @block.sync
        def _(sp):
            def load(src, slot):
                sp.dma_start(w[:, slot, :, :], src).then_inc(loaded[slot], 16)

            def load_weights(i, slot):
                for e in range(2):
                    row = d["combineT"][bass.ds(2 * i + e, 1), :]
                    sp.dma_start(cb[e * EI:(e + 1) * EI, slot, :],
                                 row.broadcast_to((EI, T))).then_inc(cb_loaded[slot], 16)

            load(d["moe_w"][0], 0)
            load(d["moe_w"][1], 1)
            load_weights(0, 1)
            sp.wait_ge(down_done, 4 + 4)
            load(d["moe_w"][2], 0)
            load_weights(1, 0)
            with sp.Fori(0, NP // 2 - 1) as i:
                for s in range(2):
                    sp.wait_ge(down_done, 4 * (2 * i + 2 + s) + 4)
                    load(d["moe_w"][bass.ds(2 * i + 3 + s, 1)].rearrange("o p a b -> p (o a) b"), 1 - s)
                    load_weights(2 * i + 2 + s, 1 - s)

        @block.tensor
        def _(pe):
            def up(slot, c, k):
                pe.wait_ge(h_ready, k + 1)
                for j in range(2):
                    mm = pe.matmul(ps[:, 2 * (c % 2) + j, :], w[:, slot, j, :], xnT[:, c * CH:(c + 1) * CH],
                                   start=True, stop=True)
                mm.then_inc(up_done, 1)

            def down(slot, c, k, first=False):
                pe.wait_ge(h_scaled, k + 1)
                pe.matmul(acc[:, c, :], w[:, slot, 2, :], h[:, c % 2, :], start=first, stop=False,
                          skip_group_check=True).then_inc(down_done, 1)

            pe.wait_ge(loaded[0], 16)
            up(0, 0, 0)
            for c in range(1, 4):
                up(0, c, c)
                down(0, c - 1, c - 1, first=True)
            pe.wait_ge(loaded[1], 16)
            up(1, 0, 4)
            down(0, 3, 3, first=True)
            with pe.Fori(0, NP // 2 - 1) as i:
                for s in range(2):
                    slot = 1 - s
                    k = 4 * (2 * i + 1 + s)
                    for c in range(1, 4):
                        up(slot, c, k + c)
                        down(slot, c - 1, k + c - 1)
                    pe.wait_ge(loaded[1 - slot], 16 * (i + 2))
                    up(1 - slot, 0, k + 4)
                    down(slot, 3, k + 3)
            for s in range(2):
                slot = 1 - s
                k = 4 * (NP - 1 + s)
                for c in range(1, 4):
                    up(slot, c, k + c)
                    down(slot, c - 1, k + c - 1)
                if s == 0:
                    pe.wait_ge(loaded[0], 16 * (NP // 2 + 1))
                    up(0, 0, k + 4)
                down(slot, 3, k + 3)

        @block.scalar
        def _(act):
            def silu(c, k):
                act.wait_ge(up_done, k + 1)
                act.wait_ge(h_ready, k + 1)
                act.activation(g[:, c % 2, :], ps[:, 2 * (c % 2), :], ACT.Silu).then_inc(silu_done, 1)

            for c in range(4):
                silu(c, c)
            with act.Fori(0, NP) as i:
                for c in range(4):
                    silu(c, 4 * i + 4 + c)
            for c in range(4):
                act.wait_ge(down_done, 4 * (NP + 1) + 4)
                act.activation(y[:, c * CH:(c + 1) * CH], acc[:, c, :], ACT.Silu).then_inc(out_silu, 1)

        @block.vector
        def _(dve):
            link = Chain(dve, chain)

            def mult(c, k):
                dve.wait_ge(silu_done, k + 1)
                dve.wait_ge(down_done, k + 3)
                dve.tensor_tensor(h[:, c % 2, :], g[:, c % 2, :], ps[:, 2 * (c % 2) + 1, :],
                                  ALU.mult).then_inc(h_ready, 1)

            dve.sem_inc(h_ready, 2)
            dve.sem_inc(down_done, 4)
            for c in range(4):
                mult(c, c)
            with dve.Fori(0, NP) as i:
                for c in range(4):
                    mult(c, 4 * i + 4 + c)
            for c in range(NC):
                cols = slice(c * CH, (c + 1) * CH)
                dve.wait_ge(out_silu, c + 1)
                link(dve.tensor_tensor(t[:, cols], y[:, cols], sT[:, cols], ALU.mult))
                dve.tensor_tensor(xT[:, cols], xT[:, cols], t[:, cols], ALU.add)

        @block.gpsimd
        def _(pool):
            for c in range(4):
                pool.wait_ge(h_ready, c + 3)
                pool.sem_inc(h_scaled, 1)
            with pool.Fori(0, NP // 2) as i:
                for s in range(2):
                    slot = 1 - s
                    pool.wait_ge(cb_loaded[slot], 32 * (i + 1))
                    for c in range(4):
                        k = 4 * (2 * i + 1 + s) + c
                        pool.wait_ge(h_ready, k + 3)
                        pool.tensor_tensor(h[:, c % 2, :], h[:, c % 2, :], cb[:, slot, c * CH:(c + 1) * CH],
                                           ALU.mult).then_inc(h_scaled, 1)


NQ1, NK1 = 32, 8
QPK = NQ1 // NK1
QPART1 = (0, 0, 0, 1, 1, 2)
KPART1 = (0, 1, 2, 0, 1, 0)
LAMBDA_INIT = 0.8 - 0.6 * 2.718281828459045 ** (-0.3)


def stage_masks(nc, d, ident, identb, negmask):
    with Stage(nc, "masks") as st:
        m = st.sb("m", [P, 2, P])
        ones = st.sb("ones", [P, S], BF16)
        loaded, ready, stored = st.sem("loaded"), st.sem("ready"), st.sem("stored")
        block = st.block()

        @block.sync
        def _(sp):
            sp.dma_start(m[:], d["negmask"]).then_inc(loaded, 16)
            sp.wait_ge(ready, 1)
            sp.dma_start(d["ones1"], ones[0:1, :]).then_inc(stored, 16)
            sp.dma_start(d["k1"][B * NK1:].rearrange("h v e s -> (h v e) s"), ones[0:2 * 3 * HD, :]).then_inc(stored, 16)
            sp.dma_start(d["m1pad"], ones[0:2 * QPK, :]).then_inc(stored, 16)
            for h in range(2):
                sp.dma_start(d["q1"][B * NQ1 + h * QPK:B * NQ1 + (h + 1) * QPK].rearrange("h v e s -> (h v e) s"),
                             ones[0:QPK * 3 * HD, :]).then_inc(stored, 16)
            sp.wait_ge(stored, 80)

        @block.vector
        def _(dve):
            dve.memset(ones[:], 1.0).then_inc(ready, 1)
            dve.tensor_copy(identb[:], ident[:])
            dve.wait_ge(loaded, 16)
            dve.tensor_copy(negmask[:], m[:])


def stage_project1(nc, d, xnT, vaug):
    with Stage(nc, "proj1") as st:
        w = st.sb("w", [P, 2 * D + 2 * NK1 * HD])
        parts = st.sb("parts", [P, 3, 3, T], BF16)
        r0, r1, r2 = st.sb("r0", [P, 3, T]), st.sb("r1", [P, T]), st.sb("r2", [P, T])
        vtok = st.sb("vtok", [P, NT, NK1 * HD])
        ps = st.ps("ps", [P, 6, CH])
        pv = st.ps("pv", [P, 2, CH])
        loaded, mm_done, copied, chain = st.sem("loaded"), st.sem("mm_done"), st.sem("copied"), st.sem("chain")
        v_mm, split_done, stored, mm_used = st.sem("v_mm"), st.sem("split_done"), st.sem("stored"), st.sem("mm_used")
        v_ready, v_stored, v_loaded, ones_ready = (st.sem("v_ready"), st.sem("v_stored"), st.sem("v_loaded"),
                                                   st.sem("ones_ready"))
        block = st.block()
        NV = NK1 * HD

        @block.sync
        def _(sp):
            sp.dma_start(w[:], d["wqkv1"]).then_inc(loaded, 16)
            sp.wait_ge(v_ready, 2)
            sp.dma_start(d["v1"].rearrange("(n p) c -> p n c", p=P), vtok[:]).then_inc(v_stored, 16)
            sp.wait_ge(v_stored, 16)
            sp.wait_ge(ones_ready, 1)
            for c in range(8):
                sp.dma_start(vaug[16 * c:16 * c + 16, :, 0:HD],
                             d["v1"][:, c * HD:(c + 1) * HD].rearrange("(j t) e -> t j e", t=16)).then_inc(v_loaded, 16)
            sp.wait_ge(v_loaded, 16 * 8)
            sp.wait_ge(split_done, 3)
            n = 0
            for b in range(B):
                for kh in range(NK1):
                    for part in range(3):
                        for c in range(8):
                            src = parts[c * HD:(c + 1) * HD, 2, part, b * S + kh * P:b * S + (kh + 1) * P]
                            sp.dma_start(d["k1"][b * NK1 + kh, part].rearrange("e (j c t) -> c e j t", c=8, t=16)[c],
                                         src.rearrange("p (j t) -> p j t", t=16)).then_inc(stored, 16)
                            n += 1
            sp.wait_ge(stored, 16 * n)

        @block.gpsimd
        def _(pool):
            n = 0
            for ct in range(2):
                pool.wait_ge(split_done, ct + 1)
                for b in range(B):
                    for part in range(3):
                        for c in range(16):
                            src = parts[c * HD:(c + 1) * HD, ct, part, b * S:(b + 1) * S]
                            dst = d["q1"][b * NQ1:(b + 1) * NQ1, part, :, (16 * ct + c) * 32:(16 * ct + c + 1) * 32]
                            pool.dma_start(dst.rearrange("h e t -> e h t"),
                                           src.rearrange("p (h t) -> p h t", t=32)).then_inc(copied, 16)
                            n += 1
            pool.wait_ge(copied, 16 * n)

        @block.tensor
        def _(pe):
            pe.wait_ge(loaded, 16)
            for n in range(NT):
                mm = pe.matmul(pv[:, n // 8, (n % 8) * NV:(n % 8 + 1) * NV], xnT[:, n * P:(n + 1) * P],
                               w[:, 2 * D + NV:2 * D + 2 * NV], start=True, stop=True)
                if n % 8 == 7:
                    mm.then_inc(v_mm, 1)
            k = 0
            for j, (lo, hi) in enumerate(((0, D), (D, 2 * D), (2 * D, 2 * D + NV))):
                for c in range(NC):
                    if k >= 6:
                        pe.wait_ge(mm_used, k - 5)
                    pe.matmul(ps[0:hi - lo, k % 6, :], w[:, lo:hi], xnT[:, c * CH:(c + 1) * CH],
                              start=True, stop=True).then_inc(mm_done, 1)
                    k += 1

        @block.scalar
        def _(act):
            for c in range(2):
                act.wait_ge(v_mm, c + 1)
                act.copy(vtok[:, 8 * c:8 * c + 8, :].rearrange("p a b -> p (a b)"), pv[:, c, :]).then_inc(v_ready, 1)
            k = 0
            for j, rows in enumerate((P, P, NV)):
                for c in range(NC):
                    act.wait_ge(mm_done, k + 1)
                    act.copy(r0[0:rows, j, c * CH:(c + 1) * CH], ps[0:rows, k % 6, :]).then_inc(mm_used, 1)
                    k += 1

        @block.vector
        def _(dve):
            link = Chain(dve, chain)
            dve.memset(vaug[:], 1.0).then_inc(ones_ready, 1)
            for j, rows in enumerate((P, P, NV)):
                dve.wait_ge(mm_used, NC * (j + 1))
                split_parts(link, dve, r0[0:rows, j, :], parts[0:rows, j, 0, :], parts[0:rows, j, 1, :],
                            parts[0:rows, j, 2, :], r1[0:rows, :], r2[0:rows, :])
                dve.sem_inc(split_done, 1)


NLOADS = 3 + 4 * QPK


def load_packed(eng, dst, src, parts, signal):
    blk = n = 0
    while blk < NPACK:
        end = blk + 1
        while end < NPACK and parts[end] == parts[end - 1] + 1:
            end += 1
        rows = dst[blk * HD:end * HD]
        eng.dma_start(rows, src[..., parts[blk]:parts[blk] + end - blk, :, :]).then_inc(signal, 16)
        blk, n = end, n + 1
    return n


def stage_max1(nc, d, ident, identb, negmask):
    NKH, NH = B * NK1, B * NQ1
    with Stage(nc, "max1") as st:
        qh = st.sb("qh", [P, 2, QPK, S], BF16)
        qt = st.sb("qt", [P, 2, QPK, ST, P], BF16)
        kh = st.sb("kh", [P, 2, S], BF16)
        mcol = st.sb("mcol", [P, ST, NH])
        mrow = st.sb("mrow", [NH, S], BF16)
        ps = st.ps("ps", [P, 4, 2 * CH])
        loaded = [st.sem("loaded0"), st.sem("loaded1")]
        zeroed, scored, maxed = st.sem("zeroed"), st.sem("scored"), st.sem("maxed")
        head_used, rows, rows_out, stored = st.sem("head_used"), st.sem("rows"), st.sem("rows_out"), st.sem("stored")
        q_turned = st.sem("q_turned")
        turning = st.sem("turning")
        block = st.block()

        @block.sync
        def _(sp):
            def load(kv, slot):
                n = load_packed(sp, kh[:, slot, :], d["k1"][kv], KPART1, loaded[slot])
                for h in range(QPK):
                    n += load_packed(sp, qh[:, slot, h, :], d["q1"][kv * QPK + h], QPART1, loaded[slot])
                assert n == NLOADS, n

            sp.wait_ge(zeroed, 1)
            load(0, 0)
            load(1, 1)
            with sp.Fori(0, NKH // 2 - 1) as i:
                for s in range(2):
                    sp.wait_ge(head_used, 2 * i + s + 3)
                    load(2 * i + 2 + s, s)
            sp.wait_ge(rows_out, ST)
            sp.dma_start(d["m1"], mrow[:]).then_inc(stored, 16)
            sp.wait_ge(stored, 16)

        @block.gpsimd
        def _(pool):
            pool.memset(qh[:], 0.0)
            pool.memset(kh[:], 0.0).then_inc(zeroed, 1)
            pool.sem_inc(head_used, 2)
            with pool.Fori(0, NKH // 2) as i:
                for s in range(2):
                    pool.wait_ge(loaded[s], 16 * NLOADS * (i + 1))
                    pool.wait_ge(head_used, 2 * i + s + 1)
                    pool.sem_inc(turning, 1)
                    for h in range(QPK):
                        pool.tensor_copy(qt[:, s, h, :, :].rearrange("p u (c t) -> p u c t", t=4),
                                         qh[:, s, h, :].rearrange("p (c u t) -> p u c t", c=32, t=4)
                                         ).then_inc(q_turned, 1)

        @block.tensor
        def _(pe):
            with pe.Fori(0, NKH // 2) as i:
                for s in range(2):
                    for h in range(QPK):
                        pe.wait_ge(q_turned, (2 * i + s) * QPK + h + 1)
                        for u in range(ST):
                            pe.wait_ge(maxed, ((2 * i + s) * QPK + h) * ST + u + 1)
                            queries = qt[:, s, h, u, :]
                            for lo in range(0, (u + 1) * P, CH):
                                hi = min(lo + CH, (u + 1) * P)
                                last = hi == (u + 1) * P
                                pe.matmul(ps[:, u % 4, lo:hi], queries, kh[:, s, lo:hi], start=True, stop=not last)
                            pe.matmul(ps[:, u % 4, u * P:(u + 1) * P], identb[:], negmask[:, 1, :], start=False,
                                      stop=True).then_inc(scored, 1)
            pe.wait_ge(maxed, NH * ST + 4)
            for u in range(ST):
                pe.transpose(ps[0:NH, u // 4, (u % 4) * P:(u % 4 + 1) * P], mcol[:, u, :], ident[:]).then_inc(rows, 1)

        @block.scalar
        def _(act):
            for u in range(ST):
                act.wait_ge(rows, ST)
                act.mul(mrow[:].rearrange("p (c t) -> p c t", t=32)[:, :, 4 * u:4 * u + 4],
                        ps[0:NH, u // 4, (u % 4) * P:(u % 4 + 1) * P].rearrange("p (c t) -> p c t", t=4),
                        -1.0).then_inc(rows_out, 1)

        @block.vector
        def _(dve):
            dve.sem_inc(maxed, 4)
            with dve.Fori(0, NKH // 2) as i:
                for s in range(2):
                    for h in range(QPK):
                        for u in range(ST):
                            dve.wait_ge(scored, ((2 * i + s) * QPK + h) * ST + u + 1)
                            dve.tensor_reduce(mcol[:, u, bass.ds((2 * i + s) * QPK + h, 1)],
                                              ps[:, u % 4, 0:(u + 1) * P], AX.X, ALU.max).then_inc(maxed, 1)
                    dve.sem_inc(head_used, 1)


def stage_attend1(nc, d, vaug, identb, negmask):
    NKH, NH = B * NK1, B * NQ1
    with Stage(nc, "att1") as st:
        qh = st.sb("qh", [P, 2, QPK, S], BF16)
        kh = st.sb("kh", [P, 2, S], BF16)
        pr = st.sb("pr", [P, 4, 2, CH])
        vh = st.sb("vh", [P, 2, ST, VW])
        ob = st.sb("ob", [P, 2, CH])
        ps = st.ps("ps", [P, 8, CH])
        loaded = [st.sem("loaded0"), st.sem("loaded1")]
        stored = [st.sem("stored0"), st.sem("stored1")]
        zeroed, qk_done, exp_done, pv_done = st.sem("zeroed"), st.sem("qk_done"), st.sem("exp_done"), st.sem("pv_done")
        out_copied, v_copied, chain = st.sem("out_copied"), st.sem("v_copied"), st.sem("chain")
        block = st.block()

        @block.sync
        def _(sp):
            def load(kv, slot):
                n = load_packed(sp, kh[:, slot, :], d["k1"][kv], KPART1, loaded[slot])
                sp.dma_start(kh[KROWS:KROWS + 1, slot, :], d["ones1"]).then_inc(loaded[slot], 16)
                for h in range(QPK):
                    n += load_packed(sp, qh[:, slot, h, :], d["q1"][kv * QPK + h], QPART1, loaded[slot])
                    sp.dma_start(qh[KROWS:KROWS + 1, slot, h, :],
                                 d["m1all"][bass.ds(kv * QPK + h, 1), :]).then_inc(loaded[slot], 16)
                return n + 1 + QPK

            def store(row, slot):
                for quad in range(4):
                    sp.dma_start(d["o1"][row, quad // 2, :, (quad % 2) * CH:(quad % 2 + 1) * CH],
                                 ob[32 * quad:32 * quad + HD + 1, slot, :]).then_inc(stored[slot], 16)

            sp.wait_ge(zeroed, 1)
            load(0, 0)
            load(1, 1)
            with sp.Fori(0, NKH // 2) as i:
                for s in range(2):
                    for h in range(QPK):
                        bh = (2 * i + s) * QPK + h
                        sp.wait_ge(out_copied, bh + 3)
                        store(bh, 1 - h % 2)
                    sp.wait_ge(qk_done, (2 * i + s + 1) * QPK * ST + 1)
                    load(2 * i + 2 + s, s)
            sp.wait_ge(out_copied, NH + 3)
            store(NH, 1)
            for s in range(2):
                sp.wait_ge(stored[s], 16 + 64 * (NH // 2 + s))
                sp.wait_ge(loaded[s], 16 * (NLOADS + 1 + QPK) * (NKH // 2 + 1))

        @block.gpsimd
        def _(pool):
            pool.memset(qh[:], 0.0)
            pool.memset(kh[:], 0.0)
            pool.memset(pr[:], 0.0)
            pool.memset(vh[:], 0.0).then_inc(zeroed, 1)
            pool.wait_ge(zeroed, 1)
            with pool.Fori(0, NKH // 2) as i:
                for s in range(2):
                    kv = 2 * i + s
                    pool.wait_ge(pv_done, kv * QPK * (ST // 2) + 1)
                    pool.tensor_copy(vh[:, s, :, 0:HD + 1], vaug[:, bass.ds(kv * ST, ST), :]).then_inc(v_copied, 1)

        @block.tensor
        def _(pe):
            def from_tile(ap, J):
                return ap.rearrange("p (c t) -> p c t", t=32)[:, :, 4 * J:32]

            def qk(slot, h, J, n):
                pe.wait_ge(exp_done, n + 1)
                for c in range(2):
                    bank = ps[:, 2 * (J % 2) + c, :]
                    pe.matmul(from_tile(bank, J), kh[:, slot, J * P:(J + 1) * P],
                              from_tile(qh[:, slot, h, c * CH:(c + 1) * CH], J), start=True, stop=False)
                    mm = pe.matmul(bank.rearrange("p (c t) -> p c t", t=32)[:, :, 4 * J:4 * J + 4], identb[:],
                                   negmask[:, 0, c * 64:(c + 1) * 64], start=False, stop=True)
                mm.then_inc(qk_done, 1)

            def pv(slot, acc, m, n):
                pe.wait_ge(exp_done, n + 3)
                for J in (2 * m, 2 * m + 1):
                    for c in range(2):
                        quad = 32 * (2 * (J % 2) + c)
                        first = 0 if J < 2 else J
                        mm = pe.matmul(from_tile(ps[quad:quad + VW, 6 + acc, :], first), vh[:, slot, J, :],
                                       from_tile(pr[:, J % 4, c, :], first), start=(m == 0),
                                       stop=(m == ST // 2 - 1), skip_group_check=True, tile_position=(0, quad))
                mm.then_inc(pv_done, 1)

            pe.sem_inc(qk_done, 1)
            pe.wait_ge(zeroed, 1)
            pe.wait_ge(out_copied, 2)
            with pe.Fori(0, NKH // 2) as i:
                for s in range(2):
                    pe.wait_ge(loaded[s], 16 * (NLOADS + 1 + QPK) * (i + 1))
                    for h in range(QPK):
                        bh = (2 * i + s) * QPK + h
                        for m in range(ST // 2):
                            n = bh * ST + 2 * m
                            qk(s, h, 2 * m, n)
                            qk(s, h, 2 * m + 1, n + 1)
                            if m == 0:
                                pv(s if h else 1 - s, 1 - h % 2, ST // 2 - 1, n - 1)
                                if h == 0:
                                    pe.wait_ge(v_copied, 2 * i + s + 1)
                                pe.wait_ge(out_copied, bh + 2)
                            else:
                                pv(s, h % 2, m - 1, n - 1)
            pv(1, 1, ST // 2 - 1, NH * ST - 1)

        @block.scalar
        def _(act):
            act.sem_inc(exp_done, 2)
            act.wait_ge(zeroed, 1)
            with act.Fori(0, NH // 2) as i:
                for s in range(2):
                    bh = 2 * i + s
                    for J in range(ST):
                        act.wait_ge(qk_done, bh * ST + J + 2)
                        act.wait_ge(pv_done, bh * (ST // 2) + J // 2 + 4)
                        act.activation(
                            pr[:, J % 4, :, :].rearrange("p b (c t) -> p (b c) t", t=32)[:, :, 4 * J:32],
                            ps[:, 2 * (J % 2):2 * (J % 2) + 2, :].rearrange("p b (c t) -> p (b c) t",
                                                                            t=32)[:, :, 4 * J:32],
                            ACT.Exp, scale=SCALE).then_inc(exp_done, 1)

        @block.vector
        def _(dve):
            link = Chain(dve, chain)
            dve.sem_inc(pv_done, 4)
            dve.sem_inc(stored[0], 16)
            dve.sem_inc(stored[1], 16)
            link(dve.memset(ps[:, 6:8, :], 0.0))
            dve.sem_inc(out_copied, 2)

            def copy_out(slot, bh_done, rounds):
                dve.wait_ge(pv_done, bh_done * (ST // 2) + 5)
                dve.wait_ge(stored[slot], rounds)
                dve.tensor_copy(ob[:, slot, :], ps[:, 6 + slot, :]).then_inc(out_copied, 1)

            with dve.Fori(0, NH // 2) as i:
                for s in range(2):
                    copy_out(1 - s, 2 * i + s, 16 + 64 * i)
            copy_out(1, NH, 16 + 64 * (NH // 2))


def stage_combine1(nc, d, sT):
    with Stage(nc, "comb1") as st:
        num = [st.sb(f"num{j}", [P, 2, T]) for j in range(2)]
        den = [st.sb(f"den{j}", [P, 2, T]) for j in range(2)]
        wp = st.sb("wp", [P, D])
        lam, lsum = st.sb("lam", [P, 4, NK1 * HD]), st.sb("lsum", [P, 4])
        newT = st.sb("newT", [P, B, D, ST])
        ps = st.ps("ps", [P, 4, CH])
        ps2 = st.ps("ps2", [P, 4, CH])
        weights, chain, mixed, y_done, y_copied = (st.sem("weights"), st.sem("chain"), st.sem("mixed"),
                                                   st.sem("y_done"), st.sem("y_copied"))
        sums = [st.sem("sums0"), st.sem("sums1")]
        lam_sum, lam_exp, projected = st.sem("lam_sum"), st.sem("lam_exp"), st.sem("projected")
        block = st.block()

        @block.sync
        def _(sp):
            sp.dma_start(wp[:], d["wproj"]).then_inc(weights, 16)
            for j in range(4):
                sp.dma_start(lam[:, j, :], d["lam"][j].partition_broadcast(P)).then_inc(weights, 16)
            for j in range(2):
                for quad in range(2):
                    for b in range(B):
                        rows = d["o1"][1 + b * NQ1:1 + (b + 1) * NQ1].rearrange("(n j) v r s -> j v n r s", j=2)[j, quad]
                        sp.dma_start(num[j][:, quad, b * S:(b + 1) * S], rows[:, 0:HD, :]).then_inc(sums[j], 16)
                        sp.dma_start(den[j][:, quad, b * S:(b + 1) * S],
                                     rows[:, HD:HD + 1, :].broadcast_to((NQ1 // 2, HD, S))).then_inc(sums[j], 16)

        @block.scalar
        def _(act):
            act.wait_ge(lam_sum, 1)
            act.activation(lsum[:, 0:2], lsum[:, 0:2], ACT.Exp).then_inc(lam_exp, 1)
            for c in range(NC):
                act.wait_ge(projected, c + 1)
                act.copy(sT[:, c * CH:(c + 1) * CH], ps2[:, c, :])

        @block.tensor
        def _(pe):
            pe.wait_ge(weights, 16 * 5)
            pe.wait_ge(mixed, 1)
            for b in range(B):
                for t in range(ST):
                    rows = num[1][:, 0, b * S + t * P:b * S + (t + 1) * P]
                    mm = pe.matmul(ps[:, 2 * b + t // 4, (t % 4) * P:(t % 4 + 1) * P], rows, wp[:],
                                   start=True, stop=True)
                    if t % 4 == 3:
                        mm.then_inc(y_done, 1)
            for c in range(NC):
                pe.wait_ge(y_copied, 2 * (c // 2) + 2)
                pe.matmul(ps2[:, c, :], wp[:],
                          newT[:, c // 2, :, :].rearrange("p c t -> p (c t)")[:, (c % 2) * CH:(c % 2 + 1) * CH],
                          start=True, stop=True).then_inc(projected, 1)

        @block.vector
        def _(dve):
            link = Chain(dve, chain)
            dve.wait_ge(weights, 16 * 5)
            for j in range(2):
                link(dve.tensor_tensor(lam[:, 2 * j, :], lam[:, 2 * j, :], lam[:, 2 * j + 1, :], ALU.mult))
                link(dve.tensor_reduce(lsum[:, j:j + 1], lam[:, 2 * j, :], AX.X, ALU.add))
            dve.sem_inc(lam_sum, 1)
            dve.wait_ge(lam_exp, 1)
            link(dve.tensor_tensor(lsum[:, 2:3], lsum[:, 1:2], lsum[:, 0:1], ALU.subtract))
            link(dve.tensor_scalar(lsum[:, 3:4], lsum[:, 2:3], -LAMBDA_INIT, None, ALU.add))
            for j in range(2):
                dve.wait_ge(sums[j], 16 * 8)
                for x in (num[j], den[j]):
                    link(dve.tensor_tensor(x[:, 0, :], x[:, 0, :], x[:, 1, :], ALU.add))
                link(dve.reciprocal(den[j][:, 0, :], den[j][:, 0, :]))
                link(dve.tensor_tensor(num[j][:, 0, :], num[j][:, 0, :], den[j][:, 0, :], ALU.mult))
            link(dve.scalar_tensor_tensor(num[0][:, 0, :], num[1][:, 0, :], lsum[:, 3:4], num[0][:, 0, :],
                                          ALU.mult, ALU.add))
            dve.tensor_scalar(num[1][:, 0, :].rearrange("p (b t c) -> p b c t", b=B, c=32),
                              num[0][:, 0, :].rearrange("p (b c t) -> p b c t", b=B, c=32), 1.0 - LAMBDA_INIT,
                              None, ALU.mult).then_inc(mixed, 1)
            for k in range(4):
                dve.wait_ge(y_done, k + 1)
                b, t0 = k // 2, 4 * (k % 2)
                dve.tensor_copy(newT[:, b, :, t0:t0 + 4], ps[:, k, :].rearrange("p (t c) -> p c t", c=P)
                                ).then_inc(y_copied, 1)


DEPTH = 6
NHP = 8
DH = 64
WIN = 32
QW = P + WIN
GI = 341
GT = (P, P, GI - 2 * P)
QK_SCALE = 8.0
NU = 2 * NHP
C_Q, C_QR, C_K, C_KR, C_G, C_B, C_B2, C_A, C_GATE, NCOL = 0, 1, 2, 3, 4, 5, 6, 7, 10, 13


def stage_transformer(nc, d, ident, identb, yT):
    with Stage(nc, "tr") as st:
        xs = st.sb("xs", [P, B, S])
        w5 = st.sb("w5", [P, 2, 5, P])
        wo = st.sb("wo", [P, NHP, P])
        w1 = st.sb("w1", [P, 2 * GI])
        w2 = st.sb("w2", [P, 3, P])
        col = st.sb("col", [P, NCOL])
        rope = st.sb("rope", [P, 4, S])
        blk = st.sb("blk", [P, P])
        mean = st.sb("mean", [P, P])
        ones = st.sb("ones", [P, DH])
        eps = st.sb("eps", [P, 1])
        band = st.sb("band", [P, 3, QW], BF16)
        sq = st.sb("sq", [P, 4, CH])
        t12 = st.sb("t12", [P, 4, 2, CH])
        rn = st.sb("rn", [P, 4, CH])
        qn = st.sb("qn", [P, 2, S])
        kz = st.sb("kz", [P, 2, 2, S])
        v = st.sb("v", [P, 2, ST, P])
        pr = st.sb("pr", [P, 2, 2, ST * QW + QW])
        rden = st.sb("rden", [P, 2, CH])
        o = st.sb("o", [P, NHP, T])
        ps = st.ps("ps", [P, 8, CH])
        S_ = st.sem
        loaded_const, const_ready, chain = S_("loaded_const"), S_("const_ready"), S_("chain")
        w_loaded = [S_("w_loaded0"), S_("w_loaded1")]
        layer_loaded, attn_w_used, xs_ready, pchain = S_("layer_loaded"), S_("attn_w_used"), S_("xs_ready"), S_("pchain")
        proj_done, sq_done, rope_done, v_copied = S_("proj_done"), S_("sq_done"), S_("rope_done"), S_("v_copied")
        ss_done, norm_done, recip_done, qk_ready = S_("ss_done"), S_("norm_done"), S_("recip_done"), S_("qk_ready")
        scores_done, exp_done, pv_done, out_done = S_("scores_done"), S_("exp_done"), S_("pv_done"), S_("out_done")
        wo_done, x_added, xs2_ready = S_("wo_done"), S_("x_added"), S_("xs2_ready")
        mean_done, centered, square_done, var_done = S_("mean_done"), S_("centered"), S_("square_done"), S_("var_done")
        std_done, normed, up_done, gelu_done, h_ready = (S_("std_done"), S_("normed"), S_("up_done"),
                                                         S_("gelu_done"), S_("h_ready"))
        pool_chain, fchain = S_("pool_chain"), S_("fchain")
        down_done, layer_done, marks = S_("down_done"), S_("layer_done"), S_("marks")
        block = st.block()
        LAYER_LOADS = 4

        @block.sync
        def _(sp):
            sp.dma_start(rope[:], d["rope"]).then_inc(loaded_const, 16)
            sp.dma_start(blk[:], d["blk64"]).then_inc(loaded_const, 16)
            sp.dma_start(t12[:, 0, 0, 0:3 * QW], d["band"]).then_inc(loaded_const, 16)

            def load_w(hp, slot):
                sp.dma_start(w5[:, slot, :, :], d["w5"][bass.ds(hp, 1)].rearrange("o p a b -> p (o a) b")
                             ).then_inc(w_loaded[slot], 16)

            with sp.Fori(0, DEPTH) as L:
                sp.wait_ge(layer_done, NC * L + 1)
                sp.dma_start(col[:], d["col"][bass.ds(L, 1)].rearrange("o p a -> (o p) a")).then_inc(layer_loaded, 16)
                load_w(L * NHP, 0)
                load_w(L * NHP + 1, 1)
                sp.dma_start(wo[:], d["wo6"][bass.ds(L, 1)].rearrange("o p a b -> (o p) a b")
                             ).then_inc(layer_loaded, 16)
                sp.dma_start(w1[:], d["w1"][bass.ds(L, 1)].rearrange("o p a -> (o p) a")).then_inc(layer_loaded, 16)
                sp.dma_start(w2[:], d["w2"][bass.ds(L, 1)].rearrange("o p a b -> (o p) a b")
                             ).then_inc(layer_loaded, 16)
                with sp.Fori(0, NHP // 2 - 1) as i:
                    for s in range(2):
                        sp.wait_ge(proj_done, 10 * (L * NU + 4 * i + 2 * s + 2) + 1)
                        load_w(L * NHP + 2 * i + 2 + s, s)

        @block.tensor
        def _(pe):
            def project(n, slot, b, c):
                cols = xs[:, b, c * CH:(c + 1) * CH]
                frees = (((norm_done, 4 * n + 3), (norm_done, 4 * n + 4), None, None, (rope_done, 8 * n + 1)),
                         ((rope_done, 8 * n + 2), (rope_done, 8 * n + 3), (rope_done, 8 * n + 4),
                          (v_copied, 2 * n + 1), (rope_done, 8 * n + 5)))[c]
                for j in range(4):
                    if frees[j] is not None:
                        pe.wait_ge(*frees[j])
                    pe.matmul(ps[:, (5 * c + j) % 4, :], w5[:, slot, j, :], cols, start=True,
                              stop=True).then_inc(proj_done, 1)
                pe.wait_ge(*frees[4])
                for t in range(4):
                    mm = pe.matmul(ps[:, (5 * c + 4) % 4, t * P:(t + 1) * P],
                                   xs[:, b, c * CH + t * P:c * CH + (t + 1) * P], w5[:, slot, 4, :],
                                   start=True, stop=True)
                mm.then_inc(proj_done, 1)

            def norms(n):
                frees = ((rope_done, 8 * n + 6), (rope_done, 8 * n + 7), (rope_done, 8 * n + 8), (v_copied, 2 * n + 2))
                for j in range(4):
                    pe.wait_ge(*frees[j])
                    pe.wait_ge(sq_done, 4 * n + j + 1)
                    pe.matmul(ps[:, (10 + j) % 4, :], blk[:], sq[:, j, :], start=True, stop=True).then_inc(ss_done, 1)

            def scores(n, b, k):
                e, J0 = k % 2, 3 * (k // 2)
                pe.wait_ge(exp_done, 6 * n + k + 1)
                pe.matmul(ps[:, 4 + k % 2, 0:3 * QW], identb[:], band[:].rearrange("p a b -> p (a b)"), start=True,
                          stop=True)
                for J in range(J0, min(J0 + 3, ST)):
                    width = min(QW, S - J * P)
                    mm = pe.matmul(ps[:, 4 + k % 2, (J - J0) * QW:(J - J0) * QW + width],
                                   kz[:, b, e, J * P:(J + 1) * P], qn[:, b, J * P:J * P + width],
                                   start=False, stop=True, skip_group_check=True)
                mm.then_inc(scores_done, 1)

            def sums(n, b, c):
                pe.wait_ge(exp_done, 6 * n + (6, 8)[c])
                pe.wait_ge(out_done, 2 * n + c + 1)
                for I in range(4 * c, 4 * c + 4):
                    out = slice((I - 4 * c) * P, (I - 4 * c + 1) * P)
                    tail = slice((I - 4 * c) * P, (I - 4 * c) * P + WIN)
                    for what in range(2):
                        for e in range(2):
                            lhs = v[:, b, I, e * DH:(e + 1) * DH] if what == 0 else ones[:]
                            pe.matmul(ps[e * DH:(e + 1) * DH, 6 + what, out], lhs,
                                      pr[:, b, e, I * QW:I * QW + P], start=True, stop=True,
                                      tile_position=(0, e * DH), skip_group_check=True)
                    if I:
                        for what in range(2):
                            for e in range(2):
                                lhs = v[:, b, I - 1, e * DH:(e + 1) * DH] if what == 0 else ones[:]
                                mm = pe.matmul(ps[e * DH:(e + 1) * DH, 6 + what, tail], lhs,
                                               pr[:, b, e, (I - 1) * QW + P:I * QW], start=False, stop=True,
                                               tile_position=(0, e * DH), skip_group_check=True)
                mm.then_inc(pv_done, 1)

            def step(n, b, nxt):
                if nxt is not None:
                    project(n + 1, nxt[0], nxt[1], 0)
                pe.wait_ge(qk_ready, 4 * n + 6)
                scores(n, b, 0)
                scores(n, b, 1)
                if nxt is not None:
                    project(n + 1, nxt[0], nxt[1], 1)
                pe.wait_ge(qk_ready, 4 * n + 8)
                for k in range(2, 6):
                    scores(n, b, k)
                if nxt is not None:
                    norms(n + 1)
                pe.wait_ge(v_copied, 2 * n + 2)
                sums(n, b, 0)
                sums(n, b, 1)

            pe.wait_ge(const_ready, 2)
            pe.wait_ge(loaded_const, 48)
            with pe.Fori(0, DEPTH) as L:
                n0 = L * NU
                pe.wait_ge(xs_ready, L + 1)
                pe.wait_ge(w_loaded[0], 64 * L + 16)
                project(n0, 0, 0, 0)
                project(n0, 0, 0, 1)
                norms(n0)
                with pe.Fori(0, NHP // 2 - 1) as i:
                    n = n0 + 4 * i
                    step(n, 0, (0, 1))
                    pe.wait_ge(w_loaded[1], 64 * L + 16 * i + 16)
                    step(n + 1, 1, (1, 0))
                    step(n + 2, 0, (1, 1))
                    pe.wait_ge(w_loaded[0], 64 * L + 16 * i + 32)
                    step(n + 3, 1, (0, 0))
                n = n0 + NU - 4
                step(n, 0, (0, 1))
                pe.wait_ge(w_loaded[1], 64 * L + 64)
                step(n + 1, 1, (1, 0))
                step(n + 2, 0, (1, 1))
                step(n + 3, 1, None)
                pe.wait_ge(layer_loaded, 64 * L + 64)
                for c in range(NC):
                    pe.wait_ge(out_done, 2 * (n0 + NU) + 1)
                    pe.wait_ge(norm_done, 4 * (n0 + NU) + 4)
                    for hp in range(NHP):
                        mm = pe.matmul(ps[:, c, :], wo[:, hp, :], o[:, hp, c * CH:(c + 1) * CH],
                                       start=(hp == 0), stop=(hp == NHP - 1))
                    mm.then_inc(wo_done, 1)
                pe.wait_ge(xs2_ready, L + 1)
                for c in range(NC):
                    cols = xs[:, c // 2, (c % 2) * CH:(c % 2 + 1) * CH]
                    k = NC * L + c
                    pe.matmul(ps[:, 4, :], mean[:], cols, start=True, stop=True).then_inc(mean_done, 1)
                    pe.wait_ge(square_done, k + 1)
                    pe.matmul(ps[:, 4, :], mean[:], sq[:, c % 2, :], start=True, stop=True).then_inc(var_done, 1)
                    pe.wait_ge(normed, k + 1)
                    for t in range(3):
                        pe.wait_ge(h_ready, 3 * k + t + 1)
                        a_bank, g_bank = ((0, 1), (2, 3))[t % 2]
                        rows, lo = GT[t], t * P
                        pe.matmul(ps[0:rows, a_bank, :], w1[:, lo:lo + rows], rn[:, c % 2, :], start=True, stop=True)
                        pe.matmul(ps[0:rows, g_bank, :], w1[:, GI + lo:GI + lo + rows], rn[:, c % 2, :], start=True,
                                  stop=True).then_inc(up_done, 1)
                    for t in range(3):
                        pe.wait_ge(h_ready, 3 * k + t + 3)
                        rows = GT[t]
                        mm = pe.matmul(ps[:, 5, :], w2[0:rows, t, :], t12[0:rows, t, 0, :], start=(t == 0), stop=(t == 2))
                    mm.then_inc(down_done, 1)

        @block.scalar
        def _(act):
            def squares(n, c):
                for j, bank in enumerate(((0, 2), (1, 3))[c]):
                    idx = 2 * c + j
                    act.wait_ge(proj_done, 10 * n + 5 * c + 2 * j + 1)
                    act.wait_ge(ss_done, 4 * n + idx + 1)
                    act.activation(sq[:, idx, :], ps[:, bank, :], ACT.Square).then_inc(sq_done, 1)

            def copy_v(n, b, c):
                act.wait_ge(proj_done, 10 * n + 5 * c + 5)
                act.wait_ge(pv_done, 2 * n + 2)
                act.copy(v[:, b, 4 * c:4 * c + 4, :].rearrange("p a b -> p (a b)"), ps[:, c, :]).then_inc(v_copied, 1)

            def roots(n):
                for j in range(4):
                    act.wait_ge(ss_done, 4 * n + j + 5)
                    act.wait_ge(qk_ready, 4 * n + j + 1)
                    act.activation(rn[:, j, :], ps[:, (10 + j) % 4, :], ACT.Sqrt).then_inc(norm_done, 1)

            def exps(n, b, ks):
                for k in ks:
                    e, J0 = k % 2, 3 * (k // 2)
                    act.wait_ge(scores_done, 6 * n + k + 13)
                    act.wait_ge(pv_done, 2 * n + 2)
                    act.activation(pr[:, b, e, J0 * QW:(J0 + 3) * QW], ps[:, 4 + k % 2, 0:3 * QW], ACT.Exp,
                                   scale=QK_SCALE).then_inc(exp_done, 1)

            def step(n, b, nb):
                if nb is not None:
                    squares(n + 1, 0)
                    copy_v(n + 1, nb, 0)
                exps(n, b, (0, 1))
                if nb is not None:
                    squares(n + 1, 1)
                    copy_v(n + 1, nb, 1)
                exps(n, b, (2, 3, 4, 5))
                if nb is not None:
                    roots(n + 1)

            act.sem_inc(exp_done, 2)
            act.sem_inc(norm_done, 4)
            act.wait_ge(const_ready, 2)
            with act.Fori(0, DEPTH) as L:
                n0 = L * NU
                for c in range(2):
                    squares(n0, c)
                    copy_v(n0, 0, c)
                roots(n0)
                with act.Fori(0, NHP // 2 - 1) as i:
                    for u in range(4):
                        step(n0 + 4 * i + u, u % 2, 1 - u % 2)
                for u in range(4):
                    step(n0 + NU - 4 + u, u % 2, 1 - u % 2 if u < 3 else None)
                for c in range(NC):
                    k = NC * L + c
                    act.wait_ge(centered, k + 1)
                    act.activation(sq[:, c % 2, :], rn[:, 2 + c % 2, :], ACT.Square).then_inc(square_done, 1)
                    act.wait_ge(var_done, k + 1)
                    act.activation(rden[:, 0, :], ps[:, 4, :], ACT.Sqrt, bias=eps[:, 0:1]).then_inc(std_done, 1)
                    for t in range(3):
                        act.wait_ge(up_done, 3 * k + t + 1)
                        rows = GT[t]
                        act.activation(t12[0:rows, t, 1, :], ps[0:rows, ((0, 1), (2, 3))[t % 2][1], :], ACT.Gelu,
                                       bias=col[0:rows, C_GATE + t:C_GATE + t + 1]).then_inc(gelu_done, 1)

        @block.vector
        def _(dve):
            link = Chain(dve, chain)

            def rotate(n, b, c):
                for isk in range(2):
                    idx = 2 * c + isk
                    cols = slice(c * CH, (c + 1) * CH)
                    dve.wait_ge(qk_ready, 4 * n + idx + 1)
                    for x in range(2):
                        slot = 2 * isk + x
                        if x == 0:
                            dve.wait_ge(sq_done, 4 * n + idx + 1)
                        else:
                            dve.wait_ge(proj_done, 10 * n + 5 * c + slot + 1)
                        dve.scalar_tensor_tensor(t12[:, idx, x, :], ps[:, (5 * c + slot) % 4, :],
                                                 col[:, slot:slot + 1], rope[:, slot, cols], ALU.mult,
                                                 ALU.mult).then_inc(rope_done, 1)

            def reciprocals(n):
                for j in range(4):
                    dve.wait_ge(norm_done, 4 * n + j + 5)
                    dve.tensor_scalar(rn[:, j, :], rn[:, j, :], 1e-12, None, ALU.max).then_inc(marks, 1)
                    dve.wait_ge(marks, 4 * n + j + 1)
                    dve.reciprocal(rn[:, j, :], rn[:, j, :]).then_inc(recip_done, 1)

            def outputs(n, hp, b):
                for c in range(2):
                    dve.wait_ge(pv_done, 2 * n + c + 5)
                    dve.reciprocal(rden[:, c, :], ps[:, 7, :]).then_inc(pchain, 1)
                    dve.wait_ge(pchain, 2 * n + c + 1)
                    dve.tensor_tensor(o[:, hp, b * S + c * CH:b * S + (c + 1) * CH], ps[:, 6, :], rden[:, c, :],
                                      ALU.mult).then_inc(out_done, 1)

            def step(n, hp, b, nb):
                if nb is not None:
                    rotate(n + 1, nb, 0)
                    rotate(n + 1, nb, 1)
                    reciprocals(n + 1)
                outputs(n, hp, b)

            def shift(dst_ready):
                dve.tensor_copy(xs[0:64, :, :], yT[0:64, :].rearrange("p (b s) -> p b s", b=B))
                dve.tensor_copy(xs[64:P, :, 1:S],
                                yT[64:P, :].rearrange("p (b s) -> p b s", b=B)[:, :, 0:S - 1]).then_inc(dst_ready, 1)

            dve.sem_inc(qk_ready, 4)
            dve.sem_inc(ss_done, 4)
            dve.sem_inc(pv_done, 4)
            dve.sem_inc(scores_done, 12)
            dve.sem_inc(out_done, 1)
            dve.sem_inc(layer_done, 1)
            dve.sem_inc(h_ready, 2)
            dve.wait_ge(loaded_const, 48)
            link(dve.tensor_copy(band[:].rearrange("p a b -> p (a b)"), t12[:, 0, 0, 0:3 * QW]))
            dve.memset(xs[64:P, :, 0:1], 0.0)
            dve.memset(ones[:], 1.0)
            dve.memset(eps[:], LN_EPS)
            link(dve.memset(mean[:], 1.0 / D))
            dve.sem_inc(const_ready, 1)
            with dve.Fori(0, DEPTH) as L:
                n0 = L * NU
                dve.wait_ge(layer_done, NC * L + 1)
                dve.wait_ge(layer_loaded, 64 * L + 64)
                shift(xs_ready)
                rotate(n0, 0, 0)
                rotate(n0, 0, 1)
                reciprocals(n0)
                with dve.Fori(0, NHP // 2 - 1) as i:
                    for u in range(4):
                        step(n0 + 4 * i + u, bass.ds(2 * i + u // 2, 1), u % 2, 1 - u % 2)
                for u in range(4):
                    step(n0 + NU - 4 + u, NHP - 2 + u // 2, u % 2, 1 - u % 2 if u < 3 else None)
                for c in range(NC):
                    cols = slice(c * CH, (c + 1) * CH)
                    dve.wait_ge(wo_done, NC * L + c + 1)
                    dve.tensor_tensor(yT[:, cols], yT[:, cols], ps[:, c, :], ALU.add).then_inc(x_added, 1)
                dve.wait_ge(x_added, NC * (L + 1))
                shift(xs2_ready)
                for c in range(NC):
                    k = NC * L + c
                    cols = slice(c * CH, (c + 1) * CH)
                    dve.wait_ge(mean_done, k + 1)
                    if c == 0:
                        dve.wait_ge(xs2_ready, L + 1)
                    dve.tensor_tensor(rn[:, 2 + c % 2, :], xs[:, c // 2, (c % 2) * CH:(c % 2 + 1) * CH], ps[:, 4, :],
                                      ALU.subtract).then_inc(centered, 1)
                    dve.wait_ge(std_done, k + 1)
                    link2 = lambda ins, m: (ins.then_inc(fchain, 1), dve.wait_ge(fchain, 2 * k + m))
                    link2(dve.reciprocal(rden[:, 1, :], rden[:, 0, :]), 1)
                    link2(dve.tensor_tensor(rn[:, c % 2, :], rn[:, 2 + c % 2, :], rden[:, 1, :], ALU.mult), 2)
                    dve.tensor_scalar(rn[:, c % 2, :], rn[:, c % 2, :], col[:, C_G:C_G + 1], col[:, C_B:C_B + 1],
                                      ALU.mult, ALU.add).then_inc(normed, 1)
                    for t in range(3):
                        dve.wait_ge(gelu_done, 3 * k + t + 1)
                        rows = GT[t]
                        dve.scalar_tensor_tensor(t12[0:rows, t, 0, :], ps[0:rows, ((0, 1), (2, 3))[t % 2][0], :],
                                                 col[0:rows, C_A + t:C_A + t + 1], t12[0:rows, t, 1, :], ALU.add,
                                                 ALU.mult).then_inc(h_ready, 1)
                    dve.wait_ge(down_done, k + 1)
                    dve.scalar_tensor_tensor(yT[:, cols], ps[:, 5, :], col[:, C_B2:C_B2 + 1], yT[:, cols], ALU.add,
                                             ALU.add).then_inc(layer_done, 1)

        @block.gpsimd
        def _(pool):
            def combine(n, b):
                for j in range(4):
                    c, isk = j // 2, j % 2
                    cols = slice(c * CH, (c + 1) * CH)
                    pool.wait_ge(rope_done, 8 * n + 2 * j + 2)
                    step = 8 * n + 4 * c + (1 if isk else 0)
                    pool.tensor_tensor(t12[:, j, 0, :], t12[:, j, 0, :], t12[:, j, 1, :], ALU.add).then_inc(pool_chain, 1)
                    pool.wait_ge(pool_chain, step + 1)
                    pool.wait_ge(recip_done, 4 * n + j + 1)
                    pool.wait_ge(scores_done, 6 * n + 6)
                    if isk:
                        pool.tensor_tensor(kz[0:DH, b, 0, cols], t12[0:DH, j, 0, :], rn[0:DH, j, :],
                                           ALU.mult).then_inc(pool_chain, 1)
                        pool.wait_ge(pool_chain, step + 2)
                        pool.tensor_tensor(kz[DH:P, b, 1, cols], t12[DH:P, j, 0, :], rn[DH:P, j, :],
                                           ALU.mult).then_inc(pool_chain, 1)
                        pool.wait_ge(pool_chain, step + 3)
                        pool.sem_inc(qk_ready, 1)
                    else:
                        pool.tensor_tensor(qn[:, b, cols], t12[:, j, 0, :], rn[:, j, :], ALU.mult).then_inc(qk_ready, 1)

            pool.memset(kz[:], 0.0)
            pool.memset(qn[:], 0.0)
            pool.memset(pr[:], 0.0).then_inc(const_ready, 1)
            pool.wait_ge(const_ready, 2)
            with pool.Fori(0, DEPTH * NU // 2) as i:
                for b in range(2):
                    combine(2 * i + b, b)


def build(nc, d):
    with ExitStack() as ctx:
        def scope():
            stack = ExitStack()
            return stack, lambda n, s, t=F32: stack.enter_context(nc.sbuf_tensor(n, s, t))

        sb = lambda n, s, t=F32: ctx.enter_context(nc.sbuf_tensor(n, s, t))
        ident = sb("ident", [P, P])
        xnT = sb("xnT", [P, T])
        outer, so = scope()
        with outer:
            xT, sT = so("xT", [P, T]), so("sT", [P, T])
            stage_norm(nc, "norm0", ident, xT, xnT, x_dram=d["x"], ident_dram=d["ident"])
            inner, si = scope()
            with inner:
                qT = si("qT", [P, T])
                relmax = si("relmax", [P, 2])
                vaug = si("vaug", [P, B * H0, ST, HD + 1])
                stage_project0(nc, d, xnT, qT, vaug, relmax)
                stage_max0(nc, d, ident, qT, relmax)
                stage_attend0(nc, d, vaug)
                stage_combine0(nc, d, qT, sT)
            stage_route(nc, d, xnT)
            stage_experts(nc, d, xnT, sT, xT)
            stage_norm(nc, "norm1", ident, xT, xnT)
            inner, si = scope()
            with inner:
                vaug1 = si("vaug1", [P, B * NK1 * ST, HD + 1])
                identb, negmask = si("identb", [P, P], BF16), si("negmask", [P, 2, P], BF16)
                stage_masks(nc, d, ident, identb, negmask)
                stage_project1(nc, d, xnT, vaug1)
                stage_max1(nc, d, ident, identb, negmask)
                stage_attend1(nc, d, vaug1, identb, negmask)
            stage_combine1(nc, d, sT)
            stage_stash(nc, d, xT, sT)
        inner, si = scope()
        with inner:
            identb = si("identb2", [P, P], BF16)
            stage_ident(nc, ident, identb)
            stage_transformer(nc, d, ident, identb, xnT)
        stage_final(nc, d, ident, xnT)


def stage_ident(nc, ident, identb):
    with Stage(nc, "ident") as st:
        block = st.block()

        @block.vector
        def _(dve):
            dve.tensor_copy(identb[:], ident[:])


def stage_stash(nc, d, xT, sT):
    with Stage(nc, "stash") as st:
        stored = st.sem("stored")
        block = st.block()

        @block.sync
        def _(sp):
            sp.dma_start(d["xs_stash"][0], xT[:]).then_inc(stored, 16)
            sp.dma_start(d["xs_stash"][1], sT[:]).then_inc(stored, 16)
            sp.wait_ge(stored, 32)


def stage_final(nc, d, ident, yT):
    with Stage(nc, "final") as st:
        xT, sT = st.sb("xT", [P, T]), st.sb("sT", [P, T])
        back = st.sem("back")
        g = st.sb("g", [P, T])
        x = st.sb("x", [P, NT, D])
        ps = st.ps("ps", [P, 4, CH])
        silu_done, chain, ready, turned, copied, stored = (st.sem("silu_done"), st.sem("chain"), st.sem("ready"),
                                                           st.sem("turned"), st.sem("copied"), st.sem("stored"))
        block = st.block()

        @block.scalar
        def _(act):
            for c in range(NC):
                cols = slice(c * CH, (c + 1) * CH)
                act.activation(g[:, cols], yT[:, cols], ACT.Silu).then_inc(silu_done, 1)
            for c in range(NC):
                act.wait_ge(turned, c + 1)
                act.copy(x[:, 4 * c:4 * c + 4, :].rearrange("p a b -> p (a b)"), ps[:, c, :]).then_inc(copied, 1)

        @block.vector
        def _(dve):
            link = Chain(dve, chain)
            dve.wait_ge(back, 32)
            for c in range(NC):
                cols = slice(c * CH, (c + 1) * CH)
                dve.wait_ge(silu_done, c + 1)
                link(dve.tensor_tensor(g[:, cols], g[:, cols], sT[:, cols], ALU.mult))
                dve.tensor_tensor(g[:, cols], g[:, cols], xT[:, cols], ALU.add).then_inc(ready, 1)

        @block.tensor
        def _(pe):
            for n in range(NT):
                if n % 4 == 0:
                    pe.wait_ge(ready, n // 4 + 1)
                mm = pe.transpose(ps[:, n // 4, (n % 4) * P:(n % 4 + 1) * P], g[:, n * P:(n + 1) * P], ident[:])
                if n % 4 == 3:
                    mm.then_inc(turned, 1)

        @block.sync
        def _(sp):
            sp.dma_start(xT[:], d["xs_stash"][0]).then_inc(back, 16)
            sp.dma_start(sT[:], d["xs_stash"][1]).then_inc(back, 16)
            out = d["out"].rearrange("(n p) d -> p n d", p=P)
            for c in range(NC):
                sp.wait_ge(copied, c + 1)
                sp.dma_start(out[:, 4 * c:4 * c + 4, :], x[:, 4 * c:4 * c + 4, :]).then_inc(stored, 16)
            sp.wait_ge(stored, 16 * NC)


def host_arrays(inputs):
    import numpy as np
    g = {k: np.asarray(v) for k, v in inputs.items()}
    c = np.ascontiguousarray
    a = {}
    a["x"] = g["L0_attn_hidden_states"].reshape(T, D)
    for n in "qkvo":
        a[f"w{n}T"] = c(g[f"L0_attn_W{n}"].T)
    for n in "qko":
        a[f"b{n}"] = g[f"L0_attn_b{n}"].reshape(D, 1)
    a["bv"] = g["L0_attn_bv"].reshape(D)
    rel = g["L0_attn_rel_emb"]
    a["rel_rows"] = c(np.tile(rel.T, (H0, 1)))
    reversed_index = np.clip(255 - np.arange(CH), -128, 128) + 128
    a["rel_reversed"] = c(rel[reversed_index].T)
    a["mrep"] = c(np.tile(g["L0_attn_M"].reshape(P, HD), (1, H0)))
    a["z"] = g["L0_attn_z"].reshape(P, 1)
    a["alpha"] = g["L0_attn_gate_alpha"].reshape(1)
    a["headblk"] = np.kron(np.eye(H0, dtype=np.float32), np.ones((HD, HD), np.float32))
    a["gate_wT"] = c(g["L0_ffn_gate_w"].T)
    a["gate_bias"] = g["L0_ffn_gate_bias"].reshape(E_)
    a["lower"] = np.tril(np.ones((E_, E_), np.float32), -1).reshape(-1)
    moe = np.zeros((E_ // 2 + 1, P, 3, P), np.float32)
    moe[0, :, 0], moe[0, :, 1], moe[0, :, 2] = g["L0_ffn_sh_gate"].T, g["L0_ffn_sh_up"].T, g["L0_ffn_sh_down"].T
    for i, n in enumerate(("w_gate", "w_up")):
        moe[1:, :, i] = g[f"L0_ffn_{n}"].reshape(E_ // 2, 2 * EI, D).transpose(0, 2, 1)
    moe[1:, :, 2] = g["L0_ffn_w_down"].transpose(0, 2, 1).reshape(E_ // 2, 2 * EI, D)
    a["moe_w"] = moe
    a["wqkv1"], a["wproj"] = g["L1_attn_Wqkv"], g["L1_attn_Wproj"]
    a["lam"] = np.stack([g[f"L1_attn_lambda_{n}"] for n in ("q1", "k1", "q2", "k2")])
    jpos = (8 * np.arange(16)[None, :] + np.arange(8)[:, None]).reshape(-1)
    ipos = (32 * np.arange(4)[None, :] + np.arange(32)[:, None]).reshape(-1)
    hidden = np.where(jpos[:, None] > ipos[None, :], np.float32(-1e30), np.float32(0))
    a["negmask"] = np.stack([hidden, hidden.T], axis=1)
    half = np.arange(0, DH, 2, dtype=np.float32)
    pos = np.arange(S, dtype=np.float32)
    freqs = pos[:, None] * (np.float32(1.0) / np.float32(10000.0) ** (half / np.float32(DH)))[None, :]
    freqs = np.concatenate([freqs, freqs], -1)
    base = (half + np.float32(0.4 * DH)) / np.float32(1.4 * DH)
    scale = base[None, :] ** ((pos - S // 2) / np.float32(WIN // 2))[:, None]
    scale = np.concatenate([scale, scale], -1)
    sign = np.where(np.arange(DH) < DH // 2, np.float32(-1), np.float32(1))
    cos, sin = np.cos(freqs), np.sin(freqs) * sign
    tables = np.stack([cos * scale, sin * scale, cos * (1 / scale), sin * (1 / scale)]).astype(np.float32)
    a["rope"] = c(np.tile(tables.transpose(2, 0, 1), (2, 1, 1)))
    a["blk64"] = np.kron(np.eye(2, dtype=np.float32), np.ones((DH, DH), np.float32))
    behind = np.arange(QW)[None, :] - np.arange(P)[:, None]
    a["band"] = c(np.tile(np.where((behind >= 0) & (behind <= WIN), np.float32(0), np.float32(-1e30)), (1, 3)))
    exchange = np.concatenate([np.arange(DH // 2, DH), np.arange(DH // 2)])
    exchange2 = np.concatenate([exchange, exchange + DH])
    wqkv = g["L1_ffn_Wqkv"].reshape(DEPTH, P, 3, NHP, P).transpose(0, 3, 1, 2, 4)
    w5 = np.stack([wqkv[..., 0, :], wqkv[..., 0, exchange2], wqkv[..., 1, :], wqkv[..., 1, exchange2],
                   wqkv[..., 2, :]], axis=3)
    a["w5"] = c(w5.reshape(DEPTH * NHP, P, 5, P))
    a["wo6"] = c(g["L1_ffn_Wo"].reshape(DEPTH, NHP, P, P).transpose(0, 2, 1, 3))
    a["w1"] = g["L1_ffn_W1"]
    w2 = np.zeros((DEPTH, 3 * P, P), np.float32)
    w2[:, :GI] = g["L1_ffn_W2"]
    a["w2"] = c(w2.reshape(DEPTH, 3, P, P).transpose(0, 2, 1, 3))
    col = np.zeros((DEPTH, P, NCOL), np.float32)
    for k, n in ((C_Q, "q_scale"), (C_K, "k_scale")):
        col[:, :, k] = np.tile(g[f"L1_ffn_{n}"], (1, 2))
        col[:, :, k + 1] = np.tile(g[f"L1_ffn_{n}"][:, exchange], (1, 2))
    col[:, :, C_G], col[:, :, C_B], col[:, :, C_B2] = g["L1_ffn_ln_g"], g["L1_ffn_ln_b"], g["L1_ffn_b2"]
    for t, rows in enumerate(GT):
        col[:, :rows, C_A + t] = g["L1_ffn_b1"][:, t * P:t * P + rows]
        col[:, :rows, C_GATE + t] = g["L1_ffn_b1"][:, GI + t * P:GI + t * P + rows]
    a["col"] = col
    a["ident"] = np.eye(P, dtype=np.float32)
    a["headsel"] = np.repeat(np.eye(H0, dtype=np.float32), HD, axis=0)
    return a


SCRATCH = {
    "xs_stash": ([2, P, T], F32),
    "v1": ([T, NK1 * HD], F32),
    "q1": ([(B * NK1 + 2) * QPK, 3, HD, S], BF16),
    "k1": ([B * NK1 + 2, 3, HD, S], BF16),
    "m1all": ([(B * NK1 + 2) * QPK, S], BF16),
    "ones1": ([1, S], BF16),
    "o1": ([B * NQ1 + 1, 2, HD + 1, S], F32),
    "combineT": ([E_, T], F32),
    "qp": ([B * H0, KROWS + 1, S], BF16),
    "o0": ([B * H0 + 1, 2, HD + 1, S], F32),
    "kp": ([3, B * H0 + 2, KROWS + 1, S], BF16),
}


def kernel(**inputs):
    import numpy as np
    import concourse.bacc as bacc
    from concourse.bass_utils import run_bass_kernel_spmd as run

    nc = bacc.Bacc("TRN2", target_bir_lowering=False, num_devices=1)
    arrays = host_arrays(inputs)
    d = {}
    for name, a in arrays.items():
        d[name] = nc.dram_tensor(f"in_{name}", a.shape, mybir.dt.from_np(a.dtype), kind="ExternalInput").ap()
    for name, (shape, dt) in SCRATCH.items():
        d[name] = nc.dram_tensor(f"scratch_{name}", shape, dt).ap()
    d["m1"], d["m1pad"] = d["m1all"][0:B * NQ1], d["m1all"][B * NQ1:]
    d["out"] = nc.dram_tensor("out", (T, D), F32, kind="ExternalOutput").ap()
    build(nc, d)
    r = run(nc, [{f"in_{n}": a for n, a in arrays.items()}], core_ids=[0])
    return r.results[0]["out"].reshape(B, S, D)
```

```python
from contextlib import ExitStack

import concourse.bass as bass
from concourse import mybir

F32 = mybir.dt.float32
BF16 = mybir.dt.bfloat16
ALU = mybir.AluOpType
ACT = mybir.ActivationFunctionType
AX = mybir.AxisListType

P = 128
B, S, D = 2, 1024, 128
T = B * S
NT = T // P
CH = 512
NC = T // CH
ST = S // P
LN2 = 0.6931471805599453
LN_EPS = 1e-5

HD = 8
H0 = 16
NREL = 257
NPACK = 6
KROWS = NPACK * HD
QPART = (0, 0, 1, 1, 0, 2)
KPART = (0, 1, 0, 1, 2, 0)
VW = 32
SCALE = float(1.0 / (HD ** 0.5))


class Chain:

    def __init__(self, eng, sem, start=0, per=0, turn=None):
        self.eng, self.sem, self.n, self.per, self.turn, self.start = eng, sem, start, per, turn, start

    def value(self):
        return self.n if self.turn is None else self.turn * self.per + self.n

    def __call__(self, ins):
        self.n += 1
        ins.then_inc(self.sem, 1)
        self.eng.wait_ge(self.sem, self.value())

    def end(self):
        assert self.turn is None or self.n - self.start == self.per, (self.n - self.start, self.per)
        return self.start + self.per


class Stage:

    def __init__(self, nc, name):
        self.nc, self.name, self.ctx, self.sems = nc, name, ExitStack(), []

    def __enter__(self):
        self.ctx.__enter__()
        return self

    def __exit__(self, *a):
        done = self.ctx.__exit__(*a)
        if a[0] is None:
            self.nc.clear_and_free_semaphores(self.sems)
            self.nc.all_engine_barrier()
        return done

    def sb(self, name, shape, dt=F32):
        return self.ctx.enter_context(self.nc.sbuf_tensor(f"{self.name}_{name}", shape, dt))

    def ps(self, name, shape, dt=F32):
        return self.ctx.enter_context(self.nc.psum_tensor(f"{self.name}_{name}", shape, dt))

    def sem(self, name):
        self.sems.append(self.nc.alloc_semaphore(f"{self.name}_{name}"))
        return self.sems[-1]

    def block(self):
        return self.ctx.enter_context(self.nc.Block())


def stage_norm(nc, name, ident, xT, xnT, x_dram=None, ident_dram=None):
    with Stage(nc, name) as st:
        x = st.sb("x", [P, NT, D])
        xc = st.sb("xc", [P, NT, D])
        sq = st.sb("sq", [P, NT, D])
        small = st.sb("small", [P, 4, NT])
        ps = st.ps("turned", [P, 8, CH])
        loaded, tokens_turned, tokens_ready = st.sem("loaded"), st.sem("tokens_turned"), st.sem("tokens_ready")
        var_ready, std_ready, normed = st.sem("var_ready"), st.sem("std_ready"), st.sem("normed")
        turned, chain = st.sem("turned"), st.sem("chain")
        block = st.block()

        @block.sync
        def _(sp):
            if x_dram is not None:
                sp.dma_start(ident[:], ident_dram).then_inc(loaded, 16)
                sp.dma_start(x[:], x_dram.rearrange("(n p) d -> p n d", p=P)).then_inc(loaded, 16)

        @block.tensor
        def _(pe):
            if x_dram is not None:
                pe.wait_ge(loaded, 32)
            for n in range(NT):
                src = x[:, n, :] if x_dram is not None else xT[:, n * P:(n + 1) * P]
                mm = pe.transpose(ps[:, n // 4, (n % 4) * P:(n % 4 + 1) * P], src, ident[:])
                if n % 4 == 3:
                    mm.then_inc(tokens_turned, 1)
            pe.wait_ge(normed, 1)
            for n in range(NT):
                mm = pe.transpose(ps[:, 4 + n // 4, (n % 4) * P:(n % 4 + 1) * P], xc[:, n, :], ident[:])
                if n % 4 == 3:
                    mm.then_inc(turned, 1)

        @block.scalar
        def _(act):
            for c in range(NC):
                act.wait_ge(tokens_turned, c + 1)
                if x_dram is not None:
                    dst = xT[:, c * CH:(c + 1) * CH]
                else:
                    dst = x[:, 4 * c:4 * c + 4, :].rearrange("p n d -> p (n d)")
                act.copy(dst, ps[:, c, :]).then_inc(tokens_ready, 1)
            act.wait_ge(var_ready, 1)
            act.activation(small[:, 2, :], small[:, 1, :], ACT.Sqrt).then_inc(std_ready, 1)

        @block.vector
        def _(dve):
            link = Chain(dve, chain)
            if x_dram is not None:
                dve.wait_ge(loaded, 32)
            else:
                dve.wait_ge(tokens_ready, NC)
            mean, var, std = small[:, 0, :], small[:, 1, :], small[:, 2, :]
            link(dve.tensor_reduce(mean, x[:], AX.X, ALU.add))
            link(dve.tensor_scalar(mean, mean, 1.0 / D, None, ALU.mult))
            link(dve.tensor_tensor(xc[:], x[:], mean.unsqueeze(2).broadcast_to((P, NT, D)), ALU.subtract))
            link(dve.tensor_tensor(sq[:], xc[:], xc[:], ALU.mult))
            link(dve.tensor_reduce(var, sq[:], AX.X, ALU.add))
            dve.tensor_scalar(var, var, 1.0 / D, LN_EPS, ALU.mult, ALU.add).then_inc(var_ready, 1)
            dve.wait_ge(std_ready, 1)
            link(dve.reciprocal(small[:, 3, :], std))
            dve.tensor_tensor(xc[:], xc[:], small[:, 3, :].unsqueeze(2).broadcast_to((P, NT, D)),
                              ALU.mult).then_inc(normed, 1)
            for c in range(NC):
                dve.wait_ge(turned, c + 1)
                dve.tensor_copy(xnT[:, c * CH:(c + 1) * CH], ps[:, 4 + c, :])


def split_parts(link, dve, src, hi, mid, lo, r1, r2):
    link(dve.tensor_copy(hi, src))
    link(dve.tensor_tensor(r1, src, hi, ALU.subtract))
    link(dve.tensor_copy(mid, r1))
    link(dve.tensor_tensor(r2, r1, mid, ALU.subtract))
    link(dve.tensor_copy(lo, r2))


def stage_project0(nc, d, xnT, qT, vaug, relmax):
    with Stage(nc, "proj0") as st:
        wq, wk, wv = st.sb("wq", [P, D]), st.sb("wk", [P, D]), st.sb("wv", [P, D])
        bq, bk, bv = st.sb("bq", [P, 1]), st.sb("bk", [P, 1]), st.sb("bv", [P, D])
        rel = st.sb("rel", [P, NREL])
        kT = st.sb("kT", [P, 3, T])
        parts = st.sb("parts", [P, 4, 3, T], BF16)
        r1, r2 = st.sb("r1", [P, T]), st.sb("r2", [P, T])
        ones = st.sb("ones", [P, S], BF16)
        ps = st.ps("qkv", [P, 8, CH])
        loaded, mm_done, copied, chain = st.sem("loaded"), st.sem("mm_done"), st.sem("copied"), st.sem("chain")
        v_mm, split_done, stored = st.sem("v_mm"), st.sem("split_done"), st.sem("stored")
        ones_ready, v_copied = st.sem("ones_ready"), st.sem("v_copied")
        block = st.block()

        @block.sync
        def _(sp):
            for dst, src in ((wq, d["wqT"]), (wk, d["wkT"]), (wv, d["wvT"]), (bq, d["bq"]), (bk, d["bk"]),
                             (rel, d["rel_rows"])):
                sp.dma_start(dst[:], src).then_inc(loaded, 16)
            sp.dma_start(bv[:], d["bv"].partition_broadcast(P)).then_inc(loaded, 16)
            sp.wait_ge(ones_ready, 1)
            n = 0
            for v in range(3):
                sp.dma_start(d["kp"][v, 0:B * H0, KROWS, :], ones[0:B * H0, :]).then_inc(stored, 16)
                sp.dma_start(d["kp"][v, B * H0:, :, :].rearrange("h r s -> (h r) s"),
                             ones[0:2 * (KROWS + 1), :]).then_inc(stored, 16)
                n += 2
            for v in range(4):
                sp.wait_ge(split_done, v + 1)
                for blk in range(NPACK):
                    part = (QPART if v == 0 else KPART)[blk]
                    for b in range(B):
                        pack = d["qp"] if v == 0 else d["kp"][v - 1]
                        dst = pack[b * H0:(b + 1) * H0, blk * HD:(blk + 1) * HD, :]
                        sp.dma_start(dst, parts[:, v, part, b * S:(b + 1) * S]).then_inc(stored, 16)
                        n += 1
            sp.wait_ge(stored, 16 * n)

        @block.tensor
        def _(pe):
            pe.wait_ge(loaded, 16 * 7)
            for c in range(NC):
                cols = xnT[:, c * CH:(c + 1) * CH]
                if c >= 2:
                    pe.wait_ge(copied, 2 * c - 2)
                pe.matmul(ps[:, 2 * (c % 2), :], wq[:], cols, start=True, stop=True).then_inc(mm_done, 1)
                pe.matmul(ps[:, 2 * (c % 2) + 1, :], wk[:], cols, start=True, stop=True).then_inc(mm_done, 1)
            for n in range(NT):
                mm = pe.matmul(ps[:, 4 + n // 4, (n % 4) * P:(n % 4 + 1) * P], xnT[:, n * P:(n + 1) * P], wv[:],
                               start=True, stop=True)
                if n % 4 == 3:
                    mm.then_inc(v_mm, 1)

        @block.scalar
        def _(act):
            for c in range(NC):
                act.wait_ge(mm_done, 2 * c + 1)
                act.activation(qT[:, c * CH:(c + 1) * CH], ps[:, 2 * (c % 2), :], ACT.Identity,
                               bias=bq[:, 0:1]).then_inc(copied, 1)
                act.wait_ge(mm_done, 2 * c + 2)
                act.activation(kT[:, 0, c * CH:(c + 1) * CH], ps[:, 2 * (c % 2) + 1, :], ACT.Identity,
                               bias=bk[:, 0:1]).then_inc(copied, 1)

        @block.vector
        def _(dve):
            link = Chain(dve, chain)
            dve.memset(ones[:], 1.0).then_inc(ones_ready, 1)
            dve.memset(vaug[:], 1.0).then_inc(v_copied, 1)
            dve.wait_ge(loaded, 16 * 7)
            dve.tensor_reduce(relmax[:, 0:1], rel[:], AX.X, ALU.max)
            dve.tensor_reduce(relmax[:, 1:2], rel[:], AX.X, ALU.min)
            dve.wait_ge(copied, 2 * NC)
            link(dve.tensor_scalar(kT[:, 1, :], kT[:, 0, :], rel[:, 0:1], None, ALU.add))
            link(dve.tensor_scalar(kT[:, 2, :], kT[:, 0, :], rel[:, NREL - 1:NREL], None, ALU.add))
            for v in range(4):
                src = qT[:] if v == 0 else kT[:, v - 1, :]
                link(dve.tensor_copy(parts[:, v, 0, :], src))
                link(dve.tensor_tensor(r1[:], src, parts[:, v, 0, :], ALU.subtract))
                link(dve.tensor_copy(parts[:, v, 1, :], r1[:]))
                link(dve.tensor_tensor(r2[:], r1[:], parts[:, v, 1, :], ALU.subtract))
                link(dve.tensor_copy(parts[:, v, 2, :], r2[:]))
                dve.sem_inc(split_done, 1)
            dve.wait_ge(v_copied, 1)
            for c in range(NC):
                dve.wait_ge(v_mm, c + 1)
                for u in range(4):
                    n = 4 * c + u
                    b, J = n // ST, n % ST
                    dve.tensor_tensor(vaug[:, b * H0:(b + 1) * H0, J, 0:HD],
                                      ps[:, 4 + c, u * P:(u + 1) * P].rearrange("p (h e) -> p h e", e=HD),
                                      bv[:].rearrange("p (h e) -> p h e", e=HD), ALU.add)


def stage_max0(nc, d, ident, qT, relmax):
    NH = B * H0
    with Stage(nc, "max0") as st:
        qh = st.sb("qh", [P, 2, S], BF16)
        kh = st.sb("kh", [P, 2, S], BF16)
        mcol = st.sb("mcol", [P, ST, NH])
        headsel = st.sb("headsel", [P, H0])
        relsel = st.sb("relsel", [P, 2, 2, NH])
        qpos, qneg = st.sb("qpos", [P, T]), st.sb("qneg", [P, T])
        mrow = st.sb("mrow", [NH, S], BF16)
        ps = st.ps("scores", [P, 4, 2 * CH])
        loaded = [st.sem("loaded0"), st.sem("loaded1")]
        zeroed, scored, maxed = st.sem("zeroed"), st.sem("scored"), st.sem("maxed")
        sel_loaded, bound_ready, rows, rows_out = (st.sem("sel_loaded"), st.sem("bound_ready"), st.sem("rows"),
                                                   st.sem("rows_out"))
        stored, chain, head_used = st.sem("stored"), st.sem("chain"), st.sem("head_used")
        block = st.block()

        @block.sync
        def _(sp):
            sp.dma_start(headsel[:], d["headsel"]).then_inc(sel_loaded, 16)
            sp.wait_ge(zeroed, 1)

            def load(bh, slot):
                sp.dma_start(qh[0:KROWS, slot, :], d["qp"][bh, 0:KROWS, :]).then_inc(loaded[slot], 16)
                sp.dma_start(kh[0:KROWS, slot, :], d["kp"][0, bh, 0:KROWS, :]).then_inc(loaded[slot], 16)

            load(0, 0)
            load(1, 1)
            with sp.Fori(0, NH // 2 - 1) as i:
                for s in range(2):
                    sp.wait_ge(head_used, 2 * i + s + 1)
                    load(2 * i + 2 + s, s)
            sp.wait_ge(rows_out, 2)
            sp.dma_start(d["qp"][:, KROWS, :], mrow[:]).then_inc(stored, 16)
            sp.wait_ge(stored, 16)

        @block.gpsimd
        def _(pool):
            pool.memset(qh[:], 0.0)
            pool.memset(kh[:], 0.0).then_inc(zeroed, 1)

        @block.tensor
        def _(pe):
            with pe.Fori(0, NH // 2) as i:
                for s in range(2):
                    pe.wait_ge(loaded[s], 32 * i + 32)
                    for u in range(ST):
                        pe.wait_ge(maxed, (2 * i + s) * ST + u + 1)
                        for c in range(2):
                            mm = pe.matmul(ps[:, u % 4, c * CH:(c + 1) * CH], qh[:, s, u * P:(u + 1) * P],
                                           kh[:, s, c * CH:(c + 1) * CH], start=True, stop=True)
                        mm.then_inc(scored, 1)
            pe.wait_ge(bound_ready, 1)
            pe.wait_ge(maxed, NH * ST + 4)
            for u in range(ST):
                out = ps[0:NH, 0, u * P:(u + 1) * P]
                pe.matmul(out, mcol[:, u, :], ident[:], start=True, stop=False)
                for b in range(B):
                    cols = slice(b * S + u * P, b * S + (u + 1) * P)
                    pe.matmul(out, relsel[:, 0, b, :], qpos[:, cols], start=False, stop=False)
                    mm = pe.matmul(out, relsel[:, 1, b, :], qneg[:, cols], start=False, stop=(b == B - 1))
                if u % 4 == 3:
                    mm.then_inc(rows, 1)

        @block.scalar
        def _(act):
            for c in range(2):
                act.wait_ge(rows, c + 1)
                act.mul(mrow[:, c * CH:(c + 1) * CH], ps[0:NH, 0, c * CH:(c + 1) * CH], -1.0).then_inc(rows_out, 1)

        @block.vector
        def _(dve):
            link = Chain(dve, chain)
            dve.sem_inc(maxed, 4)
            link(dve.tensor_scalar(qpos[:], qT[:], 0.0, None, ALU.max))
            link(dve.tensor_scalar(qneg[:], qT[:], 0.0, None, ALU.min))
            link(dve.memset(relsel[:], 0.0))
            dve.wait_ge(sel_loaded, 16)
            for w in range(2):
                for b in range(B):
                    link(dve.tensor_scalar(relsel[:, w, b, b * H0:(b + 1) * H0], headsel[:], relmax[:, w:w + 1],
                                           None, ALU.mult))
            dve.sem_inc(bound_ready, 1)
            with dve.Fori(0, NH // 2) as i:
                for s in range(2):
                    for u in range(ST):
                        dve.wait_ge(scored, (2 * i + s) * ST + u + 1)
                        dve.tensor_reduce(mcol[:, u, bass.ds(2 * i + s, 1)], ps[:, u % 4, :], AX.X,
                                          ALU.max).then_inc(maxed, 1)
                        if u == ST - 1:
                            dve.sem_inc(head_used, 1)


def stage_attend0(nc, d, vaug):
    NH = B * H0
    G = 8
    NG = NH // G
    U = CH // (ST * G)
    NW = 3 * P // U
    HALF = NW // 2
    with Stage(nc, "att0") as st:
        relrow = st.sb("relrow", [HD, CH])
        relparts = st.sb("relparts", [HD, 3, CH], BF16)
        relr = st.sb("relr", [HD, 2, CH])
        relpack = st.sb("relpack", [P, CH], BF16)
        qg = st.sb("qg", [P, G, S], BF16)
        rel = st.sb("rel", [P, 3, P, ST, G])
        kh = st.sb("kh", [P, 2, 3, S], BF16)
        pr = st.sb("pr", [P, 4, S])
        vh = st.sb("vh", [P, 2, ST, VW])
        ob = st.sb("ob", [P, 2, CH])
        ps = st.ps("ps", [P, 8, CH])
        rel_loaded, rel_split, chain = st.sem("rel_loaded"), st.sem("rel_split"), st.sem("chain")
        rel_packed, zeroed = st.sem("rel_packed"), st.sem("zeroed")
        q_loaded = st.sem("q_loaded")
        k_loaded = [st.sem("k_loaded0"), st.sem("k_loaded1")]
        stored = [st.sem("stored0"), st.sem("stored1")]
        win_done, win_act, win_dve = st.sem("win_done"), st.sem("win_act"), st.sem("win_dve")
        qk_done, rel_added, exp_done = st.sem("qk_done"), st.sem("rel_added"), st.sem("exp_done")
        pv_done, out_copied, v_copied = st.sem("pv_done"), st.sem("out_copied"), st.sem("v_copied")
        turns_begun = st.sem("turns_begun")
        block = st.block()

        @block.sync
        def _(sp):
            sp.dma_start(relrow[:], d["rel_reversed"]).then_inc(rel_loaded, 16)
            sp.wait_ge(zeroed, 1)
            sp.wait_ge(rel_split, 1)
            for blk in range(NPACK):
                sp.dma_start(relpack[blk * HD:(blk + 1) * HD, :], relparts[:, KPART[blk], :]).then_inc(rel_packed, 16)

            def load_k(bh, slot):
                sp.dma_start(kh[0:KROWS + 1, slot, :, :],
                             d["kp"][:, bh, :, :].rearrange("v r s -> r v s")).then_inc(k_loaded[slot], 16)

            def load_q(g):
                sp.dma_start(qg[0:KROWS + 1, :, :],
                             d["qp"][bass.ds(g * G, G), :, :].rearrange("h r s -> r h s")).then_inc(q_loaded, 16)

            def store(row, slot):
                for quad in range(4):
                    sp.dma_start(d["o0"][row, quad // 2, :, (quad % 2) * CH:(quad % 2 + 1) * CH],
                                 ob[32 * quad:32 * quad + HD + 1, slot, :]).then_inc(stored[slot], 16)

            load_k(0, 0)
            load_k(1, 1)
            with sp.Fori(0, NG) as g:
                sp.wait_ge(qk_done, g * G * ST + 1)
                load_q(g)
                with sp.Fori(0, G // 2) as i:
                    for s in range(2):
                        bh = g * G + 2 * i + s
                        sp.wait_ge(out_copied, bh + 3)
                        store(bh, 1 - s)
                        sp.wait_ge(qk_done, (bh + 1) * ST + 1)
                        load_k(bh + 2, s)
            sp.wait_ge(out_copied, NH + 3)
            store(NH, 1)
            for s in range(2):
                sp.wait_ge(stored[s], 16 + 64 * (NH // 2 + s))
                sp.wait_ge(k_loaded[s], 16 * (NH // 2 + 1))

        @block.gpsimd
        def _(pool):
            pool.memset(relpack[:], 0.0)
            pool.memset(qg[:], 0.0)
            pool.memset(kh[:], 0.0)
            pool.memset(pr[:], 0.0)
            pool.memset(vh[:], 0.0).then_inc(zeroed, 1)
            pool.wait_ge(zeroed, 1)
            with pool.Fori(0, NH // 2) as i:
                for s in range(2):
                    bh = 2 * i + s
                    pool.wait_ge(pv_done, bh * (ST // 2) + 1)
                    pool.tensor_copy(vh[:, s, :, 0:HD + 1], vaug[:, bass.ds(bh, 1), :, :]).then_inc(v_copied, 1)

        @block.tensor
        def _(pe):
            def qk(h, slot, J, n):
                pe.wait_ge(exp_done, n + 1)
                near = (max(J - 1, 0) * P, min(J + 2, ST) * P)
                for v, lo, hi in ((1, 0, near[0]), (0, *near), (2, near[1], S)):
                    while lo < hi:
                        end = min(hi, CH if lo < CH else S)
                        mm = pe.matmul(ps[:, 2 * (J % 2) + lo // CH, lo % CH:(end - 1) % CH + 1],
                                       kh[:, slot, v, J * P:(J + 1) * P], qg[:, h, lo:end], start=True, stop=True)
                        lo = end
                mm.then_inc(qk_done, 1)

            def pv(slot, m, n):
                pe.wait_ge(exp_done, n + 3)
                for J in (2 * m, 2 * m + 1):
                    for c in range(2):
                        quad = 32 * (2 * (J % 2) + c)
                        mm = pe.matmul(ps[quad:quad + VW, 6 + slot, :], vh[:, slot, J, :],
                                       pr[:, J % 4, c * CH:(c + 1) * CH], start=(m == 0), stop=(m == ST // 2 - 1),
                                       skip_group_check=True, tile_position=(0, quad))
                mm.then_inc(pv_done, 1)

            pe.sem_inc(qk_done, 1)
            pe.wait_ge(zeroed, 1)
            pe.wait_ge(out_copied, 2)
            pe.wait_ge(rel_packed, 16 * NPACK)
            with pe.Fori(0, NG) as g:
                pe.wait_ge(q_loaded, 16 * g + 16)
                pe.wait_ge(exp_done, g * G * ST + 2)
                for k in range(NW):
                    pe.wait_ge((win_act, win_dve)[k % 2], g * HALF + k // 2 + 1)
                    for u in range(U):
                        ii = (k // 3) * U + u
                        mm = pe.matmul(ps[:, k % 6, u * ST * G:(u + 1) * ST * G],
                                       relpack[:, 255 - P * (k % 3 - 1) - ii:][:, 0:P],
                                       qg[:].rearrange("p h (t i) -> p t h i", i=P)[:, :, :, ii],
                                       start=True, stop=True)
                    mm.then_inc(win_done, 1)
                pe.wait_ge(win_act, (g + 1) * HALF + 3)
                pe.wait_ge(win_dve, (g + 1) * HALF + 3)
                pe.sem_inc(turns_begun, 1)
                with pe.Fori(0, G // 2) as i:
                    for s in range(2):
                        bh = g * G + 2 * i + s
                        pe.wait_ge(k_loaded[s], (g * (G // 2) + i) * 16 + 16)
                        for m in range(ST // 2):
                            n = bh * ST + 2 * m
                            qk(bass.ds(2 * i + s, 1), s, 2 * m, n)
                            qk(bass.ds(2 * i + s, 1), s, 2 * m + 1, n + 1)
                            if m == 0:
                                pv(1 - s, ST // 2 - 1, n - 1)
                                pe.wait_ge(v_copied, bh + 1)
                                pe.wait_ge(out_copied, bh + 2)
                            else:
                                pv(s, m - 1, n - 1)
            pv(1, ST // 2 - 1, NH * ST - 1)

        @block.scalar
        def _(act):
            act.sem_inc(exp_done, 2)
            act.sem_inc(win_act, 3)
            act.wait_ge(zeroed, 1)
            with act.Fori(0, NG) as g:
                act.wait_ge(rel_added, g * G * ST + 1)
                for k in range(0, NW, 2):
                    act.wait_ge(win_done, g * NW + k + 1)
                    act.copy(rel[:, k % 3, (k // 3) * U:(k // 3 + 1) * U, :, :].rearrange("p a b c -> p (a b c)"),
                             ps[:, k % 6, :]).then_inc(win_act, 1)
                with act.Fori(0, G) as h:
                    for J in range(ST):
                        bh = g * G + h
                        act.wait_ge(rel_added, bh * ST + J + 2)
                        act.wait_ge(pv_done, bh * (ST // 2) + J // 2 + 4)
                        act.activation(pr[:, J % 4, :],
                                       ps[:, 2 * (J % 2):2 * (J % 2) + 2, :].rearrange("p a b -> p (a b)"),
                                       ACT.Exp, scale=SCALE).then_inc(exp_done, 1)

        @block.vector
        def _(dve):
            link = Chain(dve, chain)
            dve.sem_inc(win_dve, 3)
            dve.sem_inc(rel_added, 1)
            dve.sem_inc(pv_done, 4)
            dve.sem_inc(stored[0], 16)
            dve.sem_inc(stored[1], 16)
            link(dve.memset(ps[:, 6:8, :], 0.0))
            dve.sem_inc(out_copied, 2)
            dve.wait_ge(rel_loaded, 16)
            split_parts(link, dve, relrow[:], relparts[:, 0, :], relparts[:, 1, :], relparts[:, 2, :],
                        relr[:, 0, :], relr[:, 1, :])
            dve.sem_inc(rel_split, 1)

            def copy_out(slot, bh_done, rounds):
                dve.wait_ge(pv_done, bh_done * (ST // 2) + 5)
                dve.wait_ge(stored[slot], rounds)
                dve.tensor_copy(ob[:, slot, :], ps[:, 6 + slot, :]).then_inc(out_copied, 1)

            with dve.Fori(0, NG) as g:
                for k in range(1, NW, 2):
                    dve.wait_ge(win_done, g * NW + k + 1)
                    dve.tensor_copy(
                        rel[:, k % 3, (k // 3) * U:(k // 3 + 1) * U, :, :].rearrange("p a b c -> p (a b c)"),
                        ps[:, k % 6, :]).then_inc(win_dve, 1)
                dve.wait_ge(win_act, (g + 1) * HALF + 3)
                dve.wait_ge(win_dve, (g + 1) * HALF + 3)
                dve.sem_inc(turns_begun, 1)
                with dve.Fori(0, G // 2) as i:
                    for s in range(2):
                        bh = g * G + 2 * i + s
                        for J in range(ST):
                            dve.wait_ge(qk_done, bh * ST + J + 2)
                            for D_ in range(3):
                                I = J + D_ - 1
                                if not 0 <= I < ST:
                                    continue
                                sc = ps[:, 2 * (J % 2) + I // 4, (I % 4) * P:(I % 4 + 1) * P]
                                ins = dve.tensor_tensor(sc, sc, rel[:, D_, :, I, bass.ds(2 * i + s, 1)], ALU.add)
                            ins.then_inc(rel_added, 1)
                            if J == 3:
                                copy_out(1 - s, bh, 16 + 64 * (g * (G // 2) + i))
            copy_out(1, NH, 16 + 64 * (NH // 2))


def stage_combine0(nc, d, qT, sT):
    with Stage(nc, "comb0") as st:
        num, den = st.sb("num", [P, 2, T]), st.sb("den", [P, 2, T])
        wo, bo, mrep, z, blk = (st.sb("wo", [P, D]), st.sb("bo", [P, 1]), st.sb("mrep", [P, P]), st.sb("z", [P, 1]),
                                st.sb("blk", [P, P]))
        mblk, zblk = st.sb("mblk", [P, P]), st.sb("zblk", [P, P])
        gate = st.sb("gate", [P, 3])
        sig, neg = st.sb("sig", [P, T]), st.sb("neg", [P, T])
        ps = st.ps("ps", [P, 8, CH])
        weights, sums, chain = st.sem("weights"), st.sem("sums"), st.sem("chain")
        neg_ready, exp_ready, blocks_ready, glob = (st.sem("neg_ready"), st.sem("exp_ready"),
                                                    st.sem("blocks_ready"), st.sem("glob"))
        gate_ready, mixed, projected = st.sem("gate_ready"), st.sem("mixed"), st.sem("projected")
        block = st.block()

        @block.sync
        def _(sp):
            for dst, src in ((wo, d["woT"]), (bo, d["bo"]), (mrep, d["mrep"]), (z, d["z"]), (blk, d["headblk"])):
                sp.dma_start(dst[:], src).then_inc(weights, 16)
            sp.dma_start(gate[:, 0:1], d["alpha"].partition_broadcast(P)).then_inc(weights, 16)
            for quad in range(2):
                for b in range(B):
                    rows = d["o0"][1 + b * H0:1 + (b + 1) * H0, quad, :, :]
                    sp.dma_start(num[:, quad, b * S:(b + 1) * S], rows[:, 0:HD, :]).then_inc(sums, 16)
                    sp.dma_start(den[:, quad, b * S:(b + 1) * S],
                                 rows[:, HD:HD + 1, :].broadcast_to((H0, HD, S))).then_inc(sums, 16)

        @block.scalar
        def _(act):
            act.wait_ge(weights, 16 * 6)
            act.activation(gate[:, 1:2], gate[:, 0:1], ACT.Sigmoid).then_inc(gate_ready, 1)
            act.wait_ge(neg_ready, 1)
            act.activation(neg[:], neg[:], ACT.Exp).then_inc(exp_ready, 1)
            for c in range(NC):
                act.wait_ge(projected, c + 1)
                act.activation(sT[:, c * CH:(c + 1) * CH], ps[:, c, :], ACT.Identity, bias=bo[:, 0:1])

        @block.tensor
        def _(pe):
            pe.wait_ge(blocks_ready, 1)
            for c in range(NC):
                pe.matmul(ps[:, c, :], mblk[:], sig[:, c * CH:(c + 1) * CH], start=True, stop=True)
                mm = pe.matmul(ps[:, 4 + c, :], zblk[:], sig[:, c * CH:(c + 1) * CH], start=True, stop=True)
            mm.then_inc(glob, 1)
            pe.wait_ge(mixed, 1)
            for c in range(NC):
                pe.matmul(ps[:, c, :], wo[:], num[:, 0, c * CH:(c + 1) * CH],
                          start=True, stop=True).then_inc(projected, 1)

        @block.vector
        def _(dve):
            link = Chain(dve, chain)
            dve.tensor_scalar(neg[:], qT[:], 0.0, None, ALU.min).then_inc(neg_ready, 1)
            link(dve.tensor_scalar(sig[:], qT[:], 0.0, None, ALU.max))
            dve.wait_ge(weights, 16 * 6)
            link(dve.tensor_tensor(mblk[:], mrep[:], blk[:], ALU.mult))
            link(dve.tensor_scalar(zblk[:], blk[:], z[:, 0:1], None, ALU.mult))
            dve.wait_ge(exp_ready, 1)
            dve.tensor_tensor(sig[:], sig[:], neg[:], ALU.add).then_inc(blocks_ready, 1)
            dve.wait_ge(gate_ready, 1)
            link(dve.tensor_scalar(gate[:, 2:3], gate[:, 1:2], -1.0, 1.0, ALU.mult, ALU.add))
            dve.wait_ge(sums, 16 * 8)
            for x in (num, den):
                link(dve.tensor_tensor(x[:, 0, :], x[:, 0, :], x[:, 1, :], ALU.add))
            link(dve.reciprocal(den[:, 0, :], den[:, 0, :]))
            link(dve.tensor_tensor(num[:, 0, :], num[:, 0, :], den[:, 0, :], ALU.mult))
            dve.wait_ge(glob, 1)
            for c in range(NC):
                g = den[:, 1, c * CH:(c + 1) * CH]
                link(dve.tensor_scalar(g, ps[:, 4 + c, :], 1e-6, None, ALU.add))
                link(dve.reciprocal(g, g))
                link(dve.tensor_tensor(g, g, ps[:, c, :], ALU.mult))
            link(dve.tensor_scalar(den[:, 1, :], den[:, 1, :], gate[:, 2:3], None, ALU.mult))
            dve.scalar_tensor_tensor(num[:, 0, :], num[:, 0, :], gate[:, 1:2], den[:, 1, :], ALU.mult,
                                     ALU.add).then_inc(mixed, 1)


E_, EI = 32, 64
EG, EPG = 8, 4
TOP_GROUPS, TOP_K = 4, 8
ROUTE_SCALE = 2.5


def stage_route(nc, d, xnT):
    with Stage(nc, "route") as st:
        gw, gb = st.sb("gw", [P, E_]), st.sb("gb", [P, E_])
        score, sc, pick = st.sb("score", [P, NT, E_]), st.sb("sc", [P, NT, E_]), st.sb("pick", [P, NT, E_])
        grp, gsel, t8 = st.sb("grp", [P, NT, EG]), st.sb("gsel", [P, NT, EG]), st.sb("t8", [P, NT, EG])
        cmp_ = st.sb("cmp", [P, NT, E_, E_])
        tot = st.sb("tot", [P, NT])
        ident = st.sb("ident", [P, P])
        cT = st.sb("cT", [E_, T])
        ps = st.ps("ps", [P, CH])
        psT = st.ps("psT", [E_, 4, CH])
        loaded, logits, scored, weighted = st.sem("loaded"), st.sem("logits"), st.sem("scored"), st.sem("weighted")
        turned, copied, stored, chain = st.sem("turned"), st.sem("copied"), st.sem("stored"), st.sem("chain")
        block = st.block()

        @block.sync
        def _(sp):
            sp.dma_start(gw[:], d["gate_wT"]).then_inc(loaded, 16)
            sp.dma_start(gb[:], d["gate_bias"].partition_broadcast(P)).then_inc(loaded, 16)
            sp.dma_start(ident[:], d["ident"]).then_inc(loaded, 16)
            sp.wait_ge(copied, 4)
            sp.dma_start(d["combineT"], cT[:]).then_inc(stored, 16)
            sp.wait_ge(stored, 16)

        @block.tensor
        def _(pe):
            pe.wait_ge(loaded, 48)
            for n in range(NT):
                mm = pe.matmul(ps[:, n * E_:(n + 1) * E_], xnT[:, n * P:(n + 1) * P], gw[:], start=True, stop=True)
            mm.then_inc(logits, 1)
            pe.wait_ge(weighted, 1)
            for n in range(NT):
                mm = pe.transpose(psT[:, n // 4, (n % 4) * P:(n % 4 + 1) * P], pick[:, n, :], ident[:])
                if n % 4 == 3:
                    mm.then_inc(turned, 1)

        @block.scalar
        def _(act):
            act.wait_ge(logits, 1)
            act.activation(score[:].rearrange("p a b -> p (a b)"), ps[:], ACT.Sigmoid).then_inc(scored, 1)
            for c in range(4):
                act.wait_ge(turned, c + 1)
                act.copy(cT[:, c * CH:(c + 1) * CH], psT[:, c, :]).then_inc(copied, 1)

        @block.vector
        def _(dve):
            link = Chain(dve, chain)
            dve.wait_ge(scored, 1)
            dve.wait_ge(loaded, 48)
            link(dve.tensor_tensor(sc[:], score[:], gb[:].unsqueeze(1).broadcast_to((P, NT, E_)), ALU.add))
            v = sc[:].rearrange("p n (g e) -> p n g e", e=EPG)
            pairs = [(i, j) for i in range(EPG) for j in range(i + 1, EPG)]
            for n, (i, j) in enumerate(pairs):
                link(dve.tensor_tensor((t8 if n else grp)[:], v[:, :, :, i], v[:, :, :, j], ALU.add))
                if n:
                    link(dve.tensor_tensor(grp[:], grp[:], t8[:], ALU.max))

            def rank(vals, K, out):
                for other in range(K):
                    for lo, hi, op in ((0, other + 1, ALU.is_gt), (other + 1, K, ALU.is_ge)):
                        if hi > lo:
                            last = dve.tensor_tensor(cmp_[:, :, lo:hi, other],
                                                     vals[:, :, other:other + 1].broadcast_to((P, NT, hi - lo)),
                                                     vals[:, :, lo:hi], op)
                link(last)
                link(dve.tensor_reduce(out, cmp_[:, :, 0:K, 0:K], AX.X, ALU.add))

            rank(grp, EG, t8[:])
            link(dve.tensor_scalar(gsel[:], t8[:], TOP_GROUPS - 0.5, None, ALU.is_lt))
            link(dve.tensor_tensor(v, v, gsel[:].unsqueeze(3).broadcast_to((P, NT, EG, EPG)), ALU.mult))
            rank(sc, E_, pick[:])
            link(dve.tensor_scalar(pick[:], pick[:], TOP_K - 0.5, None, ALU.is_lt))
            link(dve.tensor_tensor(pick[:], pick[:], score[:], ALU.mult))
            link(dve.tensor_reduce(tot[:], pick[:], AX.X, ALU.add))
            link(dve.tensor_scalar(tot[:], tot[:], 1e-20, None, ALU.add))
            link(dve.reciprocal(tot[:], tot[:]))
            link(dve.tensor_scalar(tot[:], tot[:], ROUTE_SCALE, None, ALU.mult))
            dve.tensor_tensor(pick[:], pick[:], tot[:].unsqueeze(2).broadcast_to((P, NT, E_)),
                              ALU.mult).then_inc(weighted, 1)


def stage_experts(nc, d, xnT, sT, xT):
    NP = E_ // 2
    with Stage(nc, "moe") as st:
        w = st.sb("w", [P, 2, 3, P])
        cb = st.sb("cb", [P, 2, T])
        g, h = st.sb("g", [P, 2, CH]), st.sb("h", [P, 2, CH])
        y, t = st.sb("y", [P, T]), st.sb("t", [P, T])
        ps = st.ps("ps", [P, 4, CH])
        acc = st.ps("acc", [P, 4, CH])
        loaded = [st.sem("loaded0"), st.sem("loaded1")]
        cb_loaded = [st.sem("cb_loaded0"), st.sem("cb_loaded1")]
        ones_ready = st.sem("ones_ready")
        up_done, silu_done, h_ready, h_scaled, down_done = (st.sem("up_done"), st.sem("silu_done"),
                                                            st.sem("h_ready"), st.sem("h_scaled"),
                                                            st.sem("down_done"))
        out_silu, chain = st.sem("out_silu"), st.sem("chain")
        block = st.block()

        @block.sync
        def _(sp):
            def load(src, slot):
                sp.dma_start(w[:, slot, :, :], src).then_inc(loaded[slot], 16)

            def load_weights(i, slot):
                for e in range(2):
                    row = d["combineT"][bass.ds(2 * i + e, 1), :]
                    sp.dma_start(cb[e * EI:(e + 1) * EI, slot, :],
                                 row.broadcast_to((EI, T))).then_inc(cb_loaded[slot], 16)

            load(d["moe_w"][0], 0)
            load(d["moe_w"][1], 1)
            load_weights(0, 1)
            sp.wait_ge(down_done, 4 + 4)
            load(d["moe_w"][2], 0)
            load_weights(1, 0)
            with sp.Fori(0, NP // 2 - 1) as i:
                for s in range(2):
                    sp.wait_ge(down_done, 4 * (2 * i + 2 + s) + 4)
                    load(d["moe_w"][bass.ds(2 * i + 3 + s, 1)].rearrange("o p a b -> p (o a) b"), 1 - s)
                    load_weights(2 * i + 2 + s, 1 - s)

        @block.tensor
        def _(pe):
            def up(slot, c, k):
                pe.wait_ge(h_ready, k + 1)
                for j in range(2):
                    mm = pe.matmul(ps[:, 2 * (c % 2) + j, :], w[:, slot, j, :], xnT[:, c * CH:(c + 1) * CH],
                                   start=True, stop=True)
                mm.then_inc(up_done, 1)

            def down(slot, c, k, first=False):
                pe.wait_ge(h_scaled, k + 1)
                pe.matmul(acc[:, c, :], w[:, slot, 2, :], h[:, c % 2, :], start=first, stop=False,
                          skip_group_check=True).then_inc(down_done, 1)

            pe.wait_ge(loaded[0], 16)
            up(0, 0, 0)
            for c in range(1, 4):
                up(0, c, c)
                down(0, c - 1, c - 1, first=True)
            pe.wait_ge(loaded[1], 16)
            up(1, 0, 4)
            down(0, 3, 3, first=True)
            with pe.Fori(0, NP // 2 - 1) as i:
                for s in range(2):
                    slot = 1 - s
                    k = 4 * (2 * i + 1 + s)
                    for c in range(1, 4):
                        up(slot, c, k + c)
                        down(slot, c - 1, k + c - 1)
                    pe.wait_ge(loaded[1 - slot], 16 * (i + 2))
                    up(1 - slot, 0, k + 4)
                    down(slot, 3, k + 3)
            for s in range(2):
                slot = 1 - s
                k = 4 * (NP - 1 + s)
                for c in range(1, 4):
                    up(slot, c, k + c)
                    down(slot, c - 1, k + c - 1)
                if s == 0:
                    pe.wait_ge(loaded[0], 16 * (NP // 2 + 1))
                    up(0, 0, k + 4)
                down(slot, 3, k + 3)

        @block.scalar
        def _(act):
            def silu(c, k):
                act.wait_ge(up_done, k + 1)
                act.wait_ge(h_ready, k + 1)
                act.activation(g[:, c % 2, :], ps[:, 2 * (c % 2), :], ACT.Silu).then_inc(silu_done, 1)

            for c in range(4):
                silu(c, c)
            with act.Fori(0, NP) as i:
                for c in range(4):
                    silu(c, 4 * i + 4 + c)
            for c in range(4):
                act.wait_ge(down_done, 4 * (NP + 1) + 4)
                act.activation(y[:, c * CH:(c + 1) * CH], acc[:, c, :], ACT.Silu).then_inc(out_silu, 1)

        @block.vector
        def _(dve):
            link = Chain(dve, chain)

            def mult(c, k):
                dve.wait_ge(silu_done, k + 1)
                dve.wait_ge(down_done, k + 3)
                dve.tensor_tensor(h[:, c % 2, :], g[:, c % 2, :], ps[:, 2 * (c % 2) + 1, :],
                                  ALU.mult).then_inc(h_ready, 1)

            dve.sem_inc(h_ready, 2)
            dve.sem_inc(down_done, 4)
            for c in range(4):
                mult(c, c)
            with dve.Fori(0, NP) as i:
                for c in range(4):
                    mult(c, 4 * i + 4 + c)
            for c in range(NC):
                cols = slice(c * CH, (c + 1) * CH)
                dve.wait_ge(out_silu, c + 1)
                link(dve.tensor_tensor(t[:, cols], y[:, cols], sT[:, cols], ALU.mult))
                dve.tensor_tensor(xT[:, cols], xT[:, cols], t[:, cols], ALU.add)

        @block.gpsimd
        def _(pool):
            for c in range(4):
                pool.wait_ge(h_ready, c + 3)
                pool.sem_inc(h_scaled, 1)
            with pool.Fori(0, NP // 2) as i:
                for s in range(2):
                    slot = 1 - s
                    pool.wait_ge(cb_loaded[slot], 32 * (i + 1))
                    for c in range(4):
                        k = 4 * (2 * i + 1 + s) + c
                        pool.wait_ge(h_ready, k + 3)
                        pool.tensor_tensor(h[:, c % 2, :], h[:, c % 2, :], cb[:, slot, c * CH:(c + 1) * CH],
                                           ALU.mult).then_inc(h_scaled, 1)


NQ1, NK1 = 32, 8
QPK = NQ1 // NK1
QPART1 = (0, 0, 0, 1, 1, 2)
KPART1 = (0, 1, 2, 0, 1, 0)
LAMBDA_INIT = 0.8 - 0.6 * 2.718281828459045 ** (-0.3)


def stage_masks(nc, d, ident, identb, negmask):
    with Stage(nc, "masks") as st:
        m = st.sb("m", [P, 2, P])
        ones = st.sb("ones", [P, S], BF16)
        loaded, ready, stored = st.sem("loaded"), st.sem("ready"), st.sem("stored")
        block = st.block()

        @block.sync
        def _(sp):
            sp.dma_start(m[:], d["negmask"]).then_inc(loaded, 16)
            sp.wait_ge(ready, 1)
            sp.dma_start(d["ones1"], ones[0:1, :]).then_inc(stored, 16)
            for h in range(2):
                sp.dma_start(d["k1"][:, :, B * NK1 + h, :].rearrange("v e s -> (v e) s"), ones[0:3 * HD, :]
                             ).then_inc(stored, 16)
            sp.dma_start(d["m1pad"], ones[0:2 * QPK, :]).then_inc(stored, 16)
            for h in range(2 * QPK):
                sp.dma_start(d["q1"][:, :, B * NQ1 + h, :].rearrange("v e s -> (v e) s"), ones[0:3 * HD, :]
                             ).then_inc(stored, 16)
            sp.wait_ge(stored, 16 * (4 + 2 * QPK))

        @block.vector
        def _(dve):
            dve.memset(ones[:], 1.0).then_inc(ready, 1)
            dve.tensor_copy(identb[:], ident[:])
            dve.wait_ge(loaded, 16)
            dve.tensor_copy(negmask[:], m[:])


def stage_project1(nc, d, xnT, vaug):
    with Stage(nc, "proj1") as st:
        w = st.sb("w", [P, 2 * D + 2 * NK1 * HD])
        parts = st.sb("parts", [P, 3, 3, T], BF16)
        r0, r1, r2 = st.sb("r0", [P, 3, T]), st.sb("r1", [P, T]), st.sb("r2", [P, T])
        vtok = st.sb("vtok", [P, NT, NK1 * HD])
        ps = st.ps("ps", [P, 6, CH])
        pv = st.ps("pv", [P, 2, CH])
        loaded, mm_done, copied, chain = st.sem("loaded"), st.sem("mm_done"), st.sem("copied"), st.sem("chain")
        v_mm, split_done, stored, mm_used = st.sem("v_mm"), st.sem("split_done"), st.sem("stored"), st.sem("mm_used")
        v_ready, v_stored, v_loaded, ones_ready = (st.sem("v_ready"), st.sem("v_stored"), st.sem("v_loaded"),
                                                   st.sem("ones_ready"))
        block = st.block()
        NV = NK1 * HD

        def store_q(eng, ct, groups, signal):
            for part in range(3):
                for c in groups:
                    dst = d["q1"][part, :, 0:B * NQ1, (16 * ct + c) * 32:(16 * ct + c + 1) * 32]
                    eng.dma_start(dst, parts[c * HD:(c + 1) * HD, ct, part, :].rearrange("p (h t) -> p h t", t=32)
                                  ).then_inc(signal, 16)
            return 3 * len(groups)

        def store_k(eng, groups, signal):
            for part in range(3):
                for c in groups:
                    dst = d["k1"][part, :, 0:B * NK1, :].rearrange("e h (j c t) -> c e (h j) t", c=8, t=16)[c]
                    eng.dma_start(dst, parts[c * HD:(c + 1) * HD, 2, part, :].rearrange("p (j t) -> p j t", t=16)
                                  ).then_inc(signal, 16)
            return 3 * len(groups)

        @block.sync
        def _(sp):
            sp.dma_start(w[:], d["wqkv1"]).then_inc(loaded, 16)
            sp.wait_ge(v_ready, 2)
            sp.dma_start(d["v1"].rearrange("(n p) c -> p n c", p=P), vtok[:]).then_inc(v_stored, 16)
            sp.wait_ge(v_stored, 16)
            sp.wait_ge(ones_ready, 1)
            for c in range(8):
                sp.dma_start(vaug[16 * c:16 * c + 16, :, 0:HD],
                             d["v1"][:, c * HD:(c + 1) * HD].rearrange("(j t) e -> t j e", t=16)).then_inc(v_loaded, 16)
            sp.wait_ge(v_loaded, 16 * 8)
            n = 0
            for ct in range(2):
                sp.wait_ge(split_done, ct + 1)
                n += store_q(sp, ct, range(0, 8), stored)
            sp.wait_ge(split_done, 3)
            n += store_k(sp, range(0, 4), stored)
            sp.wait_ge(stored, 16 * n)

        @block.tensor
        def _(pe):
            pe.wait_ge(loaded, 16)
            for n in range(NT):
                mm = pe.matmul(pv[:, n // 8, (n % 8) * NV:(n % 8 + 1) * NV], xnT[:, n * P:(n + 1) * P],
                               w[:, 2 * D + NV:2 * D + 2 * NV], start=True, stop=True)
                if n % 8 == 7:
                    mm.then_inc(v_mm, 1)
            k = 0
            for j, (lo, hi) in enumerate(((0, D), (D, 2 * D), (2 * D, 2 * D + NV))):
                for c in range(NC):
                    if k >= 6:
                        pe.wait_ge(mm_used, k - 5)
                    pe.matmul(ps[0:hi - lo, k % 6, :], w[:, lo:hi], xnT[:, c * CH:(c + 1) * CH],
                              start=True, stop=True).then_inc(mm_done, 1)
                    k += 1

        @block.scalar
        def _(act):
            for c in range(2):
                act.wait_ge(v_mm, c + 1)
                act.copy(vtok[:, 8 * c:8 * c + 8, :].rearrange("p a b -> p (a b)"), pv[:, c, :]).then_inc(v_ready, 1)
            k = 0
            for j, rows in enumerate((P, P, NV)):
                for c in range(NC):
                    act.wait_ge(mm_done, k + 1)
                    act.copy(r0[0:rows, j, c * CH:(c + 1) * CH], ps[0:rows, k % 6, :]).then_inc(mm_used, 1)
                    k += 1
            n = 0
            for ct in range(2):
                act.wait_ge(split_done, ct + 1)
                n += store_q(act, ct, range(8, 16), copied)
            act.wait_ge(split_done, 3)
            n += store_k(act, range(4, 8), copied)
            act.wait_ge(copied, 16 * n)

        @block.vector
        def _(dve):
            link = Chain(dve, chain)
            dve.memset(vaug[:], 1.0).then_inc(ones_ready, 1)
            for j, rows in enumerate((P, P, NV)):
                dve.wait_ge(mm_used, NC * (j + 1))
                split_parts(link, dve, r0[0:rows, j, :], parts[0:rows, j, 0, :], parts[0:rows, j, 1, :],
                            parts[0:rows, j, 2, :], r1[0:rows, :], r2[0:rows, :])
                dve.sem_inc(split_done, 1)


NLOADS = 3 + 4


def load_packed(eng, dst, src, parts, signal):
    blk = n = 0
    while blk < NPACK:
        end = blk + 1
        while end < NPACK and parts[end] == parts[end - 1] + 1:
            end += 1
        rows = dst[blk * HD:end * HD]
        eng.dma_start(rows, src[parts[blk]:parts[blk] + end - blk]).then_inc(signal, 16)
        blk, n = end, n + 1
    return n


def stage_max1(nc, d, ident, identb, negmask):
    NKH, NH = B * NK1, B * NQ1
    with Stage(nc, "max1") as st:
        qh = st.sb("qh", [P, 2, QPK, S], BF16)
        qt = st.sb("qt", [P, 2, QPK, ST, P], BF16)
        kh = st.sb("kh", [P, 2, S], BF16)
        mcol = st.sb("mcol", [P, ST, NH])
        mrow = st.sb("mrow", [NH, S], BF16)
        ps = st.ps("ps", [P, 4, 2 * CH])
        loaded = [st.sem("loaded0"), st.sem("loaded1")]
        zeroed, scored, maxed = st.sem("zeroed"), st.sem("scored"), st.sem("maxed")
        head_used, rows, rows_out, stored = st.sem("head_used"), st.sem("rows"), st.sem("rows_out"), st.sem("stored")
        q_turned = st.sem("q_turned")
        turning = st.sem("turning")
        block = st.block()

        @block.sync
        def _(sp):
            def load(kv, slot):
                n = load_packed(sp, kh[:, slot, :], d["k1"][:, :, kv, :], KPART1, loaded[slot])
                n += load_packed(sp, qh[:, slot], d["q1"][:, :, bass.ds(kv * QPK, QPK), :], QPART1, loaded[slot])
                assert n == NLOADS, n

            sp.wait_ge(zeroed, 1)
            load(0, 0)
            load(1, 1)
            with sp.Fori(0, NKH // 2 - 1) as i:
                for s in range(2):
                    sp.wait_ge(head_used, 2 * i + s + 3)
                    load(2 * i + 2 + s, s)
            sp.wait_ge(rows_out, ST)
            sp.dma_start(d["m1"], mrow[:]).then_inc(stored, 16)
            sp.wait_ge(stored, 16)

        @block.gpsimd
        def _(pool):
            pool.memset(qh[:], 0.0)
            pool.memset(kh[:], 0.0).then_inc(zeroed, 1)
            pool.sem_inc(head_used, 2)
            with pool.Fori(0, NKH // 2) as i:
                for s in range(2):
                    pool.wait_ge(loaded[s], 16 * NLOADS * (i + 1))
                    pool.wait_ge(head_used, 2 * i + s + 1)
                    pool.sem_inc(turning, 1)
                    for h in range(QPK):
                        pool.tensor_copy(qt[:, s, h, :, :].rearrange("p u (c t) -> p u c t", t=4),
                                         qh[:, s, h, :].rearrange("p (c u t) -> p u c t", c=32, t=4)
                                         ).then_inc(q_turned, 1)

        @block.tensor
        def _(pe):
            with pe.Fori(0, NKH // 2) as i:
                for s in range(2):
                    for h in range(QPK):
                        pe.wait_ge(q_turned, (2 * i + s) * QPK + h + 1)
                        for u in range(ST):
                            pe.wait_ge(maxed, ((2 * i + s) * QPK + h) * ST + u + 1)
                            queries = qt[:, s, h, u, :]
                            for lo in range(0, (u + 1) * P, CH):
                                hi = min(lo + CH, (u + 1) * P)
                                last = hi == (u + 1) * P
                                pe.matmul(ps[:, u % 4, lo:hi], queries, kh[:, s, lo:hi], start=True, stop=not last)
                            pe.matmul(ps[:, u % 4, u * P:(u + 1) * P], identb[:], negmask[:, 1, :], start=False,
                                      stop=True).then_inc(scored, 1)
            pe.wait_ge(maxed, NH * ST + 4)
            for u in range(ST):
                pe.transpose(ps[0:NH, u // 4, (u % 4) * P:(u % 4 + 1) * P], mcol[:, u, :], ident[:]).then_inc(rows, 1)

        @block.scalar
        def _(act):
            for u in range(ST):
                act.wait_ge(rows, ST)
                act.mul(mrow[:].rearrange("p (c t) -> p c t", t=32)[:, :, 4 * u:4 * u + 4],
                        ps[0:NH, u // 4, (u % 4) * P:(u % 4 + 1) * P].rearrange("p (c t) -> p c t", t=4),
                        -1.0).then_inc(rows_out, 1)

        @block.vector
        def _(dve):
            dve.sem_inc(maxed, 4)
            with dve.Fori(0, NKH // 2) as i:
                for s in range(2):
                    for h in range(QPK):
                        for u in range(ST):
                            dve.wait_ge(scored, ((2 * i + s) * QPK + h) * ST + u + 1)
                            dve.tensor_reduce(mcol[:, u, bass.ds((2 * i + s) * QPK + h, 1)],
                                              ps[:, u % 4, 0:(u + 1) * P], AX.X, ALU.max).then_inc(maxed, 1)
                    dve.sem_inc(head_used, 1)


def stage_attend1(nc, d, vaug, identb, negmask):
    NKH, NH = B * NK1, B * NQ1
    with Stage(nc, "att1") as st:
        qh = st.sb("qh", [P, 2, QPK, S], BF16)
        kh = st.sb("kh", [P, 2, S], BF16)
        pr = st.sb("pr", [P, 4, 2, CH])
        vh = st.sb("vh", [P, 2, ST, VW])
        ob = st.sb("ob", [P, 2, CH])
        ps = st.ps("ps", [P, 8, CH])
        loaded = [st.sem("loaded0"), st.sem("loaded1")]
        stored = [st.sem("stored0"), st.sem("stored1")]
        zeroed, qk_done, exp_done, pv_done = st.sem("zeroed"), st.sem("qk_done"), st.sem("exp_done"), st.sem("pv_done")
        out_copied, v_copied, chain = st.sem("out_copied"), st.sem("v_copied"), st.sem("chain")
        block = st.block()

        @block.sync
        def _(sp):
            def load(kv, slot):
                n = load_packed(sp, kh[:, slot, :], d["k1"][:, :, kv, :], KPART1, loaded[slot])
                sp.dma_start(kh[KROWS:KROWS + 1, slot, :], d["ones1"]).then_inc(loaded[slot], 16)
                n += load_packed(sp, qh[:, slot], d["q1"][:, :, bass.ds(kv * QPK, QPK), :], QPART1, loaded[slot])
                sp.dma_start(qh[KROWS:KROWS + 1, slot, :, :],
                             d["m1all"][bass.ds(kv * QPK, QPK), :].rearrange("(o h) s -> o h s", o=1)
                             ).then_inc(loaded[slot], 16)
                assert n == NLOADS, n

            def store(row, slot):
                for quad in range(4):
                    sp.dma_start(d["o1"][row, quad // 2, :, (quad % 2) * CH:(quad % 2 + 1) * CH],
                                 ob[32 * quad:32 * quad + HD + 1, slot, :]).then_inc(stored[slot], 16)

            sp.wait_ge(zeroed, 1)
            load(0, 0)
            load(1, 1)
            with sp.Fori(0, NKH // 2) as i:
                for s in range(2):
                    for h in range(QPK):
                        bh = (2 * i + s) * QPK + h
                        sp.wait_ge(out_copied, bh + 3)
                        store(bh, 1 - h % 2)
                    sp.wait_ge(qk_done, (2 * i + s + 1) * QPK * ST + 1)
                    load(2 * i + 2 + s, s)
            sp.wait_ge(out_copied, NH + 3)
            store(NH, 1)
            for s in range(2):
                sp.wait_ge(stored[s], 16 + 64 * (NH // 2 + s))
                sp.wait_ge(loaded[s], 16 * (NLOADS + 2) * (NKH // 2 + 1))

        @block.gpsimd
        def _(pool):
            pool.memset(qh[:], 0.0)
            pool.memset(kh[:], 0.0)
            pool.memset(pr[:], 0.0)
            pool.memset(vh[:], 0.0).then_inc(zeroed, 1)
            pool.wait_ge(zeroed, 1)
            with pool.Fori(0, NKH // 2) as i:
                for s in range(2):
                    kv = 2 * i + s
                    pool.wait_ge(pv_done, kv * QPK * (ST // 2) + 1)
                    pool.tensor_copy(vh[:, s, :, 0:HD + 1], vaug[:, bass.ds(kv * ST, ST), :]).then_inc(v_copied, 1)

        @block.tensor
        def _(pe):
            def from_tile(ap, J):
                return ap.rearrange("p (c t) -> p c t", t=32)[:, :, 4 * J:32]

            def qk(slot, h, J, n):
                pe.wait_ge(exp_done, n + 1)
                for c in range(2):
                    bank = ps[:, 2 * (J % 2) + c, :]
                    pe.matmul(from_tile(bank, J), kh[:, slot, J * P:(J + 1) * P],
                              from_tile(qh[:, slot, h, c * CH:(c + 1) * CH], J), start=True, stop=False)
                    mm = pe.matmul(bank.rearrange("p (c t) -> p c t", t=32)[:, :, 4 * J:4 * J + 4], identb[:],
                                   negmask[:, 0, c * 64:(c + 1) * 64], start=False, stop=True)
                mm.then_inc(qk_done, 1)

            def pv(slot, acc, m, n):
                pe.wait_ge(exp_done, n + 3)
                for J in (2 * m, 2 * m + 1):
                    for c in range(2):
                        quad = 32 * (2 * (J % 2) + c)
                        first = 0 if J < 2 else J
                        mm = pe.matmul(from_tile(ps[quad:quad + VW, 6 + acc, :], first), vh[:, slot, J, :],
                                       from_tile(pr[:, J % 4, c, :], first), start=(m == 0),
                                       stop=(m == ST // 2 - 1), skip_group_check=True, tile_position=(0, quad))
                mm.then_inc(pv_done, 1)

            pe.sem_inc(qk_done, 1)
            pe.wait_ge(zeroed, 1)
            pe.wait_ge(out_copied, 2)
            with pe.Fori(0, NKH // 2) as i:
                for s in range(2):
                    pe.wait_ge(loaded[s], 16 * (NLOADS + 2) * (i + 1))
                    for h in range(QPK):
                        bh = (2 * i + s) * QPK + h
                        for m in range(ST // 2):
                            n = bh * ST + 2 * m
                            qk(s, h, 2 * m, n)
                            qk(s, h, 2 * m + 1, n + 1)
                            if m == 0:
                                pv(s if h else 1 - s, 1 - h % 2, ST // 2 - 1, n - 1)
                                if h == 0:
                                    pe.wait_ge(v_copied, 2 * i + s + 1)
                                pe.wait_ge(out_copied, bh + 2)
                            else:
                                pv(s, h % 2, m - 1, n - 1)
            pv(1, 1, ST // 2 - 1, NH * ST - 1)

        @block.scalar
        def _(act):
            act.sem_inc(exp_done, 2)
            act.wait_ge(zeroed, 1)
            with act.Fori(0, NH // 2) as i:
                for s in range(2):
                    bh = 2 * i + s
                    for J in range(ST):
                        act.wait_ge(qk_done, bh * ST + J + 2)
                        act.wait_ge(pv_done, bh * (ST // 2) + J // 2 + 4)
                        act.activation(
                            pr[:, J % 4, :, :].rearrange("p b (c t) -> p (b c) t", t=32)[:, :, 4 * J:32],
                            ps[:, 2 * (J % 2):2 * (J % 2) + 2, :].rearrange("p b (c t) -> p (b c) t",
                                                                            t=32)[:, :, 4 * J:32],
                            ACT.Exp, scale=SCALE).then_inc(exp_done, 1)

        @block.vector
        def _(dve):
            link = Chain(dve, chain)
            dve.sem_inc(pv_done, 4)
            dve.sem_inc(stored[0], 16)
            dve.sem_inc(stored[1], 16)
            link(dve.memset(ps[:, 6:8, :], 0.0))
            dve.sem_inc(out_copied, 2)

            def copy_out(slot, bh_done, rounds):
                dve.wait_ge(pv_done, bh_done * (ST // 2) + 5)
                dve.wait_ge(stored[slot], rounds)
                dve.tensor_copy(ob[:, slot, :], ps[:, 6 + slot, :]).then_inc(out_copied, 1)

            with dve.Fori(0, NH // 2) as i:
                for s in range(2):
                    copy_out(1 - s, 2 * i + s, 16 + 64 * i)
            copy_out(1, NH, 16 + 64 * (NH // 2))


def stage_combine1(nc, d, sT):
    with Stage(nc, "comb1") as st:
        num = [st.sb(f"num{j}", [P, 2, T]) for j in range(2)]
        den = [st.sb(f"den{j}", [P, 2, T]) for j in range(2)]
        wp = st.sb("wp", [P, D])
        lam, lsum = st.sb("lam", [P, 4, NK1 * HD]), st.sb("lsum", [P, 4])
        newT = st.sb("newT", [P, B, D, ST])
        ps = st.ps("ps", [P, 4, CH])
        ps2 = st.ps("ps2", [P, 4, CH])
        weights, chain, mixed, y_done, y_copied = (st.sem("weights"), st.sem("chain"), st.sem("mixed"),
                                                   st.sem("y_done"), st.sem("y_copied"))
        sums = [st.sem("sums0"), st.sem("sums1")]
        lam_sum, lam_exp, projected = st.sem("lam_sum"), st.sem("lam_exp"), st.sem("projected")
        block = st.block()

        @block.sync
        def _(sp):
            sp.dma_start(wp[:], d["wproj"]).then_inc(weights, 16)
            for j in range(4):
                sp.dma_start(lam[:, j, :], d["lam"][j].partition_broadcast(P)).then_inc(weights, 16)
            for j in range(2):
                for quad in range(2):
                    for b in range(B):
                        rows = d["o1"][1 + b * NQ1:1 + (b + 1) * NQ1].rearrange("(n j) v r s -> j v n r s", j=2)[j, quad]
                        sp.dma_start(num[j][:, quad, b * S:(b + 1) * S], rows[:, 0:HD, :]).then_inc(sums[j], 16)
                        sp.dma_start(den[j][:, quad, b * S:(b + 1) * S],
                                     rows[:, HD:HD + 1, :].broadcast_to((NQ1 // 2, HD, S))).then_inc(sums[j], 16)

        @block.scalar
        def _(act):
            act.wait_ge(lam_sum, 1)
            act.activation(lsum[:, 0:2], lsum[:, 0:2], ACT.Exp).then_inc(lam_exp, 1)
            for c in range(NC):
                act.wait_ge(projected, c + 1)
                act.copy(sT[:, c * CH:(c + 1) * CH], ps2[:, c, :])

        @block.tensor
        def _(pe):
            pe.wait_ge(weights, 16 * 5)
            pe.wait_ge(mixed, 1)
            for b in range(B):
                for t in range(ST):
                    rows = num[1][:, 0, b * S + t * P:b * S + (t + 1) * P]
                    mm = pe.matmul(ps[:, 2 * b + t // 4, (t % 4) * P:(t % 4 + 1) * P], rows, wp[:],
                                   start=True, stop=True)
                    if t % 4 == 3:
                        mm.then_inc(y_done, 1)
            for c in range(NC):
                pe.wait_ge(y_copied, 2 * (c // 2) + 2)
                pe.matmul(ps2[:, c, :], wp[:],
                          newT[:, c // 2, :, :].rearrange("p c t -> p (c t)")[:, (c % 2) * CH:(c % 2 + 1) * CH],
                          start=True, stop=True).then_inc(projected, 1)

        @block.vector
        def _(dve):
            link = Chain(dve, chain)
            dve.wait_ge(weights, 16 * 5)
            for j in range(2):
                link(dve.tensor_tensor(lam[:, 2 * j, :], lam[:, 2 * j, :], lam[:, 2 * j + 1, :], ALU.mult))
                link(dve.tensor_reduce(lsum[:, j:j + 1], lam[:, 2 * j, :], AX.X, ALU.add))
            dve.sem_inc(lam_sum, 1)
            dve.wait_ge(lam_exp, 1)
            link(dve.tensor_tensor(lsum[:, 2:3], lsum[:, 1:2], lsum[:, 0:1], ALU.subtract))
            link(dve.tensor_scalar(lsum[:, 3:4], lsum[:, 2:3], -LAMBDA_INIT, None, ALU.add))
            for j in range(2):
                dve.wait_ge(sums[j], 16 * 8)
                for x in (num[j], den[j]):
                    link(dve.tensor_tensor(x[:, 0, :], x[:, 0, :], x[:, 1, :], ALU.add))
                link(dve.reciprocal(den[j][:, 0, :], den[j][:, 0, :]))
                link(dve.tensor_tensor(num[j][:, 0, :], num[j][:, 0, :], den[j][:, 0, :], ALU.mult))
            link(dve.scalar_tensor_tensor(num[0][:, 0, :], num[1][:, 0, :], lsum[:, 3:4], num[0][:, 0, :],
                                          ALU.mult, ALU.add))
            dve.tensor_scalar(num[1][:, 0, :].rearrange("p (b t c) -> p b c t", b=B, c=32),
                              num[0][:, 0, :].rearrange("p (b c t) -> p b c t", b=B, c=32), 1.0 - LAMBDA_INIT,
                              None, ALU.mult).then_inc(mixed, 1)
            for k in range(4):
                dve.wait_ge(y_done, k + 1)
                b, t0 = k // 2, 4 * (k % 2)
                dve.tensor_copy(newT[:, b, :, t0:t0 + 4], ps[:, k, :].rearrange("p (t c) -> p c t", c=P)
                                ).then_inc(y_copied, 1)


DEPTH = 6
NHP = 8
DH = 64
WIN = 32
QW = P + WIN
GI = 341
GT = (P, P, GI - 2 * P)
QK_SCALE = 8.0
NU = 2 * NHP
C_Q, C_K, C_G, C_B, C_B2, C_A, C_GATE, NCOL = 0, 1, 2, 3, 4, 5, 8, 11


def stage_transformer(nc, d, ident, identb, yT):
    with Stage(nc, "tr") as st:
        xs = st.sb("xs", [P, B, S])
        w3 = st.sb("w3", [P, 2, 3, P])
        wo = st.sb("wo", [P, NHP, P])
        w1 = st.sb("w1", [P, 2 * GI])
        w2 = st.sb("w2", [P, 3, P])
        cols_all = st.sb("cols_all", [P, DEPTH, NCOL])
        col = st.sb("col", [P, NCOL])
        rope = st.sb("rope", [P, 4, S])
        blk = st.sb("blk", [P, P])
        mean = st.sb("mean", [P, P])
        ones = st.sb("ones", [P, DH])
        eps = st.sb("eps", [P, 1])
        ln256 = st.sb("ln256", [P, 1])
        band = st.sb("band", [P, 3, QW], BF16)
        sq = st.sb("sq", [P, 4, CH])
        t12 = st.sb("t12", [P, 4, 2, CH])
        rn = st.sb("rn", [P, 4, CH])
        qn = st.sb("qn", [P, 2, S])
        kz = st.sb("kz", [P, 2, 2, S])
        v = st.sb("v", [P, 2, ST, P])
        pr = st.sb("pr", [P, 2, 2, ST * QW + QW])
        rden = st.sb("rden", [P, 2, CH])
        o = st.sb("o", [P, NHP, T])
        ps = st.ps("ps", [P, 8, CH])
        S_ = st.sem
        loaded_const, const_ready, chain = S_("loaded_const"), S_("const_ready"), S_("chain")
        w_loaded = [S_("w_loaded0"), S_("w_loaded1")]
        layer_loaded, xs_ready, pchain = S_("layer_loaded"), S_("xs_ready"), S_("pchain")
        proj_done, sq_done, rope_done, v_copied = S_("proj_done"), S_("sq_done"), S_("rope_done"), S_("v_copied")
        ss_done, clamp_done, log_done, recip_done, qk_ready = (S_("ss_done"), S_("clamp_done"), S_("log_done"),
                                                               S_("recip_done"), S_("qk_ready"))
        scores_done, exp_done, pv_done, out_done = S_("scores_done"), S_("exp_done"), S_("pv_done"), S_("out_done")
        drained = S_("drained")
        wo_done, x_added, xs2_ready = S_("wo_done"), S_("x_added"), S_("xs2_ready")
        mean_done, centered, square_done, var_done = S_("mean_done"), S_("centered"), S_("square_done"), S_("var_done")
        rstd_log_done, rstd_done, normed = S_("rstd_log_done"), S_("rstd_done"), S_("normed")
        up_done, gelu_done, h_ready = S_("up_done"), S_("gelu_done"), S_("h_ready")
        col_ready, pool_chain, fchain = S_("col_ready"), S_("pool_chain"), S_("fchain")
        down_done, layer_done = S_("down_done"), S_("layer_done")
        block = st.block()

        def bank(b, c, j):
            return (10 * b + 5 * c + j) % 4

        @block.sync
        def _(sp):
            sp.dma_start(rope[:], d["rope"]).then_inc(loaded_const, 16)
            sp.dma_start(blk[:], d["blk64"]).then_inc(loaded_const, 16)
            sp.dma_start(cols_all[:], d["col"].rearrange("l p a -> p l a")).then_inc(loaded_const, 16)
            sp.dma_start(t12[:, 0, 0, 0:3 * QW], d["band"]).then_inc(loaded_const, 16)

            def load_w(hp, slot):
                sp.dma_start(w3[:, slot, :, :], d["w3"][bass.ds(hp, 1)].rearrange("o p a b -> p (o a) b")
                             ).then_inc(w_loaded[slot], 16)

            for slot in range(2):
                load_w(slot, slot)
            with sp.Fori(0, DEPTH) as L:
                sp.wait_ge(xs_ready, NC * L + NC)
                sp.dma_start(wo[:], d["wo6"][bass.ds(L, 1)].rearrange("o p a b -> (o p) a b")
                             ).then_inc(layer_loaded, 16)
                sp.dma_start(w1[:], d["w1"][bass.ds(L, 1)].rearrange("o p a -> (o p) a")).then_inc(layer_loaded, 16)
                sp.dma_start(w2[:], d["w2"][bass.ds(L, 1)].rearrange("o p a b -> (o p) a b")
                             ).then_inc(layer_loaded, 16)
                with sp.Fori(0, NHP // 2) as i:
                    for s in range(2):
                        sp.wait_ge(proj_done, 6 * (L * NU + 4 * i + 2 * s + 2))
                        load_w(L * NHP + 2 * i + 2 + s, s)
            for slot in range(2):
                sp.wait_ge(w_loaded[slot], 64 * DEPTH + 16)

        @block.tensor
        def _(pe):
            def project(n, slot, b, c):
                cols = xs[:, b, c * CH:(c + 1) * CH]
                frees = ((rope_done, 4 * n + 2 * c + 2), (v_copied, 2 * n + c + 2), (clamp_done, 4 * n + 2 * c + 3))
                for j in range(2):
                    pe.wait_ge(*frees[j])
                    pe.matmul(ps[:, bank(b, c, j), :], w3[:, slot, j, :], cols, start=True,
                              stop=True).then_inc(proj_done, 1)
                pe.wait_ge(*frees[2])
                for t in range(4):
                    mm = pe.matmul(ps[:, bank(b, c, 2), t * P:(t + 1) * P],
                                   xs[:, b, c * CH + t * P:c * CH + (t + 1) * P], w3[:, slot, 2, :],
                                   start=True, stop=True)
                mm.then_inc(proj_done, 1)

            def norms(n, b, c):
                frees = ((clamp_done, 4 * n + 2 * c + 4), (rope_done, 4 * n + 2 * c + 3))
                for isk in range(2):
                    pe.wait_ge(*frees[isk])
                    pe.wait_ge(sq_done, 4 * n + 2 * c + isk + 1)
                    pe.matmul(ps[:, bank(b, c, 3 + isk), :], blk[:], sq[:, 2 * c + isk, :], start=True,
                              stop=True).then_inc(ss_done, 1)

            def scores(n, b, k):
                e, J0 = k % 2, 3 * (k // 2)
                pe.wait_ge(exp_done, 6 * n + k + 1)
                pe.matmul(ps[:, 4 + k % 2, 0:3 * QW], identb[:], band[:].rearrange("p a b -> p (a b)"), start=True,
                          stop=True)
                for J in range(J0, min(J0 + 3, ST)):
                    width = min(QW, S - J * P)
                    mm = pe.matmul(ps[:, 4 + k % 2, (J - J0) * QW:(J - J0) * QW + width],
                                   kz[:, b, e, J * P:(J + 1) * P], qn[:, b, J * P:J * P + width],
                                   start=False, stop=True, skip_group_check=True)
                mm.then_inc(scores_done, 1)

            def sums(n, b, c):
                pe.wait_ge(exp_done, 6 * n + (6, 8)[c])
                pe.wait_ge(drained, 2 * n + c + 1)
                for I in range(4 * c, 4 * c + 4):
                    out = slice((I - 4 * c) * P, (I - 4 * c + 1) * P)
                    tail = slice((I - 4 * c) * P, (I - 4 * c) * P + WIN)
                    for what in range(2):
                        for e in range(2):
                            lhs = v[:, b, I, e * DH:(e + 1) * DH] if what == 0 else ones[:]
                            pe.matmul(ps[e * DH:(e + 1) * DH, 6 + what, out], lhs,
                                      pr[:, b, e, I * QW:I * QW + P], start=True, stop=True,
                                      tile_position=(0, e * DH), skip_group_check=True)
                    if I:
                        for what in range(2):
                            for e in range(2):
                                lhs = v[:, b, I - 1, e * DH:(e + 1) * DH] if what == 0 else ones[:]
                                mm = pe.matmul(ps[e * DH:(e + 1) * DH, 6 + what, tail], lhs,
                                               pr[:, b, e, (I - 1) * QW + P:I * QW], start=False, stop=True,
                                               tile_position=(0, e * DH), skip_group_check=True)
                mm.then_inc(pv_done, 1)

            def out_proj(L, c):
                for hp in range(NHP):
                    mm = pe.matmul(ps[:, c, :], wo[:, hp, :], o[:, hp, c * CH:(c + 1) * CH],
                                   start=(hp == 0), stop=(hp == NHP - 1))
                mm.then_inc(wo_done, 1)

            def step(n, b, slot, L=None):
                last = slot[0] is None
                if last:
                    pe.wait_ge(layer_loaded, 48 * L + 48)
                pe.wait_ge(qk_ready, 4 * n + 6)
                scores(n, b, 0)
                scores(n, b, 1)
                if last:
                    pe.wait_ge(out_done, 2 * n + 2)
                    pe.wait_ge(v_copied, 2 * n + 4)
                    pe.wait_ge(clamp_done, 4 * n + 8)
                    out_proj(L, 0)
                else:
                    norms(n + 1, 1 - b, 0)
                    project(n + 1, slot[0], 1 - b, 1)
                pe.wait_ge(qk_ready, 4 * n + 8)
                for k in range(2, 6):
                    scores(n, b, k)
                pe.wait_ge(v_copied, 2 * n + 4)
                sums(n, b, 0)
                if last:
                    out_proj(L, 1)
                else:
                    norms(n + 1, 1 - b, 1)
                if slot[1] is not None:
                    project(n + 2, slot[1], b, 0)
                sums(n, b, 1)

            def mean_of(L, c):
                pe.wait_ge(xs2_ready, NC * L + c + 1)
                pe.matmul(ps[:, 4 + c, :], mean[:], xs[:, c // 2, (c % 2) * CH:(c % 2 + 1) * CH], start=True,
                          stop=True).then_inc(mean_done, 1)

            def variance(L, c):
                pe.wait_ge(square_done, NC * L + c + 1)
                pe.matmul(ps[:, c, :], mean[:], sq[:, c, :], start=True, stop=True).then_inc(var_done, 1)

            def up(L, c):
                pe.wait_ge(normed, NC * L + c + 1)
                for t in range(3):
                    if c == 0:
                        pe.wait_ge(rstd_log_done, NC * L + (2, 4, 4)[t])
                    else:
                        pe.wait_ge(h_ready, 3 * (NC * L + c - 1) + t + 1)
                    rows, lo = GT[t], t * P
                    for half in range(2):
                        mm = pe.matmul(ps[0:rows, 2 * t + half, :], w1[:, half * GI + lo:half * GI + lo + rows],
                                       o[:, 1, c * CH:(c + 1) * CH], start=True, stop=True)
                    mm.then_inc(up_done, 1)

            def down(L, c):
                pe.wait_ge(h_ready, 3 * (NC * L + c) + 3)
                for t in range(3):
                    mm = pe.matmul(ps[:, 6 + c % 2, :], w2[0:GT[t], t, :], t12[0:GT[t], t, c % 2, :], start=(t == 0),
                                   stop=(t == 2))
                mm.then_inc(down_done, 1)

            pe.wait_ge(const_ready, 2)
            pe.wait_ge(loaded_const, 64)
            with pe.Fori(0, DEPTH) as L:
                n0 = L * NU
                pe.wait_ge(w_loaded[0], 64 * L + 16)
                for c in range(2):
                    pe.wait_ge(xs_ready, NC * L + c + 1)
                    project(n0, 0, 0, c)
                    if c == 1:
                        pe.wait_ge(xs_ready, NC * L + NC)
                    norms(n0, 0, c)
                project(n0 + 1, 0, 1, 0)
                with pe.Fori(0, NHP // 2 - 1) as i:
                    n = n0 + 4 * i
                    pe.wait_ge(w_loaded[1], 64 * L + 16 * i + 16)
                    step(n, 0, (0, 1))
                    step(n + 1, 1, (1, 1))
                    pe.wait_ge(w_loaded[0], 64 * L + 16 * i + 32)
                    step(n + 2, 0, (1, 0))
                    step(n + 3, 1, (0, 0))
                n = n0 + NU - 4
                pe.wait_ge(w_loaded[1], 64 * L + 64)
                step(n, 0, (0, 1))
                step(n + 1, 1, (1, 1))
                step(n + 2, 0, (1, None))
                step(n + 3, 1, (None, None), L)
                pe.wait_ge(out_done, 2 * (n0 + NU) + 2)
                out_proj(L, 2)
                mean_of(L, 0)
                mean_of(L, 1)
                out_proj(L, 3)
                mean_of(L, 2)
                variance(L, 0)
                variance(L, 1)
                mean_of(L, 3)
                variance(L, 2)
                variance(L, 3)
                up(L, 0)
                for c in range(NC):
                    if c < NC - 1:
                        up(L, c + 1)
                    down(L, c)

        @block.scalar
        def _(act):
            def squares(n, b, c):
                for j in range(2):
                    idx = 2 * c + j
                    act.wait_ge(proj_done, 6 * n + 3 * c + j + 1)
                    act.wait_ge(ss_done, 4 * n + idx + 1)
                    act.activation(sq[:, idx, :], ps[:, bank(b, c, j), :], ACT.Square).then_inc(sq_done, 1)

            def copy_v(n, b, c):
                act.wait_ge(proj_done, 6 * n + 3 * c + 3)
                act.wait_ge(pv_done, 2 * n + 2)
                act.copy(v[:, b, 4 * c:4 * c + 4, :].rearrange("p a b -> p (a b)"),
                         ps[:, bank(b, c, 2), :]).then_inc(v_copied, 1)

            def roots(n, c):
                for j in range(2 * c, 2 * c + 2):
                    act.wait_ge(clamp_done, 4 * n + j + 5)
                    act.activation(rn[:, j, :], rn[:, j, :], ACT.Ln, scale=2.0 ** 16).then_inc(log_done, 1)
                for j in range(2 * c, 2 * c + 2):
                    act.wait_ge(log_done, 4 * n + j + 1)
                    act.activation(rn[:, j, :], rn[:, j, :], ACT.Exp, scale=-0.5, bias=ln256[:, 0:1]).then_inc(recip_done, 1)

            def exps(n, b, ks):
                for k in ks:
                    e, J0 = k % 2, 3 * (k // 2)
                    act.wait_ge(scores_done, 6 * n + k + 13)
                    act.wait_ge(pv_done, 2 * n + 2)
                    act.activation(pr[:, b, e, J0 * QW:(J0 + 3) * QW], ps[:, 4 + k % 2, 0:3 * QW], ACT.Exp,
                                   scale=QK_SCALE).then_inc(exp_done, 1)

            def step(n, hp, b, left):
                exps(n, b, (0, 1))
                if left:
                    squares(n + 1, 1 - b, 1)
                    roots(n + 1, 0)
                    copy_v(n + 1, 1 - b, 1)
                exps(n, b, (2, 3, 4, 5))
                drain(n, hp, b, 0)
                if left > 1:
                    squares(n + 2, b, 0)
                if left:
                    roots(n + 1, 1)
                drain(n, hp, b, 1)
                if left > 1:
                    copy_v(n + 2, b, 0)

            def drain(n, hp, b, c):
                act.wait_ge(pv_done, 2 * n + c + 5)
                act.wait_ge(out_done, 2 * n + c + 1)
                act.copy(rden[:, c, :], ps[:, 7, :])
                act.copy(o[:, hp, b * S + c * CH:b * S + (c + 1) * CH], ps[:, 6, :]).then_inc(drained, 1)

            def center_squares(L, cs):
                for c in cs:
                    act.wait_ge(centered, NC * L + c + 1)
                    act.activation(sq[:, c, :], o[:, 0, c * CH:(c + 1) * CH], ACT.Square).then_inc(square_done, 1)

            def rstd(L, c):
                act.wait_ge(var_done, NC * L + c + 1)
                act.activation(rn[:, c, :], ps[:, c, :], ACT.Ln, bias=eps[:, 0:1]).then_inc(rstd_log_done, 1)
                act.wait_ge(rstd_log_done, NC * L + c + 1)
                act.activation(rn[:, c, :], rn[:, c, :], ACT.Exp, scale=-0.5).then_inc(rstd_done, 1)

            act.sem_inc(v_copied, 2)
            act.sem_inc(exp_done, 2)
            act.wait_ge(const_ready, 2)
            with act.Fori(0, DEPTH) as L:
                n0 = L * NU
                act.preload_act_table_set("natural_log_exp_and_others")
                for c in range(2):
                    squares(n0, 0, c)
                    copy_v(n0, 0, c)
                    roots(n0, c)
                squares(n0 + 1, 1, 0)
                copy_v(n0 + 1, 1, 0)
                with act.Fori(0, NHP // 2 - 1) as i:
                    for u in range(4):
                        step(n0 + 4 * i + u, bass.ds(2 * i + u // 2, 1), u % 2, 4)
                for u in range(4):
                    step(n0 + NU - 4 + u, NHP - 2 + u // 2, u % 2, 3 - u)
                center_squares(L, (0, 1))
                rstd(L, 0)
                center_squares(L, (2,))
                rstd(L, 1)
                center_squares(L, (3,))
                rstd(L, 2)
                rstd(L, 3)
                for c in range(NC):
                    for t in range(3):
                        act.wait_ge(up_done, 3 * (NC * L + c) + t + 1)
                        rows = GT[t]
                        act.activation(o[0:rows, 2 + t, (c % 2) * CH:(c % 2 + 1) * CH], ps[0:rows, 2 * t + 1, :],
                                       ACT.Gelu, bias=col[0:rows, C_GATE + t:C_GATE + t + 1]).then_inc(gelu_done, 1)

        @block.vector
        def _(dve):
            link = Chain(dve, chain)

            def rotate(n, b, c):
                for isk in range(2):
                    idx = 2 * c + isk
                    cols = slice(c * CH, (c + 1) * CH)
                    dve.wait_ge(qk_ready, 4 * n + idx + 1)
                    dve.wait_ge(sq_done, 4 * n + idx + 1)
                    product = ps[:, bank(b, c, isk), :]
                    dve.scalar_tensor_tensor(t12[:, idx, 0, :], product, col[:, isk:isk + 1],
                                             rope[:, 2 * isk, cols], ALU.mult, ALU.mult)
                    for src, dst in ((slice(0, DH), slice(DH, P)), (slice(DH, P), slice(0, DH))):
                        ins = dve.scalar_tensor_tensor(t12[dst, idx, 1, :], product[src], col[src, isk:isk + 1],
                                                       rope[src, 2 * isk + 1, cols], ALU.mult, ALU.mult)
                    ins.then_inc(rope_done, 1)

            def clamps(n, b, c):
                for j in range(2 * c, 2 * c + 2):
                    dve.wait_ge(ss_done, 4 * n + j + 5)
                    dve.wait_ge(qk_ready, 4 * n + j + 1)
                    dve.tensor_scalar(rn[:, j, :], ps[:, bank(b, c, 3 + j % 2), :], 1e-24, None,
                                      ALU.max).then_inc(clamp_done, 1)

            def outputs(n, hp, b, c):
                dve.wait_ge(drained, 2 * n + c + 2)
                dve.reciprocal(rden[:, c, :], rden[:, c, :]).then_inc(pchain, 1)
                dve.wait_ge(pchain, 2 * n + c + 1)
                out = o[:, hp, b * S + c * CH:b * S + (c + 1) * CH]
                dve.tensor_tensor(out, out, rden[:, c, :], ALU.mult).then_inc(out_done, 1)

            def step(n, hp, b, left, before=None, L=None):
                if left:
                    clamps(n + 1, 1 - b, 0)
                    rotate(n + 1, 1 - b, 1)
                if before is not None:
                    outputs(n - 1, before, 1 - b, 1)
                if left:
                    clamps(n + 1, 1 - b, 1)
                if left > 1:
                    rotate(n + 2, b, 0)
                if not left:
                    add_attention(L, 0)
                    add_attention(L, 1)
                outputs(n, hp, b, 0)

            def shift(c, signal):
                b, lo = c // 2, (c % 2) * CH
                src = yT[:, b * S:(b + 1) * S]
                dve.tensor_copy(xs[0:64, b, lo:lo + CH], src[0:64, lo:lo + CH])
                first = 1 if lo == 0 else lo
                dve.tensor_copy(xs[64:P, b, first:lo + CH], src[64:P, first - 1:lo + CH - 1]).then_inc(signal, 1)

            def add_attention(L, c):
                dve.wait_ge(wo_done, NC * L + c + 1)
                cols = slice(c * CH, (c + 1) * CH)
                dve.tensor_tensor(yT[:, cols], yT[:, cols], ps[:, c, :], ALU.add).then_inc(x_added, 1)
                dve.wait_ge(x_added, NC * L + c + 1)
                shift(c, xs2_ready)

            def center(L, c):
                dve.wait_ge(mean_done, NC * L + c + 1)
                dve.wait_ge(xs2_ready, NC * L + c + 1)
                dve.tensor_tensor(o[:, 0, c * CH:(c + 1) * CH], xs[:, c // 2, (c % 2) * CH:(c % 2 + 1) * CH],
                                  ps[:, 4 + c, :], ALU.subtract).then_inc(centered, 1)

            def normalize(L, c):
                cols = slice(c * CH, (c + 1) * CH)
                dve.wait_ge(rstd_done, NC * L + c + 1)
                dve.wait_ge(centered, NC * L + c + 1)
                dve.tensor_tensor(o[:, 1, cols], o[:, 0, cols], rn[:, c, :], ALU.mult).then_inc(fchain, 1)
                dve.wait_ge(fchain, NC * L + c + 1)
                dve.tensor_scalar(o[:, 1, cols], o[:, 1, cols], col[:, C_G:C_G + 1], col[:, C_B:C_B + 1],
                                  ALU.mult, ALU.add).then_inc(normed, 1)

            def gate(L, c):
                for t in range(3):
                    dve.wait_ge(gelu_done, 3 * (NC * L + c) + t + 1)
                    rows = GT[t]
                    dve.scalar_tensor_tensor(t12[0:rows, t, c % 2, :], ps[0:rows, 2 * t, :],
                                             col[0:rows, C_A + t:C_A + t + 1],
                                             o[0:rows, 2 + t, (c % 2) * CH:(c % 2 + 1) * CH], ALU.add,
                                             ALU.mult).then_inc(h_ready, 1)

            def add_feed(L, c):
                cols = slice(c * CH, (c + 1) * CH)
                dve.wait_ge(down_done, NC * L + c + 1)
                dve.scalar_tensor_tensor(yT[:, cols], ps[:, 6 + c % 2, :], col[:, C_B2:C_B2 + 1], yT[:, cols],
                                         ALU.add, ALU.add).then_inc(layer_done, 1)
                dve.wait_ge(layer_done, NC * L + c + 1)
                shift(c, xs_ready)

            dve.sem_inc(qk_ready, 4)
            dve.sem_inc(ss_done, 4)
            dve.sem_inc(rope_done, 2)
            dve.sem_inc(clamp_done, 4)
            dve.sem_inc(pv_done, 4)
            dve.sem_inc(scores_done, 12)
            dve.sem_inc(out_done, 2)
            dve.sem_inc(drained, 1)
            dve.wait_ge(loaded_const, 64)
            link(dve.tensor_copy(band[:].rearrange("p a b -> p (a b)"), t12[:, 0, 0, 0:3 * QW]))
            dve.memset(xs[64:P, :, 0:1], 0.0)
            dve.memset(ones[:], 1.0)
            dve.memset(eps[:], LN_EPS)
            dve.memset(ln256[:], 8 * LN2)
            link(dve.memset(mean[:], 1.0 / D))
            dve.sem_inc(const_ready, 1)
            for c in range(NC):
                shift(c, xs_ready)
            with dve.Fori(0, DEPTH) as L:
                n0 = L * NU
                dve.tensor_copy(col[:], cols_all[:, bass.ds(L, 1), :].rearrange("p o a -> p (o a)")
                                ).then_inc(col_ready, 1)
                dve.wait_ge(col_ready, L + 1)
                for c in range(2):
                    rotate(n0, 0, c)
                    clamps(n0, 0, c)
                rotate(n0 + 1, 1, 0)
                step(n0, 0, 0, NU)
                with dve.Fori(0, NHP // 2 - 1) as i:
                    for u in range(1, 5):
                        step(n0 + 4 * i + u, bass.ds(2 * i + u // 2, 1), u % 2, NU,
                             before=bass.ds(2 * i + (u - 1) // 2, 1))
                for u in range(NU - 3, NU):
                    step(n0 + u, u // 2, u % 2, NU - 1 - u, before=(u - 1) // 2, L=L)
                outputs(n0 + NU - 1, NHP - 1, 1, 1)
                add_attention(L, 2)
                center(L, 0)
                add_attention(L, 3)
                for c in range(1, NC):
                    center(L, c)
                for c in range(NC):
                    normalize(L, c)
                gate(L, 0)
                for c in range(NC):
                    if c < NC - 1:
                        gate(L, c + 1)
                    add_feed(L, c)

        @block.gpsimd
        def _(pool):
            def combine(n, b):
                for j in range(4):
                    c, isk = j // 2, j % 2
                    cols = slice(c * CH, (c + 1) * CH)
                    pool.wait_ge(rope_done, 4 * n + j + 3)
                    step = 12 * n + 6 * c + (1 if isk else 0)
                    pool.tensor_tensor(t12[:, j, 0, :], t12[:, j, 0, :], t12[:, j, 1, :], ALU.add).then_inc(pool_chain, 1)
                    pool.wait_ge(pool_chain, step + 1)
                    pool.wait_ge(recip_done, 4 * n + j + 1)
                    pool.wait_ge(scores_done, 6 * n + 6)
                    if isk:
                        for k in range(4):
                            rows = slice(32 * k, 32 * k + 32)
                            pool.tensor_tensor(kz[rows, b, k % 2, cols], t12[rows, j, 0, :], rn[rows, j, :],
                                               ALU.mult).then_inc(pool_chain, 1)
                            pool.wait_ge(pool_chain, step + 2 + k)
                        pool.sem_inc(qk_ready, 1)
                    else:
                        pool.tensor_tensor(qn[:, b, cols], t12[:, j, 0, :], rn[:, j, :], ALU.mult).then_inc(qk_ready, 1)

            pool.memset(kz[:], 0.0)
            pool.memset(qn[:], 0.0)
            pool.memset(pr[:], 0.0).then_inc(const_ready, 1)
            pool.wait_ge(const_ready, 2)
            with pool.Fori(0, DEPTH * NU // 2) as i:
                for b in range(2):
                    combine(2 * i + b, b)


def build(nc, d):
    with ExitStack() as ctx:
        def scope():
            stack = ExitStack()
            return stack, lambda n, s, t=F32: stack.enter_context(nc.sbuf_tensor(n, s, t))

        sb = lambda n, s, t=F32: ctx.enter_context(nc.sbuf_tensor(n, s, t))
        ident = sb("ident", [P, P])
        xnT = sb("xnT", [P, T])
        outer, so = scope()
        with outer:
            xT, sT = so("xT", [P, T]), so("sT", [P, T])
            stage_norm(nc, "norm0", ident, xT, xnT, x_dram=d["x"], ident_dram=d["ident"])
            inner, si = scope()
            with inner:
                qT = si("qT", [P, T])
                relmax = si("relmax", [P, 2])
                vaug = si("vaug", [P, B * H0, ST, HD + 1])
                stage_project0(nc, d, xnT, qT, vaug, relmax)
                stage_max0(nc, d, ident, qT, relmax)
                stage_attend0(nc, d, vaug)
                stage_combine0(nc, d, qT, sT)
            stage_route(nc, d, xnT)
            stage_experts(nc, d, xnT, sT, xT)
            stage_norm(nc, "norm1", ident, xT, xnT)
            inner, si = scope()
            with inner:
                vaug1 = si("vaug1", [P, B * NK1 * ST, HD + 1])
                identb, negmask = si("identb", [P, P], BF16), si("negmask", [P, 2, P], BF16)
                stage_masks(nc, d, ident, identb, negmask)
                stage_project1(nc, d, xnT, vaug1)
                stage_max1(nc, d, ident, identb, negmask)
                stage_attend1(nc, d, vaug1, identb, negmask)
            stage_combine1(nc, d, sT)
            stage_stash(nc, d, xT, sT)
        inner, si = scope()
        with inner:
            identb = si("identb2", [P, P], BF16)
            stage_ident(nc, ident, identb)
            stage_transformer(nc, d, ident, identb, xnT)
        stage_final(nc, d, ident, xnT)


def stage_ident(nc, ident, identb):
    with Stage(nc, "ident") as st:
        block = st.block()

        @block.vector
        def _(dve):
            dve.tensor_copy(identb[:], ident[:])


def stage_stash(nc, d, xT, sT):
    with Stage(nc, "stash") as st:
        stored = st.sem("stored")
        block = st.block()

        @block.sync
        def _(sp):
            sp.dma_start(d["xs_stash"][0], xT[:]).then_inc(stored, 16)
            sp.dma_start(d["xs_stash"][1], sT[:]).then_inc(stored, 16)
            sp.wait_ge(stored, 32)


def stage_final(nc, d, ident, yT):
    with Stage(nc, "final") as st:
        xT, sT = st.sb("xT", [P, T]), st.sb("sT", [P, T])
        back = st.sem("back")
        g = st.sb("g", [P, T])
        x = st.sb("x", [P, NT, D])
        ps = st.ps("ps", [P, 4, CH])
        silu_done, chain, ready, turned, copied, stored = (st.sem("silu_done"), st.sem("chain"), st.sem("ready"),
                                                           st.sem("turned"), st.sem("copied"), st.sem("stored"))
        block = st.block()

        @block.scalar
        def _(act):
            for c in range(NC):
                cols = slice(c * CH, (c + 1) * CH)
                act.activation(g[:, cols], yT[:, cols], ACT.Silu).then_inc(silu_done, 1)
            for c in range(NC):
                act.wait_ge(turned, c + 1)
                act.copy(x[:, 4 * c:4 * c + 4, :].rearrange("p a b -> p (a b)"), ps[:, c, :]).then_inc(copied, 1)

        @block.vector
        def _(dve):
            link = Chain(dve, chain)
            dve.wait_ge(back, 32)
            for c in range(NC):
                cols = slice(c * CH, (c + 1) * CH)
                dve.wait_ge(silu_done, c + 1)
                link(dve.tensor_tensor(g[:, cols], g[:, cols], sT[:, cols], ALU.mult))
                dve.tensor_tensor(g[:, cols], g[:, cols], xT[:, cols], ALU.add).then_inc(ready, 1)

        @block.tensor
        def _(pe):
            for n in range(NT):
                if n % 4 == 0:
                    pe.wait_ge(ready, n // 4 + 1)
                mm = pe.transpose(ps[:, n // 4, (n % 4) * P:(n % 4 + 1) * P], g[:, n * P:(n + 1) * P], ident[:])
                if n % 4 == 3:
                    mm.then_inc(turned, 1)

        @block.sync
        def _(sp):
            sp.dma_start(xT[:], d["xs_stash"][0]).then_inc(back, 16)
            sp.dma_start(sT[:], d["xs_stash"][1]).then_inc(back, 16)
            out = d["out"].rearrange("(n p) d -> p n d", p=P)
            for c in range(NC):
                sp.wait_ge(copied, c + 1)
                sp.dma_start(out[:, 4 * c:4 * c + 4, :], x[:, 4 * c:4 * c + 4, :]).then_inc(stored, 16)
            sp.wait_ge(stored, 16 * NC)


def host_arrays(inputs):
    import numpy as np
    g = {k: np.asarray(v) for k, v in inputs.items()}
    c = np.ascontiguousarray
    a = {}
    a["x"] = g["L0_attn_hidden_states"].reshape(T, D)
    for n in "qkvo":
        a[f"w{n}T"] = c(g[f"L0_attn_W{n}"].T)
    for n in "qko":
        a[f"b{n}"] = g[f"L0_attn_b{n}"].reshape(D, 1)
    a["bv"] = g["L0_attn_bv"].reshape(D)
    rel = g["L0_attn_rel_emb"]
    a["rel_rows"] = c(np.tile(rel.T, (H0, 1)))
    reversed_index = np.clip(255 - np.arange(CH), -128, 128) + 128
    a["rel_reversed"] = c(rel[reversed_index].T)
    a["mrep"] = c(np.tile(g["L0_attn_M"].reshape(P, HD), (1, H0)))
    a["z"] = g["L0_attn_z"].reshape(P, 1)
    a["alpha"] = g["L0_attn_gate_alpha"].reshape(1)
    a["headblk"] = np.kron(np.eye(H0, dtype=np.float32), np.ones((HD, HD), np.float32))
    a["gate_wT"] = c(g["L0_ffn_gate_w"].T)
    a["gate_bias"] = g["L0_ffn_gate_bias"].reshape(E_)
    moe = np.zeros((E_ // 2 + 1, P, 3, P), np.float32)
    moe[0, :, 0], moe[0, :, 1], moe[0, :, 2] = g["L0_ffn_sh_gate"].T, g["L0_ffn_sh_up"].T, g["L0_ffn_sh_down"].T
    for i, n in enumerate(("w_gate", "w_up")):
        moe[1:, :, i] = g[f"L0_ffn_{n}"].reshape(E_ // 2, 2 * EI, D).transpose(0, 2, 1)
    moe[1:, :, 2] = g["L0_ffn_w_down"].transpose(0, 2, 1).reshape(E_ // 2, 2 * EI, D)
    a["moe_w"] = moe
    a["wqkv1"], a["wproj"] = g["L1_attn_Wqkv"], g["L1_attn_Wproj"]
    a["lam"] = np.stack([g[f"L1_attn_lambda_{n}"] for n in ("q1", "k1", "q2", "k2")])
    jpos = (8 * np.arange(16)[None, :] + np.arange(8)[:, None]).reshape(-1)
    ipos = (32 * np.arange(4)[None, :] + np.arange(32)[:, None]).reshape(-1)
    hidden = np.where(jpos[:, None] > ipos[None, :], np.float32(-1e30), np.float32(0))
    a["negmask"] = np.stack([hidden, hidden.T], axis=1)
    half = np.arange(0, DH, 2, dtype=np.float32)
    pos = np.arange(S, dtype=np.float32)
    freqs = pos[:, None] * (np.float32(1.0) / np.float32(10000.0) ** (half / np.float32(DH)))[None, :]
    freqs = np.concatenate([freqs, freqs], -1)
    base = (half + np.float32(0.4 * DH)) / np.float32(1.4 * DH)
    scale = base[None, :] ** ((pos - S // 2) / np.float32(WIN // 2))[:, None]
    scale = np.concatenate([scale, scale], -1)
    sign = np.where(np.arange(DH) < DH // 2, np.float32(-1), np.float32(1))
    cos, sin = np.cos(freqs), np.sin(freqs) * sign
    tables = np.stack([cos * scale, sin * scale, cos * (1 / scale), sin * (1 / scale)]).astype(np.float32)
    rows = np.arange(P).reshape(2, 2, DH // 2).transpose(1, 0, 2).reshape(-1)
    rope = np.tile(tables.transpose(2, 0, 1), (2, 1, 1))[rows]
    rope[:, 1::2] = rope[(np.arange(P) + DH) % P][:, 1::2]
    a["rope"] = c(rope)
    a["blk64"] = c(np.kron(np.eye(2, dtype=np.float32), np.ones((DH, DH), np.float32))[rows][:, rows])
    behind = np.arange(QW)[None, :] - np.arange(P)[:, None]
    a["band"] = c(np.tile(np.where((behind >= 0) & (behind <= WIN), np.float32(0), np.float32(-1e30)), (1, 3)))
    wqkv = g["L1_ffn_Wqkv"].reshape(DEPTH, P, 3, NHP, P).transpose(0, 3, 1, 2, 4)
    w3 = np.stack([wqkv[..., 0, :][..., rows], wqkv[..., 1, :][..., rows], wqkv[..., 2, :]], axis=3)
    a["w3"] = np.concatenate([w3.reshape(DEPTH * NHP, P, 3, P), np.zeros((2, P, 3, P), np.float32)])
    a["wo6"] = c(g["L1_ffn_Wo"].reshape(DEPTH, NHP, P, P).transpose(0, 2, 1, 3))
    a["w1"] = g["L1_ffn_W1"]
    w2 = np.zeros((DEPTH, 3 * P, P), np.float32)
    w2[:, :GI] = g["L1_ffn_W2"]
    a["w2"] = c(w2.reshape(DEPTH, 3, P, P).transpose(0, 2, 1, 3))
    col = np.zeros((DEPTH, P, NCOL), np.float32)
    for k, n in ((C_Q, "q_scale"), (C_K, "k_scale")):
        col[:, :, k] = np.tile(g[f"L1_ffn_{n}"], (1, 2))[:, rows]
    col[:, :, C_G], col[:, :, C_B], col[:, :, C_B2] = g["L1_ffn_ln_g"], g["L1_ffn_ln_b"], g["L1_ffn_b2"]
    for t, n in enumerate(GT):
        col[:, :n, C_A + t] = g["L1_ffn_b1"][:, t * P:t * P + n]
        col[:, :n, C_GATE + t] = g["L1_ffn_b1"][:, GI + t * P:GI + t * P + n]
    a["col"] = col
    a["ident"] = np.eye(P, dtype=np.float32)
    a["headsel"] = np.repeat(np.eye(H0, dtype=np.float32), HD, axis=0)
    return a


SCRATCH = {
    "xs_stash": ([2, P, T], F32),
    "v1": ([T, NK1 * HD], F32),
    "q1": ([3, HD, (B * NK1 + 2) * QPK, S], BF16),
    "k1": ([3, HD, B * NK1 + 2, S], BF16),
    "m1all": ([(B * NK1 + 2) * QPK, S], BF16),
    "ones1": ([1, S], BF16),
    "o1": ([B * NQ1 + 1, 2, HD + 1, S], F32),
    "combineT": ([E_, T], F32),
    "qp": ([B * H0, KROWS + 1, S], BF16),
    "o0": ([B * H0 + 1, 2, HD + 1, S], F32),
    "kp": ([3, B * H0 + 2, KROWS + 1, S], BF16),
}


def kernel(**inputs):
    import numpy as np
    import concourse.bacc as bacc
    from concourse.bass_utils import run_bass_kernel_spmd as run

    nc = bacc.Bacc("TRN2", target_bir_lowering=False, num_devices=1)
    arrays = host_arrays(inputs)
    d = {}
    for name, a in arrays.items():
        d[name] = nc.dram_tensor(f"in_{name}", a.shape, mybir.dt.from_np(a.dtype), kind="ExternalInput").ap()
    for name, (shape, dt) in SCRATCH.items():
        d[name] = nc.dram_tensor(f"scratch_{name}", shape, dt).ap()
    d["m1"], d["m1pad"] = d["m1all"][0:B * NQ1], d["m1all"][B * NQ1:]
    d["out"] = nc.dram_tensor("out", (T, D), F32, kind="ExternalOutput").ap()
    build(nc, d)
    r = run(nc, [{f"in_{n}": a for n, a in arrays.items()}], core_ids=[0])
    return r.results[0]["out"].reshape(B, S, D)
```
